# Optimizing a Trainium2 kernel written in Bass

```python
import numpy as np
import jax
import jax.numpy as jnp

def _softmax(x, axis=-1):
    return jax.nn.softmax(x, axis=axis)

def _gelu(x):
    return jax.nn.gelu(x, approximate=True)

def _silu(x):
    return jax.nn.silu(x)

def _sigmoid(x):
    return jax.nn.sigmoid(x)

def _layernorm(x, axis=-1, eps=1e-05):
    m = jnp.mean(x, axis=axis, keepdims=True)
    v = jnp.var(x, axis=axis, keepdims=True)
    return (x - m) / jnp.sqrt(v + eps)

def _scatter_add(tgt, idx, src, axis=0):
    return tgt.at[idx].add(src)

def _segment_sum(src, seg, n):
    return jax.ops.segment_sum(src, seg, n)
kernel_name = 'mk_flamingo_gated_d4_seqx_r4_0fc532'

def setup_inputs(seed: int=0):
    np.random.seed(seed)
    _w = jnp.asarray

    def _rec_inputs():
        import jax
        import jax.numpy as jnp
        _rk = jax.random.key(seed)
        x = -0.0003929 + 0.9999 * jax.random.normal(jax.random.fold_in(_rk, 1), (8, 256, 256), jnp.float32)
        _lenS = 256 - jax.random.randint(jax.random.fold_in(_rk, 7), (8,), 0, max(1, 256 // 4) + 1, jnp.int32)
        _lenS2 = 120 - jax.random.randint(jax.random.fold_in(_rk, 8), (8,), 0, max(1, 120 // 4) + 1, jnp.int32)
        _ctx_1024P = jax.random.normal(jax.random.fold_in(_rk, 11), (8, 16, 256), jnp.float32)
        _ctx_1024c = jax.random.dirichlet(jax.random.fold_in(_rk, 511), 0.3 * jnp.ones((16,), jnp.float32), (8, 120))
        _ctx_1024t = jnp.einsum('bsk,bkd->bsd', _ctx_1024c, _ctx_1024P)
        _ctx_1024t = _ctx_1024t * jax.lax.rsqrt(jnp.mean(jnp.square(_ctx_1024t)) + 1e-12) * 0.953939
        ctx_1024 = 2.81802e-05 + 1.00001 * (_ctx_1024t + 0.3 * jax.random.normal(jax.random.fold_in(_rk, 611), (8, 120, 256), jnp.float32))
        fside_BxS2_0 = 0.0132156 + 1.00766 * jax.random.normal(jax.random.fold_in(_rk, 13), (8, 120), jnp.float32)
        _validS = jnp.arange(256)[None, :] < _lenS[:, None]
        _validS2 = jnp.arange(120)[None, :] < _lenS2[:, None]
        _causal = jnp.tril(jnp.ones((256, 256), dtype=bool))
        mask_BxS2_ik1 = jnp.where(jnp.broadcast_to(_validS2[:, :], (8, 120)), 1, 0).astype(jnp.int32)
        mask_BxS2_bk0 = jnp.logical_not(jnp.broadcast_to(_validS2[:, :], (8, 120)))
        mask_BxS2_ik0 = jnp.where(jnp.broadcast_to(_validS2[:, :], (8, 120)), 0, 1).astype(jnp.int32)
        _g = jax.random.normal(jax.random.fold_in(_rk, 9001), (2, 4), jnp.float32)
        _g = jnp.sign(_g) * jnp.maximum(jnp.abs(_g), 1.0) + (_g == 0) * 1.0
        g_xattn = _g[0]
        g_ffn = _g[1]
        return (x, ctx_1024, fside_BxS2_0, mask_BxS2_ik1, mask_BxS2_bk0, mask_BxS2_ik0, g_xattn, g_ffn)
    x, ctx_1024, fside_BxS2_0, mask_BxS2_ik1, mask_BxS2_bk0, mask_BxS2_ik0, g_xattn, g_ffn = _rec_inputs()

    def _L0_xattn_setup():
        import jax, jax.numpy as jnp
        import numpy as np
        D_MODEL = 256
        OUT = 256
        BS, SEQ = (8, 512)
        key = jax.random.key(seed)
        ks = jax.random.split(key, 11)
        scale = 1.0 / np.sqrt(D_MODEL)
        return {'q': jax.random.normal(ks[0], (BS, SEQ, D_MODEL), dtype=jnp.float32), 'k': jax.random.normal(ks[1], (BS, SEQ, D_MODEL), dtype=jnp.float32), 'v': jax.random.normal(ks[2], (BS, SEQ, D_MODEL), dtype=jnp.float32), 'Wq': jax.random.normal(ks[3], (D_MODEL, OUT), dtype=jnp.float32) * scale, 'bq': jnp.zeros((OUT,), dtype=jnp.float32), 'Wk': jax.random.normal(ks[4], (D_MODEL, OUT), dtype=jnp.float32) * scale, 'bk': jnp.zeros((OUT,), dtype=jnp.float32), 'Wv': jax.random.normal(ks[5], (D_MODEL, OUT), dtype=jnp.float32) * scale, 'bv': jnp.zeros((OUT,), dtype=jnp.float32), 'mask': jax.random.randint(ks[6], (BS, SEQ), 0, 2, dtype=jnp.int32)}
    _L0_xattn_all = _L0_xattn_setup()
    _L0_xattn_in = {k: v for k, v in _L0_xattn_all.items() if k in ('Wq', 'bq', 'Wk', 'bk', 'Wv', 'bv')}
    del _L0_xattn_all

    def _L0_ffn_setup():
        import jax, jax.numpy as jnp
        import numpy as np
        NUM_EXPERTS = 8
        CAP_FACTOR = 1.0
        MIN_CAP = 8
        key = jax.random.key(seed)
        ks = jax.random.split(key, 10)
        G, S, D, H, E = (4, 1024, 256, 1024, NUM_EXPERTS)
        s = 0.02
        return {'x': jax.random.normal(ks[0], (G, S, D), dtype=jnp.float32), 'gate': jax.random.normal(ks[1], (D, E), dtype=jnp.float32) * s, 'W1': jax.random.normal(ks[2], (E, D, H), dtype=jnp.float32) * s, 'b1': jnp.zeros((E, H), dtype=jnp.float32), 'W2': jax.random.normal(ks[3], (E, H, D), dtype=jnp.float32) * s, 'b2': jnp.zeros((E, D), dtype=jnp.float32), 'Ws1': jax.random.normal(ks[4], (D, H), dtype=jnp.float32) * s, 'bs1': jnp.zeros((H,), dtype=jnp.float32), 'Ws2': jax.random.normal(ks[5], (H, D), dtype=jnp.float32) * s, 'bs2': jnp.zeros((D,), dtype=jnp.float32)}
    _L0_ffn_all = _L0_ffn_setup()
    _L0_ffn_in = {k: v for k, v in _L0_ffn_all.items() if k in ('gate', 'W1', 'b1', 'W2', 'b2', 'Ws1', 'bs1', 'Ws2', 'bs2')}
    del _L0_ffn_all

    def _L1_xattn_setup():
        import jax, jax.numpy as jnp
        import numpy as np
        EMBED_DIM = 256
        NUM_HEADS = 16
        HEAD_DIM = EMBED_DIM // NUM_HEADS
        B, SQ, SK = (2, 512, 512)
        key = jax.random.key(seed)
        ks = jax.random.split(key, 10)
        s = 1.0 / np.sqrt(EMBED_DIM)
        return {'tgt': jax.random.normal(ks[0], (B, SQ, EMBED_DIM), jnp.float32), 'mem': jax.random.normal(ks[1], (B, SK, EMBED_DIM), jnp.float32), 'attn_bias': jax.random.normal(ks[2], (B, SK), jnp.float32), 'memory_key_padding_mask': jax.random.randint(ks[3], (B, SK), 0, 2).astype(bool), 'Wq_w': jax.random.normal(ks[4], (EMBED_DIM, EMBED_DIM), jnp.float32) * s, 'Wq_b': jnp.zeros((EMBED_DIM,), jnp.float32), 'Wkv_w': jax.random.normal(ks[5], (2 * EMBED_DIM, EMBED_DIM), jnp.float32) * s, 'Wkv_b': jnp.zeros((2 * EMBED_DIM,), jnp.float32), 'out_w': jax.random.normal(ks[6], (EMBED_DIM, EMBED_DIM), jnp.float32) * s, 'out_b': jnp.zeros((EMBED_DIM,), jnp.float32)}
    _L1_xattn_all = _L1_xattn_setup()
    _L1_xattn_in = {k: v for k, v in _L1_xattn_all.items() if k in ('Wq_w', 'Wq_b', 'Wkv_w', 'Wkv_b', 'out_w', 'out_b')}
    del _L1_xattn_all

    def _L1_ffn_setup():
        import jax, jax.numpy as jnp
        import numpy as np
        B, N, D = (4, 512, 256)
        SPARSITY = 0.01
        key = jax.random.key(seed)
        k1, k2, k3 = jax.random.split(key, 3)
        x = jax.random.normal(k1, (B, N, D), dtype=jnp.float32)
        spatial = jax.random.normal(k2, (D, D), dtype=jnp.float32) * 0.02
        freq = jnp.fft.fft(spatial, axis=-1)
        k = int(D * SPARSITY)
        mag = jnp.abs(freq)
        kth = jax.lax.top_k(mag, k)[0][:, -1:]
        w_sparse = jnp.where(mag >= kth, freq, 0.0 + 0j)
        bias = jax.random.normal(k3, (D,), dtype=jnp.float32) * 0.01
        return {'x': x, 'w_freq_real': jnp.real(w_sparse).astype(jnp.float32), 'w_freq_imag': jnp.imag(w_sparse).astype(jnp.float32), 'bias': bias}
    _L1_ffn_all = _L1_ffn_setup()
    _L1_ffn_in = {k: v for k, v in _L1_ffn_all.items() if k in ('w_freq_real', 'w_freq_imag', 'bias')}
    del _L1_ffn_all

    def _L2_xattn_setup():
        import jax, jax.numpy as jnp
        import numpy as np
        H = 256
        NH = 16
        HD = H // NH
        key = jax.random.key(seed)
        ks = jax.random.split(key, 12)
        inp = {'query': jax.random.normal(ks[0], (4, 256, H), dtype=jnp.float32), 'key': jax.random.normal(ks[1], (4, 512, H), dtype=jnp.float32), 'value': jax.random.normal(ks[2], (4, 512, H), dtype=jnp.float32), 'key_padding_mask': jax.random.randint(ks[3], (4, 512), 0, 2, dtype=jnp.int32), 'Wq': jax.random.normal(ks[4], (H, H), dtype=jnp.float32) * (1.0 / np.sqrt(H)), 'bq': jnp.zeros((H,), dtype=jnp.float32), 'Wk': jax.random.normal(ks[5], (H, H), dtype=jnp.float32) * (1.0 / np.sqrt(H)), 'bk': jnp.zeros((H,), dtype=jnp.float32), 'Wv': jax.random.normal(ks[6], (H, H), dtype=jnp.float32) * (1.0 / np.sqrt(H)), 'bv': jnp.zeros((H,), dtype=jnp.float32), 'Wo': jax.random.normal(ks[7], (H, H), dtype=jnp.float32) * (1.0 / np.sqrt(H)), 'bo': jnp.zeros((H,), dtype=jnp.float32)}
        return inp
    _L2_xattn_all = _L2_xattn_setup()
    _L2_xattn_in = {k: v for k, v in _L2_xattn_all.items() if k in ('Wq', 'bq', 'Wk', 'bk', 'Wv', 'bv', 'Wo', 'bo')}
    del _L2_xattn_all

    def _L2_ffn_setup():
        import jax, jax.numpy as jnp
        import numpy as np
        EPS = 1e-06
        LN_EPS = 1e-05

        def _absmean_core(W):
            gamma = jnp.mean(jnp.abs(W)) + EPS
            Ws = W / gamma
            Wq = jnp.sign(Ws) * jnp.minimum(jnp.round(jnp.abs(Ws)), 1.0)
            return (Wq, gamma)

        @jax.custom_vjp
        def absmean(W):
            return _absmean_core(W)[0]

        def _absmean_fwd(W):
            Wq, gamma = _absmean_core(W)
            return (Wq, gamma)

        def _absmean_bwd(gamma, g):
            return (g / gamma,)
        absmean.defvjp(_absmean_fwd, _absmean_bwd)

        def layernorm(x, w, b, eps=LN_EPS):
            mu = jnp.mean(x, axis=-1, keepdims=True)
            var = jnp.mean((x - mu) ** 2, axis=-1, keepdims=True)
            return (x - mu) * jax.lax.rsqrt(var + eps) * w + b
        key = jax.random.key(seed)
        k1, k2, k3 = jax.random.split(key, 3)
        d, h = (256, 1024)
        B, T = (8, 512)
        return {'x': jax.random.normal(k1, (B, T, d), jnp.float32), 'W_fc': jax.random.normal(k2, (h, d), jnp.float32), 'ln_w': jnp.ones((h,), jnp.float32), 'ln_b': jnp.zeros((h,), jnp.float32), 'W_proj': jax.random.normal(k3, (d, h), jnp.float32)}
    _L2_ffn_all = _L2_ffn_setup()
    _L2_ffn_in = {k: v for k, v in _L2_ffn_all.items() if k in ('W_fc', 'ln_w', 'ln_b', 'W_proj')}
    del _L2_ffn_all

    def _L3_xattn_setup():
        import jax, jax.numpy as jnp
        import numpy as np
        D_MODEL = 256
        B, S = (4, 512)
        key = jax.random.key(seed)
        ks = jax.random.split(key, 10)
        s = 1.0 / np.sqrt(D_MODEL)
        return {'k': jax.random.normal(ks[0], (B, S, D_MODEL), jnp.float32), 'v': jax.random.normal(ks[1], (B, S, D_MODEL), jnp.float32), 'q': jax.random.normal(ks[2], (B, S, D_MODEL), jnp.float32), 'Wk': jax.random.normal(ks[3], (D_MODEL, D_MODEL), jnp.float32) * s, 'Wv': jax.random.normal(ks[4], (D_MODEL, D_MODEL), jnp.float32) * s, 'bv': jnp.zeros((D_MODEL,), jnp.float32), 'Wq': jax.random.normal(ks[5], (D_MODEL, D_MODEL), jnp.float32) * s, 'bq': jnp.zeros((D_MODEL,), jnp.float32), 'Wo': jax.random.normal(ks[6], (D_MODEL, D_MODEL), jnp.float32) * s, 'bo': jnp.zeros((D_MODEL,), jnp.float32)}
    _L3_xattn_all = _L3_xattn_setup()
    _L3_xattn_in = {k: v for k, v in _L3_xattn_all.items() if k in ('Wk', 'Wv', 'bv', 'Wq', 'bq', 'Wo', 'bo')}
    del _L3_xattn_all

    def _L3_ffn_setup():
        import jax, jax.numpy as jnp
        import numpy as np
        CAPACITY_FACTOR = 1.0

        def _top1_gate(x2d, wg):
            S, _ = x2d.shape
            E = wg.shape[1]
            C = int(CAPACITY_FACTOR * S / E)
            logits = x2d @ wg
            gates = jax.nn.softmax(logits, axis=-1)
            idx = jnp.argmax(gates, axis=-1)
            mask = jax.nn.one_hot(idx, E, dtype=jnp.int32)
            loc = jnp.cumsum(mask, axis=0) - 1
            me = jnp.mean(gates, axis=0)
            ce = jnp.mean(mask.astype(gates.dtype), axis=0)
            l_aux = E * jnp.sum(me * ce)
            mask = mask * (loc < C).astype(jnp.int32)
            gate_s = jnp.sum(gates * mask, axis=-1)
            loc_s = jnp.sum(loc * mask, axis=-1)
            loc_oh = jax.nn.one_hot(loc_s, C, dtype=gates.dtype)
            combine = (gate_s[:, None] * mask.astype(gates.dtype))[:, :, None] * loc_oh[:, None, :]
            dispatch = (combine > 0).astype(gates.dtype)
            return (l_aux, combine, dispatch)
        key = jax.random.key(seed)
        k1, k2, k3, k4 = jax.random.split(key, 4)
        s, b, m, E, ffn = (512, 4, 256, 8, 1024)
        x = jax.random.normal(k1, (s, b, m), dtype=jnp.float32)
        wg = jax.random.normal(k2, (m, E), dtype=jnp.float32) * 0.02
        w1 = jax.random.normal(k3, (E, m, ffn), dtype=jnp.float32) * 0.02
        w2 = jax.random.normal(k4, (E, ffn, m), dtype=jnp.float32) * 0.02
        return {'x': x, 'wg': wg, 'w1': w1, 'w2': w2}
    _L3_ffn_all = _L3_ffn_setup()
    _L3_ffn_in = {k: v for k, v in _L3_ffn_all.items() if k in ('wg', 'w1', 'w2')}
    del _L3_ffn_all
    return {'x': x, 'ctx_1024': ctx_1024, 'fside_BxS2_0': fside_BxS2_0, 'mask_BxS2_ik1': mask_BxS2_ik1, 'mask_BxS2_bk0': mask_BxS2_bk0, 'mask_BxS2_ik0': mask_BxS2_ik0, 'g_xattn': g_xattn, 'g_ffn': g_ffn, 'L0_xattn_Wq': _L0_xattn_in['Wq'], 'L0_xattn_bq': _L0_xattn_in['bq'], 'L0_xattn_Wk': _L0_xattn_in['Wk'], 'L0_xattn_bk': _L0_xattn_in['bk'], 'L0_xattn_Wv': _L0_xattn_in['Wv'], 'L0_xattn_bv': _L0_xattn_in['bv'], 'L0_ffn_gate': _L0_ffn_in['gate'], 'L0_ffn_W1': _L0_ffn_in['W1'], 'L0_ffn_b1': _L0_ffn_in['b1'], 'L0_ffn_W2': _L0_ffn_in['W2'], 'L0_ffn_b2': _L0_ffn_in['b2'], 'L0_ffn_Ws1': _L0_ffn_in['Ws1'], 'L0_ffn_bs1': _L0_ffn_in['bs1'], 'L0_ffn_Ws2': _L0_ffn_in['Ws2'], 'L0_ffn_bs2': _L0_ffn_in['bs2'], 'L1_xattn_Wq_w': _L1_xattn_in['Wq_w'], 'L1_xattn_Wq_b': _L1_xattn_in['Wq_b'], 'L1_xattn_Wkv_w': _L1_xattn_in['Wkv_w'], 'L1_xattn_Wkv_b': _L1_xattn_in['Wkv_b'], 'L1_xattn_out_w': _L1_xattn_in['out_w'], 'L1_xattn_out_b': _L1_xattn_in['out_b'], 'L1_ffn_w_freq_real': _L1_ffn_in['w_freq_real'], 'L1_ffn_w_freq_imag': _L1_ffn_in['w_freq_imag'], 'L1_ffn_bias': _L1_ffn_in['bias'], 'L2_xattn_Wq': _L2_xattn_in['Wq'], 'L2_xattn_bq': _L2_xattn_in['bq'], 'L2_xattn_Wk': _L2_xattn_in['Wk'], 'L2_xattn_bk': _L2_xattn_in['bk'], 'L2_xattn_Wv': _L2_xattn_in['Wv'], 'L2_xattn_bv': _L2_xattn_in['bv'], 'L2_xattn_Wo': _L2_xattn_in['Wo'], 'L2_xattn_bo': _L2_xattn_in['bo'], 'L2_ffn_W_fc': _L2_ffn_in['W_fc'], 'L2_ffn_ln_w': _L2_ffn_in['ln_w'], 'L2_ffn_ln_b': _L2_ffn_in['ln_b'], 'L2_ffn_W_proj': _L2_ffn_in['W_proj'], 'L3_xattn_Wk': _L3_xattn_in['Wk'], 'L3_xattn_Wv': _L3_xattn_in['Wv'], 'L3_xattn_bv': _L3_xattn_in['bv'], 'L3_xattn_Wq': _L3_xattn_in['Wq'], 'L3_xattn_bq': _L3_xattn_in['bq'], 'L3_xattn_Wo': _L3_xattn_in['Wo'], 'L3_xattn_bo': _L3_xattn_in['bo'], 'L3_ffn_wg': _L3_ffn_in['wg'], 'L3_ffn_w1': _L3_ffn_in['w1'], 'L3_ffn_w2': _L3_ffn_in['w2']}

def reference(x, ctx_1024, fside_BxS2_0, mask_BxS2_ik1, mask_BxS2_bk0, mask_BxS2_ik0, g_xattn, g_ffn, L0_xattn_Wq, L0_xattn_bq, L0_xattn_Wk, L0_xattn_bk, L0_xattn_Wv, L0_xattn_bv, L0_ffn_gate, L0_ffn_W1, L0_ffn_b1, L0_ffn_W2, L0_ffn_b2, L0_ffn_Ws1, L0_ffn_bs1, L0_ffn_Ws2, L0_ffn_bs2, L1_xattn_Wq_w, L1_xattn_Wq_b, L1_xattn_Wkv_w, L1_xattn_Wkv_b, L1_xattn_out_w, L1_xattn_out_b, L1_ffn_w_freq_real, L1_ffn_w_freq_imag, L1_ffn_bias, L2_xattn_Wq, L2_xattn_bq, L2_xattn_Wk, L2_xattn_bk, L2_xattn_Wv, L2_xattn_bv, L2_xattn_Wo, L2_xattn_bo, L2_ffn_W_fc, L2_ffn_ln_w, L2_ffn_ln_b, L2_ffn_W_proj, L3_xattn_Wk, L3_xattn_Wv, L3_xattn_bv, L3_xattn_Wq, L3_xattn_bq, L3_xattn_Wo, L3_xattn_bo, L3_ffn_wg, L3_ffn_w1, L3_ffn_w2):
    import jax
    import jax.numpy as jnp

    def _L0_xattn_ref(q, k, v, Wq, bq, Wk, bk, Wv, bv, mask):
        import jax, jax.numpy as jnp
        import numpy as np
        D_MODEL = 256
        OUT = 256
        BS, SEQ = (8, 512)
        query = q @ Wq + bq
        key_p = k @ Wk + bk
        value = v @ Wv + bv
        dim_k = key_p.shape[-1]
        scores = jnp.einsum('btd,bsd->bts', query, key_p) / jnp.sqrt(jnp.asarray(dim_k, dtype=query.dtype))
        scores = jnp.where(mask[:, None, :] == 0, -jnp.inf, scores)
        weights = jax.nn.softmax(scores, axis=-1)
        outputs = jnp.einsum('bts,bsd->btd', weights, value)
        return outputs

    def _L0_ffn_ref(x, gate, W1, b1, W2, b2, Ws1, bs1, Ws2, bs2):
        import jax, jax.numpy as jnp
        import numpy as np
        NUM_EXPERTS = 8
        CAP_FACTOR = 1.0
        MIN_CAP = 8
        G, S, D = x.shape
        E = gate.shape[1]
        T = G * S
        capacity = max(MIN_CAP, int(CAP_FACTOR * T / E))
        logits = jnp.einsum('gsd,de->gse', x, gate)
        probs = jax.nn.softmax(logits, axis=-1)
        flat_probs = probs.transpose(2, 0, 1).reshape(E, T)
        scores, token_idx = jax.lax.top_k(flat_probs, k=capacity)
        scores = jnp.where(scores > -100000000.0, scores, 0.0)
        flat_x = x.reshape(T, D)
        tok = flat_x[token_idx]
        h = jax.nn.gelu(jnp.einsum('ecd,edh->ech', tok, W1) + b1[:, None, :])
        out_tok = jnp.einsum('ech,ehd->ecd', h, W2) + b2[:, None, :]
        scaled = out_tok * scores[..., None]
        routed = jnp.zeros_like(flat_x).at[token_idx.reshape(-1)].add(scaled.reshape(E * capacity, D)).reshape(G, S, D)
        shared = jax.nn.gelu(jnp.einsum('gsd,dh->gsh', x, Ws1) + bs1)
        shared = jnp.einsum('gsh,hd->gsd', shared, Ws2) + bs2
        return routed + shared

    def _L1_xattn_ref(tgt, mem, attn_bias, memory_key_padding_mask, Wq_w, Wq_b, Wkv_w, Wkv_b, out_w, out_b):
        import jax, jax.numpy as jnp
        import numpy as np
        EMBED_DIM = 256
        NUM_HEADS = 16
        HEAD_DIM = EMBED_DIM // NUM_HEADS
        B, SQ, SK = (2, 512, 512)
        b, sq, _ = tgt.shape
        sk = mem.shape[1]
        q = (tgt @ Wq_w.T + Wq_b).reshape(b, sq, NUM_HEADS, HEAD_DIM)
        kv = (mem @ Wkv_w.T + Wkv_b).reshape(b, sk, 2, NUM_HEADS, HEAD_DIM)
        k, v = (kv[:, :, 0], kv[:, :, 1])
        scale = 1.0 / np.sqrt(HEAD_DIM)
        scores = jnp.einsum('bthd,bshd->bhts', q, k * scale)
        scores = scores + attn_bias[:, None, None, :]
        pad = jnp.where(memory_key_padding_mask, 0.0, -jnp.inf).astype(scores.dtype)
        scores = scores + pad[:, None, None, :]
        attn = jax.nn.softmax(scores, axis=-1)
        ctx = jnp.einsum('bhts,bshd->bthd', attn, v)
        out = ctx.reshape(b, sq, EMBED_DIM) @ out_w.T + out_b
        return out

    def _L1_ffn_ref(x, w_freq_real, w_freq_imag, bias):
        import jax, jax.numpy as jnp
        import numpy as np
        B, N, D = (4, 512, 256)
        SPARSITY = 0.01
        w = jax.lax.complex(w_freq_real, w_freq_imag)
        x_freq = jnp.fft.fft(x, axis=-1)
        y_freq = jnp.einsum('bnd,do->bno', x_freq, w)
        y = jnp.real(jnp.fft.ifft(y_freq, axis=-1))
        return y + bias

    def _L2_xattn_ref(query, key, value, key_padding_mask, Wq, bq, Wk, bk, Wv, bv, Wo, bo):
        import jax, jax.numpy as jnp
        import numpy as np
        H = 256
        NH = 16
        HD = H // NH
        B, Sq, _ = query.shape
        Sk = key.shape[1]
        scaling = HD ** (-0.5)
        q = (query @ Wq + bq).reshape(B, Sq, NH, HD).transpose(0, 2, 1, 3)
        k = (key @ Wk + bk).reshape(B, Sk, NH, HD).transpose(0, 2, 1, 3)
        v = (value @ Wv + bv).reshape(B, Sk, NH, HD).transpose(0, 2, 1, 3)
        scores = jnp.einsum('bhqd,bhkd->bhqk', q, k) * scaling
        scores = jnp.where((key_padding_mask == 0)[:, None, None, :], -jnp.inf, scores)
        attn = jax.nn.softmax(scores, axis=-1)
        out = jnp.einsum('bhqk,bhkd->bhqd', attn, v)
        out = out.transpose(0, 2, 1, 3).reshape(B, Sq, H)
        return out @ Wo + bo

    def _L2_ffn_ref(x, W_fc, ln_w, ln_b, W_proj):
        import jax, jax.numpy as jnp
        import numpy as np
        EPS = 1e-06
        LN_EPS = 1e-05

        def _absmean_core(W):
            gamma = jnp.mean(jnp.abs(W)) + EPS
            Ws = W / gamma
            Wq = jnp.sign(Ws) * jnp.minimum(jnp.round(jnp.abs(Ws)), 1.0)
            return (Wq, gamma)

        @jax.custom_vjp
        def absmean(W):
            return _absmean_core(W)[0]

        def _absmean_fwd(W):
            Wq, gamma = _absmean_core(W)
            return (Wq, gamma)

        def _absmean_bwd(gamma, g):
            return (g / gamma,)
        absmean.defvjp(_absmean_fwd, _absmean_bwd)

        def layernorm(x, w, b, eps=LN_EPS):
            mu = jnp.mean(x, axis=-1, keepdims=True)
            var = jnp.mean((x - mu) ** 2, axis=-1, keepdims=True)
            return (x - mu) * jax.lax.rsqrt(var + eps) * w + b
        h = jnp.einsum('btd,hd->bth', x, absmean(W_fc))
        h = jax.nn.gelu(h, approximate=False)
        h = layernorm(h, ln_w, ln_b)
        return jnp.einsum('bth,dh->btd', h, absmean(W_proj))

    def _L3_xattn_ref(k, v, q, Wk, Wv, bv, Wq, bq, Wo, bo):
        import jax, jax.numpy as jnp
        import numpy as np
        D_MODEL = 256
        B, S = (4, 512)
        kp = jnp.einsum('bsd,ed->bse', k, Wk)
        vp = jnp.einsum('bsd,ed->bse', v, Wv) + bv
        qp = jnp.einsum('bsd,ed->bse', q, Wq) + bq
        scale = 1.0 / jnp.sqrt(jnp.float32(kp.shape[-1]))
        scores = jnp.einsum('bqd,bkd->bqk', qp, kp) * scale
        probs = jax.nn.softmax(scores, axis=-1)
        ctx = jnp.einsum('bqk,bkd->bqd', probs, vp)
        return jnp.einsum('bqd,ed->bqe', ctx, Wo) + bo

    def _L3_ffn_ref(x, wg, w1, w2):
        import jax, jax.numpy as jnp
        import numpy as np
        CAPACITY_FACTOR = 1.0

        def _top1_gate(x2d, wg):
            S, _ = x2d.shape
            E = wg.shape[1]
            C = int(CAPACITY_FACTOR * S / E)
            logits = x2d @ wg
            gates = jax.nn.softmax(logits, axis=-1)
            idx = jnp.argmax(gates, axis=-1)
            mask = jax.nn.one_hot(idx, E, dtype=jnp.int32)
            loc = jnp.cumsum(mask, axis=0) - 1
            me = jnp.mean(gates, axis=0)
            ce = jnp.mean(mask.astype(gates.dtype), axis=0)
            l_aux = E * jnp.sum(me * ce)
            mask = mask * (loc < C).astype(jnp.int32)
            gate_s = jnp.sum(gates * mask, axis=-1)
            loc_s = jnp.sum(loc * mask, axis=-1)
            loc_oh = jax.nn.one_hot(loc_s, C, dtype=gates.dtype)
            combine = (gate_s[:, None] * mask.astype(gates.dtype))[:, :, None] * loc_oh[:, None, :]
            dispatch = (combine > 0).astype(gates.dtype)
            return (l_aux, combine, dispatch)
        s, b, m = x.shape
        x2d = x.reshape(-1, m)
        l_aux, combine, dispatch = _top1_gate(x2d, wg)
        combine = combine[:, None]
        dispatch = dispatch[:, None]
        xr = x2d[:, None, :]
        dispatched = jnp.einsum('szfc,szm->zfcm', dispatch, xr)
        E = w1.shape[0]
        di = dispatched.reshape(E, -1, m)
        h = jax.nn.relu(jnp.einsum('ecm,emh->ech', di, w1))
        eo = jnp.einsum('ech,ehm->ecm', h, w2)
        eo = eo[None]
        out = jnp.einsum('szfc,zfcm->sm', combine, eo)
        return out.reshape(s, b, m)
    x = x + jnp.tanh(g_xattn[0]) * _L0_xattn_ref(_layernorm(x, axis=-1), ctx_1024, ctx_1024, L0_xattn_Wq, L0_xattn_bq, L0_xattn_Wk, L0_xattn_bk, L0_xattn_Wv, L0_xattn_bv, mask_BxS2_ik1)
    x = x + jnp.tanh(g_ffn[0]) * _L0_ffn_ref(_layernorm(x, axis=-1), L0_ffn_gate, L0_ffn_W1, L0_ffn_b1, L0_ffn_W2, L0_ffn_b2, L0_ffn_Ws1, L0_ffn_bs1, L0_ffn_Ws2, L0_ffn_bs2)
    x = x + jnp.tanh(g_xattn[1]) * _L1_xattn_ref(_layernorm(x, axis=-1), ctx_1024, fside_BxS2_0, mask_BxS2_bk0, L1_xattn_Wq_w, L1_xattn_Wq_b, L1_xattn_Wkv_w, L1_xattn_Wkv_b, L1_xattn_out_w, L1_xattn_out_b)
    x = x + jnp.tanh(g_ffn[1]) * _L1_ffn_ref(_layernorm(x, axis=-1), L1_ffn_w_freq_real, L1_ffn_w_freq_imag, L1_ffn_bias)
    x = x + jnp.tanh(g_xattn[2]) * _L2_xattn_ref(_layernorm(x, axis=-1), ctx_1024, ctx_1024, mask_BxS2_ik0, L2_xattn_Wq, L2_xattn_bq, L2_xattn_Wk, L2_xattn_bk, L2_xattn_Wv, L2_xattn_bv, L2_xattn_Wo, L2_xattn_bo)
    x = x + jnp.tanh(g_ffn[2]) * _L2_ffn_ref(_layernorm(x, axis=-1), L2_ffn_W_fc, L2_ffn_ln_w, L2_ffn_ln_b, L2_ffn_W_proj)
    x = x + jnp.tanh(g_xattn[3]) * _L3_xattn_ref(ctx_1024, ctx_1024, _layernorm(x, axis=-1), L3_xattn_Wk, L3_xattn_Wv, L3_xattn_bv, L3_xattn_Wq, L3_xattn_bq, L3_xattn_Wo, L3_xattn_bo)
    x = x + jnp.tanh(g_ffn[3]) * _L3_ffn_ref(_layernorm(x, axis=-1), L3_ffn_wg, L3_ffn_w1, L3_ffn_w2)
    return x

_drawn_inputs = setup_inputs


def setup_inputs(seed=0):
    import zlib

    import numpy as np

    out = dict(_drawn_inputs(seed))
    spreads = {'L0_xattn_bq': (0.0, 0.484),
     'L0_xattn_bk': (0.0, 2.0),
     'L0_xattn_bv': (0.0, 0.1),
     'L0_ffn_b1': (0.0, 0.8),
     'L0_ffn_b2': (0.0, 0.61),
     'L0_ffn_bs1': (0.0, 0.355),
     'L0_ffn_bs2': (0.0, 0.1),
     'L1_xattn_Wq_b': (0.0, 0.301),
     'L1_xattn_Wkv_b': (0.0, 0.1),
     'L1_xattn_out_b': (0.0, 0.1),
     'L2_xattn_bq': (0.0, 0.485),
     'L2_xattn_bk': (0.0, 2.0),
     'L2_xattn_bv': (0.0, 0.1),
     'L2_xattn_bo': (0.0, 0.1),
     'L2_ffn_ln_w': (1.0, 0.2),
     'L2_ffn_ln_b': (0.0, 0.1),
     'L3_xattn_bv': (0.0, 0.8),
     'L3_xattn_bq': (0.0, 0.8),
     'L3_xattn_bo': (0.0, 0.8)}
    factors = {'g_ffn': 23.984,
     'L0_ffn_gate': 3.024,
     'L0_ffn_W1': 3.938,
     'L0_ffn_W2': 3.674,
     'L1_ffn_bias': 7.717,
     'L3_xattn_Wk': 7.764,
     'L3_xattn_Wv': 2.787,
     'L3_xattn_Wq': 7.911,
     'L3_xattn_Wo': 2.745,
     'L3_ffn_wg': 8.0,
     'L3_ffn_w1': 8.0,
     'L3_ffn_w2': 8.0}
    for name, (base, spread) in spreads.items():
        noise = np.random.default_rng([zlib.crc32(name.encode()), seed]).standard_normal(out[name].shape)
        drawn = base * np.exp(spread * noise) if base else spread * noise
        out[name] = jnp.asarray(drawn.astype(out[name].dtype))
    for name, factor in factors.items():
        out[name] = (out[name] * factor).astype(out[name].dtype)
    return out
```

```python
from contextlib import ExitStack

import concourse.bass as bass
from concourse import mybir

ALU = mybir.AluOpType
ACT = mybir.ActivationFunctionType
F32 = mybir.dt.float32
BF16 = mybir.dt.bfloat16
F16 = mybir.dt.float16
I32 = mybir.dt.int32
AX = mybir.AxisListType

P = 128
D = 256
KC = D // P
NB, SQ, SK = 8, 256, 120
T = NB * SQ
NT = T // P
TB = SQ // P
NH, HD = 16, 16
HC = P // HD
HID = 1024
MC = HID // P
E = 8
CAP = T // E
ROW = D + E
EPS = 1e-5
NEG = -1e30
BITS = 32
HALF = BITS // (T // 512)

COL = {n: 2 * i for i, n in enumerate(["q0", "k0", "q1", "k1", "q2", "k2", "q3", "k3", "v3"])}
ROWS = ["v0", "s0", "v1", "o1", "f1", "v2", "o2", "o3"]
WEIGHTS = ["q0", "k0", "v0", "q1", "k1", "v1", "o1", "q2", "k2", "v2", "o2", "q3", "k3", "v3", "o3"]


def bcast(ap, axis, n):
    ap = ap.unsqueeze(axis)
    shape = list(ap.shape)
    shape[axis] = n
    return ap.to_broadcast(shape)


def flamingo_kernel(nc, d, out):
    ctx = ExitStack()
    with ctx:
        def sb(name, shape, dt):
            return ctx.enter_context(nc.sbuf_tensor(name, shape, dt))

        def sems(phase, names):
            return {n: ctx.enter_context(nc.semaphore(f"{phase}_{n}")) for n in names.split()}

        x = sb("x", [P, NT, D], F32)
        ctxT = sb("ctxT", [P, KC, NB * SK], F32)
        W = {n: sb(f"W{n}", [P, KC, D], F32) for n in WEIGHTS if n not in ("q3", "k3", "v3")}
        W |= {f"{n}3": W[f"{n}0"] for n in "qkv"}
        Mf = sb("Mf", [P, KC, D], F32)
        ident = sb("ident", [P, P], F32)
        tri = sb("tri", [P, P], BF16)
        ones = sb("ones", [P, P], BF16)
        headmask = sb("headmask", [P, HC], F32)
        cols = sb("cols", [P, 2 * len(COL)], F32)
        rows = sb("rows", [P, len(ROWS), D], F32)
        tg = sb("tg", [P, 8], F32)
        gates = sb("gates", [P, 2, KC, E], F32)
        brow = sb("brow", [96, 3, NB * SK], BF16)
        mhalf = sb("mhalf", [P, 4], F32)
        ffw = sb("ffw", [P, 2, 2048], F32)
        ew = sb("ew", [P, 2, 2, 2048], F32)
        small = sb("small", [P, 1024], F32)
        arena = sb("arena", [P, 22016], F32)

        class Cut:

            def __init__(self, buf):
                self.buf, self.at = buf, 0

            def take(self, n, pat=None, dt=F32, **kw):
                words = n if dt not in (BF16, F16) else (n + 1) // 2
                v = self.buf[:, self.at:self.at + words]
                self.at += words
                assert self.at <= self.buf.shape[1], self.at
                if dt != F32:
                    v = v.bitcast(dt)
                return v if pat is None else v.rearrange(pat, **kw)

        psum = [ctx.enter_context(nc.psum_tensor(f"bank{i}", [P, 512], F32)) for i in range(8)]
        MISC = psum[6:8]

        zrow = nc.dram_tensor("zrow", (T, ROW), F32, kind="Internal").ap()
        zrow3 = nc.dram_tensor("zrow3", (T, D), F32, kind="Internal").ap()
        acc = nc.dram_tensor("acc", (T, D), F32, kind="Internal").ap()
        eo = nc.dram_tensor("eo", (T, D), F32, kind="Internal").ap()
        slotd = [nc.dram_tensor(f"slotd{i}", (P, 16), F32, kind="Internal").ap() for i in range(2)]

        c = Cut(arena)
        z = c.take(4 * D, "p (t n) -> p t n", t=4)
        zT = c.take(2 * KC * SQ, "p (u k n) -> p u k n", u=2, k=KC)
        qT = c.take(2 * KC * SQ, "p (u k n) -> p u k n", u=2, k=KC)
        OT = c.take(2 * KC * SQ, "p (u k n) -> p u k n", u=2, k=KC)
        KT = c.take(2 * KC * SK, "p (u k n) -> p u k n", u=2, k=KC)
        cT = c.take(2 * KC * SK, "p (u k n) -> p u k n", u=2, k=KC)
        Vp = c.take(2 * NH * 32, "p (u h n) -> p u h n", u=2, h=NH)
        after_common = c.at
        KBD = c.take(2 * KC * HC * SK, "p (u k h n) -> p u k h n", u=2, k=KC, h=HC)
        Pr = c.take(4 * HC * SK, "p (b h n) -> p b h n", b=4, h=HC)
        PT = c.take(2 * NH * SQ, "p (u h n) -> p u h n", u=2, h=NH)
        c.at = after_common
        V1 = c.take(2 * D, "p (u n) -> p u n", u=2)
        P1 = c.take(2 * TB * SK, "p (u t n) -> p u t n", u=2, t=TB)
        PT1 = c.take(2 * SQ, "p (u n) -> p u n", u=2)
        VT1 = c.take(2 * KC * SK, "p (u k n) -> p u k n", u=2, k=KC)
        c.at = after_common
        zT_all = c.take(KC * T, "p (k n) -> p k n", k=KC)
        hT = c.take(MC * 512, "p (m n) -> p m n", m=MC)
        c.at = 0
        b2row = c.take(E * D, "p (e n) -> p e n", e=E)
        G = c.take(2 * TB * ROW, "p (u t n) -> p u t n", u=2, t=TB)
        assert c.at <= after_common
        c.at = after_common
        xeT = c.take(2 * KC * CAP, "p (u k n) -> p u k n", u=2, k=KC)
        heT = c.take(2 * MC * CAP, "p (u m n) -> p u m n", u=2, m=MC)
        eout = c.take(2 * TB * D, "p (u t n) -> p u t n", u=2, t=TB)
        c.at = 18432
        hi1 = c.take(NT * P, "p (t e a) -> p t e a", dt=BF16, t=NT, e=E)
        lo1 = c.take(NT * P, "p (t e a) -> p t e a", dt=BF16, t=NT, e=E)
        c.at = 0
        lo2 = c.take(NT * 2 * P, "p (t w n) -> p t w n", dt=BF16, t=NT, w=2)
        c.at = 15360
        bits = c.take(BITS * E, "p (b e) -> p b e", dt=I32, b=BITS)
        bitf = c.take(BITS * E, "p (b e) -> p b e", b=BITS)
        work = c.take(3 * P, "p (a n) -> p a n", a=3)
        posi = c.take(3 * P, "p (a n) -> p a n", dt=I32, a=3)
        c.at = after_common
        h2 = c.take(4 * HID, "p (u n) -> p u n", u=4)
        h2T = c.take(2 * HID, "p (u m n) -> p u m n", u=2, m=MC)
        h2s = c.take(2 * 2 * HID, "p (a u m n) -> p a u m n", dt=F16, a=2, u=2, m=MC)
        zTs = c.take(2 * 2 * KC * SQ, "p (a u k n) -> p a u k n", dt=F16, a=2, u=2, k=KC)
        sign = c.take(HID * KC, dt=BF16)
        below = c.take(HID * KC, dt=BF16)
        tern = [ffw[:, a, 0:HID * KC // 2].bitcast(BF16) for a in range(2)]
        c.at = 0
        dft = c.take(5 * KC * D, "p (a k n) -> p a k n", a=5, k=KC)
        ABT = c.take(2 * KC * D, "p (a k n) -> p a k n", a=2, k=KC)
        mrow = c.take(3 * NB * SK, "p (a n) -> p a n", a=3)
        mrow_i = c.take(3 * NB * SK, "p (a n) -> p a n", a=3, dt=I32)
        mrow_r = c.take(NB * SK)
        mrow_b = c.take(NB * SK, dt=BF16)
        fside_r = c.take(NB * SK)

        c = Cut(small)
        st = c.take(24, "p (t n) -> p t n", t=4)
        mv = c.take(8, "p (t n) -> p t n", t=4)
        ve = c.take(4)
        rstd = c.take(4)
        mx = c.take(4 * HC, "p (b h) -> p b h", b=4)
        sm = c.take(4 * HC, "p (b h) -> p b h", b=4)
        rs = c.take(4 * HC, "p (b h) -> p b h", b=4)
        logit = c.take(NT * E, "p (t e) -> p t e", t=NT)
        prob = c.take(NT * E, "p (t e) -> p t e", t=NT)
        pos = c.take(NT * E, "p (t e) -> p t e", t=NT)
        thr = c.take(E, dt=I32)
        cand = c.take(E, dt=I32)
        flag = c.take(E, dt=I32)
        cnt = c.take(E)
        sumT = c.take(NT)
        gmax = c.take(NT)
        sel = c.take(NT * E, "p (t e) -> p t e", dt=BF16, t=NT)
        sel2 = c.take(NT * E, "p (t e) -> p t e", dt=BF16, t=NT)
        idx = c.take(16, dt=I32)
        slot16 = c.take(16)
        wtok = c.take(NT)
        slotf = c.take(NT)
        slot_i = c.take(NT, dt=I32)
        b1u = c.take(2 * MC, "p (u m) -> p u m", u=2)
        wsl = c.take(4, "p (u j) -> p u j", u=2)
        gam = c.take(8)
        b1T = sb("b1T", [P, (E + 1) * MC], F32)
        lnwb = sb("lnwb", [P, 2, MC], F32)
        onesf = sb("onesf", [P, P], F32)
        iota16 = sb("iota16", [P, 16], F32)
        tokt = sb("tokt", [P, NT + 2 + E + P], F32)
        tcol, pcol, m8 = tokt[:, 0:NT], tokt[:, NT:NT + 1], tokt[:, NT + 2:NT + 2 + E]
        blk = tokt[:, NT + 2 + E:].rearrange("p (e a) -> p e a", e=E)

        load = sems("load", "x base weights dft masks shared ternary b2row")
        s_phase = ctx.enter_context(nc.semaphore("phase_done"))
        s_store = ctx.enter_context(nc.semaphore("stored"))

        def in_range(t):
            return not isinstance(t, int) or 0 <= t < NT

        def phase_end(eng, n):
            eng.drain().then_inc(s_phase, 1)
            eng.wait_ge(s_phase, 5 * n)

        ln_names = "var rstd z zT_ps zT_sb"
        kv_names = "cT K_ps V_ps KT_sb V_sb"
        su = sems("setup", "AB_ps AB_sb M_ps tanh gsum_in gsum_ps gsum_out tri")
        R = NB // 2
        BASE = {0: 0, 1: 0, 2: R, 3: R}
        one = sems("one", f"{ln_names} {kv_names} q_ps q_sb s_ps nmax p_sb pT_ps pT_sb y_ps x VT_sb")
        multi = sems("multi", f"{ln_names} {kv_names} q_ps q_sb kbd s_ps sub p_exp rsum p_norm pT_ps pT_sb "
                              "O_ps O_sb y_ps x")
        gt = sems("gate", f"{ln_names} zT_all l_ps l_sb stored")
        f1 = sems("ffn1", f"{ln_names} y_ps x")
        f2 = sems("ffn2", f"{ln_names} zTs h_ps h_sb st2 rstd2 n2 nT_ps nT_sb nTh nTs y_ps x")
        sh = sems("shared", "cmp cnt_ps h_ps h_sb y_ps x")
        rt = sems("route", "logit prob_exp prob probs_out rank_in rank_ps hot idx_ps idxf slot_out slot_in sT_ps idx c_ps c_in")
        ex = sems("experts", "w0 w1 gather0 gather1 idx b1 xT_ps xT_sb h_ps h_sb y_ps y_sb o0 o1 e0 e1 acc")
        fin = sems("final", "g0 g1 x")

        block = ctx.enter_context(nc.Block())
        ds = bass.ds
        N_ONE = {0: 2, 3: 9}

        @block.sync
        def _(sp):
            sp.dma_start(cols[:, :], d["cols"]).then_inc(load["base"], 16)
            sp.dma_start(ident[:, :], d["ident"]).then_inc(load["base"], 16)
            sp.dma_start(tokt[:, :], d["tokt"]).then_inc(load["base"], 16)
            sp.dma_start(headmask[:, :], d["headmask"]).then_inc(load["base"], 16)
            sp.dma_start(iota16[:, :], d["iota16"]).then_inc(load["base"], 16)
            sp.dma_start(tg[:, :], d["g"].partition_broadcast(P)).then_inc(load["base"], 16)
            sp.dma_start(bits[:, :, :], d["bits"]).then_inc(load["base"], 16)
            sp.dma_start(gates[:, :, :, :], d["gates"]).then_inc(load["base"], 16)
            sp.dma_start(b1T[:, :], d["b1T"]).then_inc(load["base"], 16)
            sp.dma_start(lnwb[:, :, :], d["lnwb"]).then_inc(load["base"], 16)
            for r, n in enumerate(ROWS):
                sp.dma_start(rows[:, r, :], d["rows"][r].partition_broadcast(P)).then_inc(load["base"], 16)
            sp.dma_start(mrow_i[0:1, 0, :], d["m0"]).then_inc(load["masks"], 16)
            sp.dma_start(mrow_i[0:1, 2, :], d["m2"]).then_inc(load["masks"], 16)
            sp.dma_start(mrow_i[0:1, 1, 0:NB * SK // 4].bitcast(mybir.dt.uint8), d["m1"]).then_inc(load["masks"], 16)
            sp.dma_start(fside_r[0:1, :], d["fside"]).then_inc(load["masks"], 16)
            sp.dma_start(ctxT[:, :, :], d["ctxT"]).then_inc(load["weights"], 16)
            sp.dma_start(x[:, :, :], d["x"]).then_inc(load["x"], 16)
            for n in WEIGHTS[:-4] + ["o3"]:
                sp.dma_start(W[n][:, :, :], d["W" + n]).then_inc(load["weights"], 16)
            for a, n in enumerate(["cosm", "sinm", "nsinm", "wr", "wi"]):
                sp.dma_start(dft[:, a, :, :], d[n]).then_inc(load["dft"], 16)
            for a in range(2):
                sp.dma_start(ffw[:, a, :], d[f"shared{a}"]).then_inc(load["shared"], 16)

            eo_v = eo.rearrange("(e t p) n -> p e t n", p=P, t=TB)

            def first_experts(L):
                for u in range(2):
                    for a in range(2):
                        sp.dma_start(ew[:, u, a, :], d[f"w{a}_{L}"][u]).then_inc(ex[f"w{u}"], 16)

            def experts(L):
                def weights(i, b, u):
                    sp.wait_ge(ex["y_ps"], i * 2 + u + 1)
                    for a in range(2):
                        sp.dma_start(ew[:, u, a, :],
                                     d[f"w{a}_{L}"][ds(b * 2 + u + 2, 1), :, :].rearrange("e p n -> p (e n)"))\
                          .then_inc(ex[f"w{u}"], 16)

                def store(i, b, u):
                    sp.wait_ge(ex["y_sb"], i * 2 + u + 1)
                    sp.dma_start(eo_v[:, ds(b * 2 + u, 1), :, :].rearrange("p e t n -> p (e t) n"), eout[:, u, :, :])\
                      .then_inc(ex[f"e{u}"], 16)

                with sp.Fori(0, E // 2 - 1) as b:
                    for u in range(2):
                        weights(b + BASE[L], b, u)
                        if L == 3:
                            store(b + BASE[L], b, u)
                if L == 3:
                    for u in range(2):
                        store(BASE[L] + E // 2 - 1, E // 2 - 1, u)

            first_experts(0)
            phase_end(sp, 1)
            phase_end(sp, 2)
            for n in ("q3", "k3", "v3"):
                sp.dma_start(W[n][:, :, :], d["W" + n]).then_inc(load["weights"], 16)
            zr = zrow.rearrange("(t p) n -> p t n", p=P)
            q = gt
            with sp.Fori(0, R) as i:
                for u in range(2):
                    sp.wait_ge(q["z"], i * 2 + u + 1)
                    sp.dma_start(zr[:, ds(i * 4 + 2 * u, 2), 0:D], z[:, 2 * u:2 * u + 2, :]).then_inc(q["stored"], 16)
            phase_end(sp, 3)
            q = rt
            sp.wait_ge(q["prob"], 1)
            sp.dma_start(zr[:, :, D:ROW], prob).then_inc(q["probs_out"], 16)
            phase_end(sp, 4)

            def route(L, q):
                n = 1 + L // 3
                sp.wait_ge(q["idxf"], n)
                sp.dma_start(slotd[L // 3], work[:, 1, 0:16]).then_inc(q["slot_out"], 16)
                sp.wait_ge(q["slot_out"], 16 * n)
                sp.dma_start(work[0:16, 2, :], slotd[L // 3].rearrange("(j a) b -> j (a b)", j=16)).then_inc(q["slot_in"], 16)

            sp.dma_start(acc.rearrange("(t p) n -> p t n", p=P), x[:, :, :]).then_inc(ex["acc"], 16)
            route(0, q)
            sp.wait_ge(q["idx"], 1)
            sp.dma_start(b2row[:, :, :], d["b2"].partition_broadcast(P)).then_inc(load["b2row"], 16)
            phase_end(sp, 5)
            for a in range(2):
                sp.dma_start(ffw[:, a, :], d[f"tern{a}"]).then_inc(load["ternary"], 16)
            experts(0)
            phase_end(sp, 6)
            sp.dma_start(x[:, :, :], acc.rearrange("(t p) n -> p t n", p=P)).then_inc(load["x"], 16)
            first_experts(3)
            for n in range(7, 12):
                phase_end(sp, n)
            q = gt
            zr3 = zrow3.rearrange("(t p) n -> p t n", p=P)
            with sp.Fori(0, R) as b:
                for u in range(2):
                    sp.wait_ge(q["z"], (b + R) * 2 + u + 1)
                    sp.dma_start(zr3[:, ds(b * 4 + 2 * u, 2), :], z[:, 2 * u:2 * u + 2, :]).then_inc(q["stored"], 16)
            phase_end(sp, 12)
            route(3, rt)
            phase_end(sp, 13)
            experts(3)
            phase_end(sp, 14)
            phase_end(sp, 15)
            sp.dma_start(out, x[:, :, :]).then_inc(s_store, 16)
            sp.wait_ge(s_store, 16)
            for u in range(2):
                sp.wait_ge(ex[f"o{u}"], 32 * (E // 2))
                sp.wait_ge(ex[f"e{u}"], 16 * (E // 2))
            sp.wait_ge(gt["stored"], 16 * NT)

        @block.gpsimd
        def _(g):
            def rstd_step(q, i):
                g.wait_ge(q["var"], i + 1)
                g.tensor_tensor(rstd, ve, mhalf[:, :], ALU.pow).then_inc(q["rstd"], 1)

            g.memset(mhalf[:, :], -0.5)
            g.memset(ones[:, :], 1.0)
            g.memset(onesf[:, :], 1.0)
            g.memset(tri[:, :], 1.0)
            g.memset(brow[:, :, :], 0.0)
            g.drain()
            g.affine_select(out=tri[:, :], in_=tri[:, :], compare_op=ALU.is_ge, fill=0.0,
                            base=0, pattern=[[1, P]], channel_multiplier=-1).then_inc(su["tri"], 1)
            phase_end(g, 1)

            def one_head(L):
                q = one
                with g.Fori(0, NB // 2) as b:
                    i = b + BASE[L]
                    for u in range(2):
                        g.tensor_copy(cT[:, u], ctxT[:, :, ds((b * 2 + u) * SK, SK)]).then_inc(q["cT"], 1)
                    rstd_step(q, i)
                    g.wait_ge(q["x"], i * 4 + 4)

            one_head(0)
            phase_end(g, 2)
            with g.Fori(0, NB // 2) as i:
                rstd_step(gt, i)
                for u in range(2):
                    g.wait_ge(gt["zT_sb"], i * 2 + u + 1)
                    g.tensor_copy(zT_all[:, :, ds((i * 2 + u) * SQ, SQ)], zT[:, u]).then_inc(gt["zT_all"], 1)
            phase_end(g, 3)
            phase_end(g, 4)
            phase_end(g, 5)

            def experts(L):
                q = ex
                src = zrow if L == 0 else zrow3
                rounds = BASE[L]

                def gather(e):
                    u = e % 2
                    g.tensor_copy(b1u[:, u], b1T[:, e * MC:(e + 1) * MC]).then_inc(q["b1"], 1)
                    for j in range(TB):
                        g.indirect_dma_start(
                            G[:, u, j, 0:src.shape[1]], None, src,
                            bass.IndirectOffsetOnAxis(ap=idx[:, TB * e + j:TB * e + j + 1], axis=0))\
                         .then_inc(q[f"gather{u}"], 16)

                if L == 0:
                    g.wait_ge(rt["probs_out"], 16)
                g.wait_ge(gt["stored"], 16 * (NT // 2) * (1 + L // 3))
                gather(0)
                gather(1)
                if L == 0:
                    g.wait_ge(q["acc"], 16)
                for e in range(E):
                    g.wait_ge(q["y_sb"], 2 * rounds + e + 1)
                    if e + 2 < E:
                        gather(e + 2)
                    if L == 0:
                        if e >= 1:
                            g.wait_ge(q[f"o{(e - 1) % 2}"], 32 * ((e - 1) // 2 + 1))
                        for j in range(TB):
                            g.indirect_dma_start(
                                acc, bass.IndirectOffsetOnAxis(ap=idx[:, TB * e + j:TB * e + j + 1], axis=0),
                                eout[:, e % 2, j, :], None, compute_op=ALU.add).then_inc(q[f"o{e % 2}"], 16)

            experts(0)
            phase_end(g, 6)

            def multi_head(L):
                q = multi
                with g.Fori(0, NB // 2) as b:
                    i = b + BASE[L]
                    for u in range(2):
                        g.tensor_copy(cT[:, u], ctxT[:, :, ds((b * 2 + u) * SK, SK)]).then_inc(q["cT"], 1)
                    rstd_step(q, i)
                    for u in range(2):
                        g.wait_ge(q["KT_sb"], i * 2 + u + 1)
                        for k in range(KC):
                            g.tensor_tensor(KBD[:, u, k], bcast(KT[:, u, k], 1, HC), bcast(headmask[:, :], 2, SK),
                                            ALU.mult).then_inc(q["kbd"], 1)
                    for n in range(8):
                        g.wait_ge(q["rsum"], i * 8 + n + 1)
                        g.tensor_tensor(Pr[:, n % 4], Pr[:, n % 4], bcast(rs[:, n % 4], 2, SK), ALU.mult)\
                         .then_inc(q["p_norm"], 1)
                    g.wait_ge(q["x"], i * 2 + 2)

            multi_head(1)
            phase_end(g, 7)
            with g.Fori(0, NB // 2) as i:
                rstd_step(f1, i)
            phase_end(g, 8)
            multi_head(2)
            phase_end(g, 9)
            q = f2

            def step(r, n):
                t = r * 4 + n
                if in_range(t):
                    g.wait_ge(q["st2"], t + 1)
                    g.tensor_tensor(rs[:, n, 0:1], sm[:, n, 0:1], mhalf[:, 0:1], ALU.pow).then_inc(q["rstd2"], 1)
                if in_range(r * 4 + 4):
                    if n == 0:
                        rstd_step(q, r + 1)
                if in_range(t - 2):
                    g.wait_ge(q["nTh"], t - 1)
                    g.tensor_tensor(h2s[:, 1, n % 2], h2T[:, n % 2], h2s[:, 0, n % 2], ALU.subtract).then_inc(q["nTs"], 1)

            rstd_step(q, 0)
            for n in range(4):
                step(0, n)
            with g.Fori(1, NT // 4 - 1) as r:
                for n in range(4):
                    step(r, n)
            for t in range(NT - 4, NT + 2):
                step(t // 4, t % 4)
            phase_end(g, 10)
            one_head(3)
            phase_end(g, 11)
            with g.Fori(0, R) as b:
                rstd_step(gt, b + R)
            phase_end(g, 12)
            phase_end(g, 13)
            experts(3)
            phase_end(g, 14)
            for u in range(2):
                g.wait_ge(ex[f"e{u}"], 16 * (E // 2))
            for t in range(NT):
                if t >= 4:
                    g.wait_ge(fin["x"], t // 2 - 1)
                g.indirect_dma_start(eout[:, t // 2 % 2, t % 2, :], None, eo,
                                     bass.IndirectOffsetOnAxis(ap=slot_i[:, t:t + 1], axis=0))\
                 .then_inc(fin[f"g{t // 2 % 2}"], 16)
            phase_end(g, 15)

        @block.tensor
        def _(pe):
            def mm(o, l, r, a, b):
                return pe.matmul(o, l, r, start=a, stop=b)

            def transposed_z(q, i, u):
                pe.wait_ge(q["z"], i * 2 + u + 1)
                o = MISC[u][:, :].rearrange("p (k n) -> p k n", k=KC)
                for k in range(KC):
                    for t in range(TB):
                        m = pe.transpose(o[:, k, t * P:(t + 1) * P], z[:, 2 * u + t, k * P:(k + 1) * P], ident[:, :])
                m.then_inc(q["zT_ps"], 1)

            def project_q(q, L, i, u):
                pe.wait_ge(q["zT_sb"], i * 2 + u + 1)
                o = MISC[u][:, :].rearrange("p (k n) -> p k n", k=KC)
                for m_ in range(KC):
                    for k in range(KC):
                        m = mm(o[:, m_, :], W[f"q{L}"][:, k, m_ * P:(m_ + 1) * P], zT[:, u, k, :], k == 0, k == KC - 1)
                m.then_inc(q["q_ps"], 1)

            def keys_values(q, L, i, b, u):
                pe.wait_ge(q["cT"], i * 2 + u + 1)
                bank = MISC[u]
                for m_ in range(KC):
                    for k in range(KC):
                        m = mm(bank[:, m_ * SK:(m_ + 1) * SK], W[f"k{L}"][:, k, m_ * P:(m_ + 1) * P], cT[:, u, k, :],
                               k == 0, k == KC - 1)
                if L != 3:
                    for k in range(KC):
                        m = mm(bank[0:SK, 256:512], cT[:, u, k, :], W[f"v{L}"][:, k, :], k == 0, k == KC - 1)
                    m.then_inc(q["K_ps"], 1)
                else:
                    for m_ in range(KC):
                        for k in range(KC):
                            m = mm(bank[:, 256 + m_ * SK:256 + (m_ + 1) * SK], W["v3"][:, k, m_ * P:(m_ + 1) * P],
                                   cT[:, u, k, :], k == 0, k == KC - 1)
                    m.then_inc(q["K_ps"], 1)
                    pe.wait_ge(q["VT_sb"], b * 2 + u + 1)
                    for k in range(KC):
                        m = mm(bank[0:SK, 256:512], VT1[:, u, k, :], W["o3"][:, k, :], k == 0, k == KC - 1)
                    m.then_inc(q["V_ps"], 1)

            pe.wait_ge(load["base"], 16 * (10 + len(ROWS)))
            pe.wait_ge(load["dft"], 16 * 5)
            C, S, nS, Wr, Wi = range(5)
            for a, terms in enumerate([[(Wr, C), (Wi, S)], [(Wi, C), (Wr, nS)]]):
                o = psum[a][:, :].rearrange("p (k n) -> p k n", k=KC)
                for m_ in range(KC):
                    for n, (w, f) in enumerate(terms):
                        for k in range(KC):
                            m = mm(o[:, m_, :], dft[:, w, k, m_ * P:(m_ + 1) * P], dft[:, f, k, :],
                                   n == 0 and k == 0, n == 1 and k == KC - 1)
            m.then_inc(su["AB_ps"], 1)
            pe.wait_ge(su["AB_sb"], 1)
            o = psum[2][:, :].rearrange("p (k n) -> p k n", k=KC)
            for m_ in range(KC):
                for a, f in enumerate([C, nS]):
                    for k in range(KC):
                        m = mm(o[:, m_, :], ABT[:, a, k, m_ * P:(m_ + 1) * P], dft[:, f, k, :],
                               a == 0 and k == 0, a == 1 and k == KC - 1)
            m.then_inc(su["M_ps"], 1)
            phase_end(pe, 1)

            def one_head(L):
                q = one
                pe.wait_ge(load["weights"], 16 * (1 + len(WEIGHTS) - (3 if L == 0 else 0)))
                with pe.Fori(0, NB // 2) as b:
                    i = b + BASE[L]
                    for u in range(2):
                        keys_values(q, L, i, b, u)
                    for u in range(2):
                        pe.wait_ge(q["V_sb"], i * 2 + u + 1)
                        pe.wait_ge(q["KT_sb"], i * 2 + u + 1)
                        transposed_z(q, i, u)
                    for u in range(2):
                        project_q(q, L, i, u)
                    for u in range(2):
                        pe.wait_ge(q["q_sb"], i * 2 + u + 1)
                        o = psum[u][:, 0:TB * SK].rearrange("p (t n) -> p t n", t=TB)
                        if L == 0:
                            mm(o, ones[0:96, :], bcast(brow[:, 0, ds((b * 2 + u) * SK, SK)], 1, TB), True, False)
                        for t in range(TB):
                            for k in range(KC):
                                m = mm(o[:, t, :], qT[:, u, k, t * P:(t + 1) * P], KT[:, u, k, :],
                                       L == 3 and k == 0, k == KC - 1 and (L == 3 or t == TB - 1))
                        m.then_inc(q["s_ps"], 1)
                    for u in range(2):
                        pe.wait_ge(q["p_sb"], i * 2 + u + 1)
                        for t in range(TB):
                            m = pe.transpose(psum[2 + u][0:SK, t * P:(t + 1) * P], P1[:, u, t, :], ident[:, :])
                        m.then_inc(q["pT_ps"], 1)
                    for u in range(2):
                        pe.wait_ge(q["pT_sb"], i * 2 + u + 1)
                        for t in range(TB):
                            m = mm(MISC[u][:, t * D:(t + 1) * D], PT1[0:SK, u, t * P:(t + 1) * P], V1[0:SK, u, :], True, True)
                        m.then_inc(q["y_ps"], 1)
                    pe.wait_ge(q["x"], i * 4 + 4)

            one_head(0)
            phase_end(pe, 2)

            def gate(L):
                q = gt
                with pe.Fori(0, NB // 2) as b:
                    i = b + BASE[L]
                    for u in range(2):
                        transposed_z(q, i, u)
                    for u in range(2):
                        pe.wait_ge(q["zT_sb"], i * 2 + u + 1)
                        for t in range(TB):
                            for k in range(KC):
                                m = mm(psum[u][:, t * E:(t + 1) * E], zT[:, u, k, t * P:(t + 1) * P],
                                       gates[:, L // 3, k, :], k == 0, k == KC - 1)
                        m.then_inc(q["l_ps"], 1)
                    pe.wait_ge(q["l_sb"], i * 2 + 2)

            gate(0)
            phase_end(pe, 3)

            pe.wait_ge(load["shared"], 32)
            ws1 = ffw[:, 0, :].rearrange("p (k n) -> p k n", k=KC)
            ws2 = ffw[:, 1, :].rearrange("p (m n) -> p m n", m=MC)
            q = sh
            with pe.Fori(0, T // 512) as i:
                for m_ in range(MC):
                    if m_ >= 4:
                        pe.wait_ge(q["h_sb"], i * MC + m_ - 3)
                    for k in range(KC):
                        m = mm(psum[m_ % 4][:, :], ws1[:, k, m_ * P:(m_ + 1) * P], zT_all[:, k, ds(i * 512, 512)],
                               k == 0, k == KC - 1)
                    m.then_inc(q["h_ps"], 1)
                    pe.wait_ge(q["cmp"], i * HALF + m_ + 1)
                    mm(psum[6][:, 0:P], ones[:, :], sel.rearrange("p t e -> p (t e)"), True, True).then_inc(q["cnt_ps"], 1)
                pe.wait_ge(q["h_sb"], i * MC + MC)
                for t in range(4):
                    for k in range(MC):
                        m = mm(psum[4 + t // 2][:, (t % 2) * D:(t % 2 + 1) * D], hT[:, k, t * P:(t + 1) * P], ws2[:, k, :],
                               k == 0, k == MC - 1)
                    if t % 2:
                        m.then_inc(q["y_ps"], 1)
                pe.wait_ge(q["x"], i * 2 + 2)
            phase_end(pe, 4)

            def ranks(bank, s):
                o = bank[:, 0:P].rearrange("p (t e) -> p t e", t=NT)
                m = mm(o, tri[:, :], s, True, False)
                for t in range(NT - 1):
                    m = mm(o[:, t + 1:, :], ones[:, :], bcast(s[:, t, :], 1, NT - 1 - t), False, t == NT - 2)
                return m

            def route(L):
                q = rt
                n = 1 + L // 3
                if L == 0:
                    pe.wait_ge(q["c_in"], 1)
                    mm(psum[0][:, 0:P], ones[:, :], sel.rearrange("p t e -> p (t e)"), True, True)
                    ranks(psum[1], sel2).then_inc(q["c_ps"], 1)
                pe.wait_ge(q["rank_in"], n)
                ranks(psum[2], sel).then_inc(q["rank_ps"], 1)
                pe.wait_ge(q["hot"], n)
                for t in range(NT):
                    m = mm(psum[3][:, 0:2 * P], hi1[:, t].rearrange("p e a -> p (e a)"),
                           lo2[:, t].rearrange("p w n -> p (w n)"), t == 0, t == NT - 1)
                m.then_inc(q["idx_ps"], 1)
                pe.wait_ge(q["slot_in"], 16 * n)
                pe.transpose(psum[4][:, 0:16], work[0:16, 2, :], ident[0:16, 0:16]).then_inc(q["sT_ps"], 1)

            route(0)
            phase_end(pe, 5)

            def experts(L):
                q = ex

                def prepare(i, u):
                    pe.wait_ge(q[f"gather{u}"], i * 32 + 32)
                    o = MISC[u][:, :].rearrange("p (k n) -> p k n", k=KC)
                    for k in range(KC):
                        for t in range(TB):
                            m = pe.transpose(o[:, k, t * P:(t + 1) * P], G[:, u, t, k * P:(k + 1) * P], ident[:, :])
                    m.then_inc(q["xT_ps"], 1)

                def first(i, u):
                    pe.wait_ge(q["xT_sb"], i * 2 + u + 1)
                    pe.wait_ge(q[f"w{u}"], i * 32 + 32)
                    w = ew[:, u, 0, :].rearrange("p (k n) -> p k n", k=KC)
                    for m_ in range(MC):
                        if m_ % 2 == 0:
                            pe.wait_ge(q["h_sb"], i * 2 * MC + u * MC + m_ - 6) if u * MC + m_ >= 8 else None
                        for k in range(KC):
                            m = mm(psum[m_ // 2][:, (m_ % 2) * CAP:(m_ % 2 + 1) * CAP], w[:, k, m_ * P:(m_ + 1) * P],
                                   xeT[:, u, k, :], k == 0, k == KC - 1)
                        if m_ % 2:
                            m.then_inc(q["h_ps"], 1)

                def second(i, u):
                    pe.wait_ge(q["h_sb"], i * 2 * MC + (u + 1) * MC)
                    w = ew[:, u, 1, :].rearrange("p (m n) -> p m n", m=MC)
                    for t in range(TB):
                        for k in range(MC):
                            m = mm(psum[4 + u][:, t * D:(t + 1) * D], heT[:, u, k, t * P:(t + 1) * P], w[:, k, :],
                                   k == 0, k == MC - 1)
                    m.then_inc(q["y_ps"], 1)

                with pe.Fori(0, E // 2) as b:
                    i = b + BASE[L]
                    prepare(i, 0)
                    first(i, 0)
                    prepare(i, 1)
                    second(i, 0)
                    first(i, 1)
                    second(i, 1)

            pe.wait_ge(su["gsum_in"], 1)
            mm(psum[5][:, 0:2], onesf[:, :], gam[:, 0:2], True, True).then_inc(su["gsum_ps"], 1)
            pe.wait_ge(su["gsum_out"], 1)
            experts(0)
            phase_end(pe, 6)

            def multi_head(L):
                q = multi

                def scores(i, b, n):
                    u, t, c = n // 4, n // 2 % 2, n % 2
                    if n % 4 == 0:
                        pe.wait_ge(q["q_sb"], i * 2 + u + 1)
                        pe.wait_ge(q["kbd"], i * 4 + 2 * u + 2)
                    if n >= 2:
                        pe.wait_ge(q["sub"], i * 8 + n - 1)
                    for j in range(2):
                        o = psum[2 * (n % 2) + j][:, 0:4 * SK].rearrange("p (h n) -> p h n", h=4)
                        mm(o, ones[0:96, :], bcast(brow[:, L, ds((b * 2 + u) * SK, SK)], 1, 4), True, False)
                        m = mm(o, qT[:, u, c, t * P:(t + 1) * P], KBD[:, u, c, 4 * j:4 * j + 4, :], False, True)
                    m.then_inc(q["s_ps"], 1)

                def turn(i, n):
                    pe.wait_ge(q["p_norm"], i * 8 + n + 1)
                    for j in range(2):
                        if n >= 1:
                            pe.wait_ge(q["pT_sb"], i * 16 + 2 * n + j - 1)
                        for h in range(4):
                            m = pe.transpose(psum[4 + j][0:SK, h * P:(h + 1) * P], Pr[:, n % 4, 4 * j + h, :], ident[:, :])
                        m.then_inc(q["pT_ps"], 1)

                def attend(i, u):
                    pe.wait_ge(q["pT_sb"], i * 16 + 8 * u + 8)
                    o = MISC[u][:, :].rearrange("p (k n) -> p k n", k=KC)
                    for c in range(KC):
                        for j in range(2):
                            for g_ in range(4):
                                h = c * HC + 2 * g_ + j
                                m = mm(o[32 * g_:32 * g_ + 32, c, :], Vp[0:SK, u, h, :], PT[0:SK, u, h, :], j == 0, j == 1)
                    m.then_inc(q["O_ps"], 1)

                def output(i, u):
                    pe.wait_ge(q["O_sb"], i * 2 + u + 1)
                    for t in range(TB):
                        for k in range(KC):
                            m = mm(MISC[u][:, t * D:(t + 1) * D], OT[:, u, k, t * P:(t + 1) * P], W[f"o{L}"][:, k, :],
                                   k == 0, k == KC - 1)
                    m.then_inc(q["y_ps"], 1)

                with pe.Fori(0, NB // 2) as b:
                    i = b + BASE[L]
                    for u in range(2):
                        keys_values(q, L, i, b, u)
                    for u in range(2):
                        pe.wait_ge(q["V_sb"], i * 2 + u + 1)
                        pe.wait_ge(q["KT_sb"], i * 2 + u + 1)
                        transposed_z(q, i, u)
                    for u in range(2):
                        project_q(q, L, i, u)
                    for n in range(8 + 3):
                        if n < 8:
                            scores(i, b, n)
                        if n >= 3:
                            turn(i, n - 3)
                        if n == 7:
                            attend(i, 0)
                            output(i, 0)
                    attend(i, 1)
                    output(i, 1)
                    pe.wait_ge(q["x"], i * 2 + 2)

            multi_head(1)
            phase_end(pe, 7)

            q = f1
            with pe.Fori(0, NB // 2) as i:
                for u in range(2):
                    transposed_z(q, i, u)
                for u in range(2):
                    pe.wait_ge(q["zT_sb"], i * 2 + u + 1)
                    for t in range(TB):
                        for k in range(KC):
                            m = mm(psum[u][:, t * D:(t + 1) * D], zT[:, u, k, t * P:(t + 1) * P], Mf[:, k, :],
                                   k == 0, k == KC - 1)
                    m.then_inc(q["y_ps"], 1)
                pe.wait_ge(q["x"], i * 2 + 2)
            phase_end(pe, 8)
            multi_head(2)
            phase_end(pe, 9)
            q = f2
            wf = tern[0].rearrange("p (k n) -> p k n", k=KC)
            wp = tern[1].rearrange("p (m n) -> p m n", m=MC)

            def turn_z(r, u):
                pe.wait_ge(q["z"], r * 2 + u + 1)
                if in_range(r * 4 - 4) or u:
                    pe.wait_ge(q["zT_sb"], r * 2 + u)
                o = psum[6][:, :].rearrange("p (k n) -> p k n", k=KC)
                for k in range(KC):
                    for t in range(TB):
                        m = pe.transpose(o[:, k, t * P:(t + 1) * P], z[:, 2 * u + t, k * P:(k + 1) * P], ident[:, :])
                m.then_inc(q["zT_ps"], 1)

            def step(r, n):
                t = r * 4 + n
                if in_range(t):
                    pe.wait_ge(q["zTs"], r * 2 + n // 2 + 1)
                    if in_range(t - 2):
                        pe.wait_ge(q["h_sb"], t - 1)
                    for j in range(2):
                        for k in range(KC):
                            for a in range(2):
                                m = mm(psum[2 * (n % 2) + j][:, :], zTs[:, a, n // 2, k, (n % 2) * P:(n % 2 + 1) * P],
                                       wf[:, k, j * 512:(j + 1) * 512], k == 0 and a == 0, k == KC - 1 and a == 1)
                    m.then_inc(q["h_ps"], 1)
                if in_range(t - 2):
                    pe.wait_ge(q["n2"], t - 1)
                    if in_range(t - 3):
                        pe.wait_ge(q["nT_sb"], t - 2)
                    for h in range(MC):
                        m = pe.transpose(psum[4 + h // 4][:, (h % 4) * P:(h % 4 + 1) * P],
                                         h2[:, (n + 2) % 4, h * P:(h + 1) * P], ident[:, :])
                    m.then_inc(q["nT_ps"], 1)
                if in_range(t - 4):
                    pe.wait_ge(q["nTs"], t - 3)
                    if in_range(t - 5):
                        pe.wait_ge(q["x"], t - 4)
                    for h in range(MC):
                        for a in range(2):
                            m = mm(psum[7][:, 0:D], h2s[:, a, n % 2, h, :], wp[:, h, :],
                                   h == 0 and a == 0, h == MC - 1 and a == 1)
                    m.then_inc(q["y_ps"], 1)
                if n in (1, 2) and in_range(r * 4 + 4):
                    turn_z(r + 1, n - 1)

            for u in range(2):
                turn_z(0, u)
            for n in range(4):
                step(0, n)
            with pe.Fori(1, NT // 4 - 1) as r:
                for n in range(4):
                    step(r, n)
            for t in range(NT - 4, NT + 4):
                step(t // 4, t % 4)
            phase_end(pe, 10)
            one_head(3)
            phase_end(pe, 11)
            gate(3)
            phase_end(pe, 12)
            route(3)
            phase_end(pe, 13)
            experts(3)
            phase_end(pe, 14)
            phase_end(pe, 15)

        @block.scalar
        def _(act):
            def copy(o, i_):
                return nc.scalar.activation(o, i_, ACT.Copy)

            def take_z(q, i, u):
                act.wait_ge(q["zT_ps"], i * 2 + u + 1)
                copy(zT[:, u], MISC[u][:, :].rearrange("p (k n) -> p k n", k=KC)).then_inc(q["zT_sb"], 1)

            def take_q(q, L, i, u):
                act.wait_ge(q["q_ps"], i * 2 + u + 1)
                for k in range(KC):
                    c = COL[f"q{L}"] + k
                    m = nc.scalar.activation(qT[:, u, k], MISC[u][:, k * SQ:(k + 1) * SQ], ACT.Identity, bias=cols[:, c:c + 1])
                m.then_inc(q["q_sb"], 1)

            def take_k(q, L, i, u, scale):
                act.wait_ge(q["K_ps"], i * 2 + u + 1)
                for k in range(KC):
                    c = COL[f"k{L}"] + k
                    m = nc.scalar.activation(KT[:, u, k], MISC[u][:, k * SK:(k + 1) * SK], ACT.Identity,
                                             bias=cols[:, c:c + 1], scale=scale)
                m.then_inc(q["KT_sb"], 1)

            act.wait_ge(load["base"], 16 * (10 + len(ROWS)))
            nc.scalar.activation(tg[:, :], tg[:, :], ACT.Tanh).then_inc(su["tanh"], 1)
            act.wait_ge(su["AB_ps"], 1)
            for a in range(2):
                m = copy(ABT[:, a], psum[a][:, :].rearrange("p (k n) -> p k n", k=KC))
            m.then_inc(su["AB_sb"], 1)
            phase_end(act, 1)

            def one_head(L):
                q = one
                with act.Fori(0, NB // 2) as b:
                    i = b + BASE[L]
                    for u in range(2):
                        take_k(q, L, i, u, 1.0 / 16)
                        if L == 3:
                            for k in range(KC):
                                c = COL["v3"] + k
                                m = nc.scalar.activation(VT1[:, u, k], MISC[u][:, 256 + k * SK:256 + (k + 1) * SK],
                                                         ACT.Identity, bias=cols[:, c:c + 1])
                            m.then_inc(q["VT_sb"], 1)
                    for u in range(2):
                        take_z(q, i, u)
                    for u in range(2):
                        take_q(q, L, i, u)
                    for u in range(2):
                        act.wait_ge(q["nmax"], i * 2 + u + 1)
                        for t in range(TB):
                            m = nc.scalar.activation(P1[:, u, t, :], psum[u][:, t * SK:(t + 1) * SK], ACT.Exp,
                                                     bias=mx[:, u, t:t + 1], accum_out=sm[:, u, t:t + 1])
                        m.then_inc(q["p_sb"], 1)
                    for u in range(2):
                        act.wait_ge(q["pT_ps"], i * 2 + u + 1)
                        copy(PT1[0:SK, u, :], psum[2 + u][0:SK, 0:SQ]).then_inc(q["pT_sb"], 1)

            one_head(0)
            phase_end(act, 2)

            def gate(L):
                q = gt
                with act.Fori(0, NB // 2) as b:
                    i = b + BASE[L]
                    for u in range(2):
                        take_z(q, i, u)
                    act.wait_ge(q["l_ps"], i * 2 + 2)
                    if L == 0:
                        act.wait_ge(q["zT_all"], i * 2 + 2)
                act.wait_ge(rt["logit"], 1 + L // 3)
                nc.scalar.activation(prob, logit, ACT.Exp).then_inc(rt["prob_exp"], 1)

            gate(0)
            phase_end(act, 3)
            q = sh
            with act.Fori(0, T // 512) as i:
                for m_ in range(MC):
                    act.wait_ge(q["h_ps"], i * MC + m_ + 1)
                    nc.scalar.activation(hT[:, m_, :], psum[m_ % 4][:, :], ACT.Gelu_apprx_tanh,
                                         bias=b1T[:, E * MC + m_:E * MC + m_ + 1]).then_inc(q["h_sb"], 1)
            phase_end(act, 4)
            phase_end(act, 5)

            def experts(L):
                q = ex
                with act.Fori(0, E // 2) as b:
                    i = b + BASE[L]

                    def take_rows(u):
                        act.wait_ge(q["b1"], i * 2 + u + 1)
                        act.wait_ge(q["xT_ps"], i * 2 + u + 1)
                        copy(xeT[:, u], MISC[u][:, :].rearrange("p (k n) -> p k n", k=KC)).then_inc(q["xT_sb"], 1)

                    take_rows(0)
                    for u in range(2):
                        if u == 1:
                            take_rows(1)
                        for m_ in range(MC):
                            if m_ % 2 == 0:
                                act.wait_ge(q["h_ps"], i * MC + u * 4 + m_ // 2 + 1)
                            src = psum[m_ // 2][:, (m_ % 2) * CAP:(m_ % 2 + 1) * CAP]
                            if L == 0:
                                m = nc.scalar.activation(heT[:, u, m_, :], src, ACT.Gelu_apprx_tanh, bias=b1u[:, u, m_:m_ + 1])
                            else:
                                m = nc.scalar.activation(heT[:, u, m_, :], src, ACT.Relu)
                            m.then_inc(q["h_sb"], 1)

            experts(0)
            phase_end(act, 6)

            def multi_head(L):
                q = multi
                with act.Fori(0, NB // 2) as b:
                    i = b + BASE[L]
                    for u in range(2):
                        take_k(q, L, i, u, 0.25)
                    for u in range(2):
                        take_z(q, i, u)
                    for u in range(2):
                        take_q(q, L, i, u)

                    def take_O(u):
                        act.wait_ge(q["O_ps"], i * 2 + u + 1)
                        copy(OT[:, u], MISC[u][:, :].rearrange("p (k n) -> p k n", k=KC)).then_inc(q["O_sb"], 1)

                    for n in range(8 + 3):
                        if n < 8:
                            act.wait_ge(q["sub"], i * 8 + n + 1)
                            nc.scalar.activation(Pr[:, n % 4], Pr[:, n % 4], ACT.Exp).then_inc(q["p_exp"], 1)
                        if n >= 3:
                            w = n - 3
                            u, t, c = w // 4, w // 2 % 2, w % 2
                            for j in range(2):
                                act.wait_ge(q["pT_ps"], i * 16 + 2 * w + j + 1)
                                copy(PT[0:SK, u, c * HC + 4 * j:c * HC + 4 * j + 4, t * P:(t + 1) * P],
                                     psum[4 + j][0:SK, :].rearrange("p (h n) -> p h n", h=4)).then_inc(q["pT_sb"], 1)
                        if n == 7:
                            take_O(0)
                    take_O(1)

            multi_head(1)
            phase_end(act, 7)
            with act.Fori(0, NB // 2) as i:
                for u in range(2):
                    take_z(f1, i, u)
                act.wait_ge(f1["y_ps"], i * 2 + 2)
            phase_end(act, 8)
            multi_head(2)
            phase_end(act, 9)
            q = f2

            def take_turned_z(r, u):
                act.wait_ge(q["zT_ps"], r * 2 + u + 1)
                if in_range(r * 4 - 4):
                    act.wait_ge(q["zTs"], r * 2 + u - 1)
                    act.wait_ge(q["h_ps"], r * 4 + 2 * u - 2)
                copy(zTs[:, 0, u], psum[6][:, :].rearrange("p (k n) -> p k n", k=KC))
                copy(zT[:, u], psum[6][:, :].rearrange("p (k n) -> p k n", k=KC)).then_inc(q["zT_sb"], 1)

            def step(r, n):
                t = r * 4 + n
                if in_range(t):
                    act.wait_ge(q["h_ps"], t + 1)
                    if in_range(t - 4):
                        act.wait_ge(q["nT_ps"], t - 3)
                    for j in range(2):
                        m = nc.scalar.activation(h2[:, n, j * 512:(j + 1) * 512], psum[2 * (n % 2) + j][:, :], ACT.Gelu)
                    m.then_inc(q["h_sb"], 1)
                if in_range(t - 2):
                    act.wait_ge(q["nT_ps"], t - 1)
                    if in_range(t - 4):
                        act.wait_ge(q["nTs"], t - 3)
                    for h in range(MC):
                        m = nc.scalar.activation(h2T[:, n % 2, h, :], psum[4 + h // 4][:, (h % 4) * P:(h % 4 + 1) * P],
                                                 ACT.Identity, bias=lnwb[:, 1, h:h + 1], scale=lnwb[:, 0, h:h + 1])
                    m.then_inc(q["nT_sb"], 1)
                if n in (1, 3) and in_range(r * 4 + 4):
                    take_turned_z(r + 1, n // 2)

            for u in range(2):
                take_turned_z(0, u)
            for n in range(4):
                step(0, n)
            with act.Fori(1, NT // 4 - 1) as r:
                for n in range(4):
                    step(r, n)
            for t in range(NT - 4, NT + 2):
                step(t // 4, t % 4)
            phase_end(act, 10)
            one_head(3)
            phase_end(act, 11)
            gate(3)
            phase_end(act, 12)
            phase_end(act, 13)
            experts(3)
            phase_end(act, 14)
            phase_end(act, 15)

        @block.vector
        def _(v):
            V = nc.vector

            def norm(q, i, b, add=None):
                for t in range(4):
                    V.bn_stats(st[:, t, :], x[:, ds(b * 4 + t, 1), :].rearrange("p t n -> p (t n)"))
                v.drain()
                for t in range(4):
                    V.bn_aggr(mv[:, t, :], st[:, t, :])
                v.drain()
                V.tensor_scalar(ve, mv[:, :, 1], EPS, None, ALU.add).then_inc(q["var"], 1)
                v.wait_ge(q["rstd"], i + 1)
                for t in range(4):
                    m = V.tensor_scalar(z[:, t, :], x[:, ds(b * 4 + t, 1), :].rearrange("p t n -> p (t n)"), mv[:, t, 0:1],
                                        rstd[:, t:t + 1], ALU.subtract, ALU.mult)
                    if t % 2:
                        m.then_inc(q["z"], 1)
                if add is not None:
                    v.drain()
                    V.tensor_tensor(x[:, ds(b * 4, 4), :], x[:, ds(b * 4, 4), :], bcast(rows[:, ROWS.index(add), :], 1, 4), ALU.add)

            v.wait_ge(load["base"], 16 * (10 + len(ROWS)))
            v.wait_ge(su["tanh"], 1)
            for n in range(4):
                c = COL[f"k{n}"]
                V.tensor_scalar(cols[:, c:c + 2], cols[:, c:c + 2], 0.25 if n in (1, 2) else 1.0 / 16, None, ALU.mult)
            for n, t_ in (("s0", 4), ("o1", 1), ("f1", 5), ("o2", 2), ("o3", 3)):
                r = rows[:, ROWS.index(n), :]
                V.tensor_scalar(r, r, tg[:, t_:t_ + 1], None, ALU.mult)
            V.tensor_copy(bitf[:, :, :], bits[:, :, :])
            v.wait_ge(load["masks"], 64)
            v.wait_ge(su["tri"], 1)
            for a in range(3):
                src = mrow_i[0:1, a, :] if a != 1 else mrow_i[0:1, 1, 0:NB * SK // 4].bitcast(mybir.dt.uint8)
                V.tensor_scalar(mrow[0:1, a, :], src, 0.0, NEG, ALU.is_equal, ALU.mult)
            v.drain()
            V.tensor_tensor(mrow[0:1, 1, :], mrow[0:1, 1, :], fside_r[0:1, :], ALU.add)
            v.drain()
            for a in range(3):
                for part in range(3):
                    V.tensor_copy(mrow_b[0:1, :], mrow[0:1, a, :])
                    v.drain()
                    V.tensor_copy(brow[32 * part:32 * part + 1, a, :], mrow_b[0:1, :])
                    V.tensor_tensor(mrow[0:1, a, :], mrow[0:1, a, :], mrow_b[0:1, :], ALU.subtract)
                    v.drain()
            v.wait_ge(su["M_ps"], 1)
            V.tensor_scalar(Mf[:, :, :], psum[2][:, :].rearrange("p (k n) -> p k n", k=KC), tg[:, 5:6], 1.0 / D,
                            ALU.mult, ALU.mult)
            phase_end(v, 1)

            def one_head(L):
                q = one
                v.wait_ge(load["x"], 16 if L == 0 else 32)
                with v.Fori(0, NB // 2) as b:
                    i = b + BASE[L]
                    norm(q, i, b, "o3" if L == 3 else None)
                    for u in range(2):
                        v.wait_ge(q["V_ps" if L == 3 else "KT_sb"], (b if L == 3 else i) * 2 + u + 1)
                        if L == 0:
                            V.tensor_tensor(V1[0:SK, u, :], MISC[u][0:SK, 256:512], rows[0:SK, ROWS.index("v0"), :], ALU.add)\
                             .then_inc(q["V_sb"], 1)
                        else:
                            V.tensor_copy(V1[0:SK, u, :], MISC[u][0:SK, 256:512]).then_inc(q["V_sb"], 1)
                    for u in range(2):
                        v.wait_ge(q["s_ps"], i * 2 + u + 1)
                        V.tensor_reduce(mx[:, u, 0:TB], psum[u][:, 0:TB * SK].rearrange("p (t n) -> p t n", t=TB),
                                        AX.X, ALU.max, negate=True).then_inc(q["nmax"], 1)
                    for u in range(2):
                        v.wait_ge(q["p_sb"], i * 2 + u + 1)
                        V.reciprocal(rs[:, u, 0:TB], sm[:, u, 0:TB])
                        v.drain()
                        V.tensor_scalar(rs[:, u, 0:TB], rs[:, u, 0:TB], tg[:, L:L + 1], None, ALU.mult)
                        v.drain()
                        v.wait_ge(q["y_ps"], i * 2 + u + 1)
                        for t in range(TB):
                            xt = x[:, ds(b * 4 + 2 * u + t, 1), :].rearrange("p t n -> p (t n)")
                            V.scalar_tensor_tensor(xt, MISC[u][:, t * D:(t + 1) * D], rs[:, u, t:t + 1], xt,
                                                   ALU.mult, ALU.add).then_inc(q["x"], 1)
                    v.drain()

            one_head(0)
            phase_end(v, 2)

            def gate(L):
                q = gt
                with v.Fori(0, NB // 2) as b:
                    i = b + BASE[L]
                    norm(q, i, b)
                    for u in range(2):
                        v.wait_ge(q["l_ps"], i * 2 + u + 1)
                        V.tensor_copy(logit[:, ds(b * 4 + 2 * u, 2), :],
                                      psum[u][:, 0:TB * E].rearrange("p (t e) -> p t e", t=TB)).then_inc(q["l_sb"], 1)
                    v.wait_ge(q["stored"], i * 32 + 32)
                q = rt
                v.drain()
                V.tensor_reduce(gmax, logit, AX.X, ALU.max)
                v.drain()
                V.tensor_tensor(logit, logit, bcast(gmax, 2, E), ALU.subtract).then_inc(q["logit"], 1)
                v.wait_ge(q["prob_exp"], 1 + L // 3)
                V.tensor_reduce(sumT, prob, AX.X, ALU.add)
                v.drain()
                V.reciprocal(sumT, sumT)
                v.drain()
                V.tensor_tensor(prob, prob, bcast(sumT, 2, E), ALU.mult).then_inc(q["prob"], 1)

            gate(0)
            v.drain()
            V.memset(thr, 0)
            phase_end(v, 3)
            q = sh
            with v.Fori(0, T // 512) as i:
                V.tensor_tensor(x[:, ds(i * 4, 4), :], x[:, ds(i * 4, 4), :], bcast(rows[:, ROWS.index("s0"), :], 1, 4), ALU.add)
                for m_ in range(HALF):
                    b = i * HALF + m_
                    V.tensor_tensor(cand, thr, bits[:, ds(b, 1), :].rearrange("p t n -> p (t n)"), ALU.bitwise_or)
                    v.drain()
                    V.tensor_tensor(sel, prob, bcast(cand.bitcast(F32), 1, NT), ALU.is_ge).then_inc(q["cmp"], 1)
                    v.wait_ge(q["cnt_ps"], i * HALF + m_ + 1)
                    V.tensor_reduce(cnt, psum[6][:, 0:P].rearrange("p (t e) -> p e t", t=NT), AX.X, ALU.add)
                    v.drain()
                    V.scalar_tensor_tensor(flag, cnt, float(CAP), bitf[:, ds(b, 1), :].rearrange("p t n -> p (t n)"),
                                           ALU.is_ge, ALU.mult)
                    v.drain()
                    V.tensor_tensor(thr, thr, flag, ALU.bitwise_or)
                    v.drain()
                for t in range(2):
                    v.wait_ge(q["y_ps"], i * 2 + t + 1)
                    xt = x[:, ds(i * 4 + 2 * t, 2), :]
                    V.scalar_tensor_tensor(xt.rearrange("p t n -> p (t n)"), psum[4 + t][:, :], tg[:, 4:5],
                                           xt.rearrange("p t n -> p (t n)"), ALU.mult, ALU.add).then_inc(q["x"], 1)
            phase_end(v, 4)

            def route(L):
                n = 1 + L // 3
                q = rt
                w0 = work[:, 0, :].rearrange("p (t e) -> p t e", t=NT)
                w1 = work[:, 1, :].rearrange("p (t e) -> p t e", t=NT)
                w2 = work[:, 2, :].rearrange("p (t e) -> p t e", t=NT)
                if L == 0:
                    tf = bcast(thr.bitcast(F32), 1, NT)
                    V.tensor_tensor(sel, prob, tf, ALU.is_gt)
                    V.tensor_tensor(sel2, prob, tf, ALU.is_equal).then_inc(q["c_in"], 1)
                    v.wait_ge(q["c_ps"], 1)
                    V.tensor_reduce(cnt, psum[0][:, 0:P].rearrange("p (t e) -> p e t", t=NT), AX.X, ALU.add)
                    v.drain()
                    V.tensor_tensor(w0, psum[1][:, 0:P].rearrange("p (t e) -> p t e", t=NT), bcast(cnt, 1, NT), ALU.add)
                    v.drain()
                    V.tensor_scalar(w0, w0, float(CAP), None, ALU.is_le)
                    v.drain()
                    V.tensor_tensor(w0, w0, sel2, ALU.mult)
                    v.drain()
                    V.tensor_tensor(sel, w0, sel, ALU.add).then_inc(q["rank_in"], 1)
                else:
                    V.tensor_reduce(gmax, prob, AX.X, ALU.max)
                    v.drain()
                    V.tensor_tensor(w0, prob, bcast(gmax, 2, E), ALU.is_equal)
                    v.drain()
                    V.tensor_tensor(w0, w0, bcast(m8, 1, NT), ALU.mult)
                    v.drain()
                    V.tensor_reduce(sumT, w0, AX.X, ALU.max)
                    v.drain()
                    V.tensor_tensor(sel, w0, bcast(sumT, 2, E), ALU.is_equal).then_inc(q["rank_in"], 1)
                v.wait_ge(q["rank_ps"], n)
                V.tensor_copy(w1, psum[2][:, 0:P].rearrange("p (t e) -> p t e", t=NT))
                v.drain()
                V.scalar_tensor_tensor(work[:, 0, :], work[:, 1, :], float(CAP), sel.rearrange("p t e -> p (t e)"),
                                       ALU.is_le, ALU.mult)
                v.drain()
                V.tensor_tensor(work[:, 1, :], work[:, 1, :], work[:, 0, :], ALU.mult)
                v.drain()
                if L == 3:
                    V.tensor_scalar(w2, bcast(m8, 1, NT), -float(CAP), float(CAP * E - 1), ALU.mult, ALU.add)
                    v.drain()
                    V.tensor_tensor(w2, w2, w0, ALU.mult)
                    v.drain()
                    V.tensor_tensor(w2, w2, w1, ALU.add)
                    v.drain()
                    V.tensor_reduce(slotf, w2, AX.X, ALU.add)
                    V.tensor_reduce(wtok, w0, AX.X, ALU.add)
                    v.drain()
                    V.tensor_copy(slot_i, slotf)
                    V.tensor_tensor(wtok, wtok, gmax, ALU.mult)
                    v.drain()
                    V.tensor_scalar(wtok, wtok, tg[:, 7:8], None, ALU.mult)
                V.tensor_scalar(work[:, 1, :], work[:, 1, :], -1.0, None, ALU.add)
                v.drain()
                V.tensor_copy(posi[:, 0, :], work[:, 1, :])
                v.drain()
                V.tensor_scalar(posi[:, 1, :], posi[:, 0, :], 4, None, ALU.arith_shift_right)
                V.tensor_scalar(posi[:, 2, :], posi[:, 0, :], 15, None, ALU.bitwise_and)
                v.drain()
                V.tensor_copy(work[:, 0, :], posi[:, 1, :])
                V.tensor_copy(work[:, 1, :], posi[:, 2, :])
                v.drain()
                for t in range(NT):
                    V.tensor_tensor(hi1[:, t], bcast(work[:, 0, t * E:(t + 1) * E], 2, 16), bcast(iota16[:, :], 1, E), ALU.is_equal)
                    V.tensor_tensor(lo1[:, t], bcast(work[:, 1, t * E:(t + 1) * E], 2, 16), bcast(iota16[:, :], 1, E), ALU.is_equal)
                v.drain()
                v.wait_ge(gt["stored"], 16 * (NT // 2) * n)
                for t in range(NT):
                    l = lo1[:, t].rearrange("p e a -> p (e a)")
                    V.tensor_scalar(lo2[:, t, 0, :], l, float(t), None, ALU.mult)
                    m = V.tensor_scalar(lo2[:, t, 1, :], l, pcol, None, ALU.mult)
                m.then_inc(q["hot"], 1)
                v.wait_ge(q["idx_ps"], n)
                V.tensor_scalar(work[:, 0, :], psum[3][:, 0:P], float(P), None, ALU.mult)
                v.drain()
                V.tensor_tensor(work[:, 0, :], work[:, 0, :], psum[3][:, P:2 * P], ALU.add)
                v.drain()
                V.tensor_tensor(work[:, 0, :].rearrange("p (e b) -> p e b", e=E), work[:, 0, :].rearrange("p (e b) -> p e b", e=E),
                                blk, ALU.mult)
                v.drain()
                V.tensor_reduce(work[:, 1, 0:16], work[:, 0, :].rearrange("p (e b) -> p b e", e=E), AX.X, ALU.add)\
                 .then_inc(q["idxf"], 1)
                v.wait_ge(q["sT_ps"], n)
                V.tensor_copy(idx, psum[4][:, 0:16]).then_inc(q["idx"], 1)

            route(0)
            v.wait_ge(load["b2row"], 16)
            phase_end(v, 5)

            def experts(L):
                q = ex
                with v.Fori(0, E // 2) as b:
                    i = b + BASE[L]
                    for u in range(2):
                        v.wait_ge(q["y_ps"], i * 2 + u + 1)
                        if L == 0:
                            v.wait_ge(q[f"gather{u}"], i * 32 + 32)
                            V.tensor_scalar(wsl[:, u, :], G[:, u, :, ds(D + b * 2 + u, 1)].rearrange("p t n -> p (t n)"),
                                            tg[:, 4:5], None, ALU.mult)
                            V.tensor_tensor(eout[:, u], psum[4 + u][:, :].rearrange("p (t n) -> p t n", t=TB),
                                            bcast(b2row[:, ds(b * 2 + u, 1), :].rearrange("p t n -> p (t n)"), 1, TB), ALU.add)
                            v.drain()
                            for t in range(TB):
                                m = V.tensor_scalar(eout[:, u, t, :], eout[:, u, t, :], wsl[:, u, t:t + 1], None, ALU.mult)
                        else:
                            m = V.tensor_copy(eout[:, u], psum[4 + u][:, :].rearrange("p (t n) -> p t n", t=TB))
                        m.then_inc(q["y_sb"], 1)
                    for u in range(2):
                        v.wait_ge(q[f"o{u}"], i * 32 + 32) if L == 0 else v.wait_ge(q[f"e{u}"], b * 16 + 16)

            v.wait_ge(load["ternary"], 32)
            for a in range(2):
                V.tensor_reduce(gam[:, a:a + 1], ffw[:, a, :], AX.X, ALU.add, apply_absolute_value=True)
            v.drain().then_inc(su["gsum_in"], 1)
            v.wait_ge(su["gsum_ps"], 1)
            V.tensor_scalar(gam[:, 4:6], psum[5][:, 0:2], 0.5 / (HID * D), 0.5e-6, ALU.mult, ALU.add)
            v.drain()
            V.tensor_scalar(gam[:, 2:4], gam[:, 4:6], -1.0, None, ALU.mult)
            v.drain().then_inc(su["gsum_out"], 1)
            for a in range(2):
                V.tensor_scalar(below, ffw[:, a, :], gam[:, 2 + a:3 + a], None, ALU.is_lt)
                v.drain()
                V.scalar_tensor_tensor(sign, ffw[:, a, :], gam[:, 4 + a:5 + a], below, ALU.is_gt, ALU.subtract)
                v.drain()
                V.tensor_copy(tern[a], sign)
                v.drain()
            experts(0)
            phase_end(v, 6)

            def multi_head(L):
                q = multi
                v.wait_ge(load["x"], 32)
                V.memset(Vp, 0.0)
                v.drain()
                with v.Fori(0, NB // 2) as b:
                    i = b + BASE[L]
                    norm(q, i, b, f"o{L}")
                    for u in range(2):
                        v.wait_ge(q["KT_sb"], i * 2 + u + 1)
                        for j in range(2):
                            o = Vp[0:SK, u].rearrange("p (a b) (c n) -> p a b c n", b=2, c=2)[:, :, j, j, :]
                            s = MISC[u][0:SK, 256:512].rearrange("p (a b n) -> p a b n", b=2, n=HD)[:, :, j, :]
                            r = rows[0:SK, ROWS.index(f"v{L}"), :].rearrange("p (a b n) -> p a b n", b=2, n=HD)[:, :, j, :]
                            m = V.tensor_tensor(o, s, r, ALU.add)
                        m.then_inc(q["V_sb"], 1)

                    def shift(n):
                        v.wait_ge(q["s_ps"], i * 8 + n + 1)
                        if n >= 4:
                            v.wait_ge(q["pT_ps"], i * 16 + 2 * n - 6)
                        for j in range(2):
                            V.tensor_reduce(mx[:, n % 4, 4 * j:4 * j + 4],
                                            psum[2 * (n % 2) + j][:, 0:4 * SK].rearrange("p (h n) -> p h n", h=4), AX.X, ALU.max)
                        v.drain()
                        for j in range(2):
                            m = V.tensor_tensor(Pr[:, n % 4, 4 * j:4 * j + 4, :],
                                                psum[2 * (n % 2) + j][:, 0:4 * SK].rearrange("p (h n) -> p h n", h=4),
                                                bcast(mx[:, n % 4, 4 * j:4 * j + 4], 2, SK), ALU.subtract)
                        m.then_inc(q["sub"], 1)

                    def sums(n):
                        v.wait_ge(q["p_exp"], i * 8 + n + 1)
                        V.tensor_reduce(sm[:, n % 4], Pr[:, n % 4], AX.X, ALU.add)
                        v.drain()
                        V.reciprocal(rs[:, n % 4], sm[:, n % 4]).then_inc(q["rsum"], 1)

                    for n in range(9):
                        if n < 8:
                            shift(n)
                        if n >= 1:
                            sums(n - 1)
                    for u in range(2):
                        v.wait_ge(q["y_ps"], i * 2 + u + 1)
                        xt = x[:, ds(b * 4 + 2 * u, 2), :].rearrange("p t n -> p (t n)")
                        V.scalar_tensor_tensor(xt, MISC[u][:, :], tg[:, L:L + 1], xt, ALU.mult, ALU.add).then_inc(q["x"], 1)
                    v.drain()

            v.wait_ge(load["x"], 32)
            multi_head(1)
            phase_end(v, 7)
            q = f1
            with v.Fori(0, NB // 2) as i:
                norm(q, i, i, "f1")
                v.drain()
                for u in range(2):
                    v.wait_ge(q["y_ps"], i * 2 + u + 1)
                    xt = x[:, ds(i * 4 + 2 * u, 2), :].rearrange("p t n -> p (t n)")
                    V.tensor_tensor(xt, psum[u][:, :], xt, ALU.add).then_inc(q["x"], 1)
                v.drain()
            phase_end(v, 8)
            multi_head(2)
            phase_end(v, 9)

            q = f2

            def step(r, n):
                t = r * 4 + n
                if in_range(t):
                    v.wait_ge(q["h_sb"], t + 1)
                    for j in range(2):
                        V.bn_stats(st[:, j, :], h2[:, n, j * 512:(j + 1) * 512])
                    v.drain()
                    V.bn_aggr(mx[:, n, 0:2], st[:, 0:2, :])
                    v.drain()
                    V.tensor_scalar(sm[:, n, 0:1], mx[:, n, 1:2], EPS, None, ALU.add).then_inc(q["st2"], 1)
                if in_range(t):
                    v.wait_ge(q["rstd2"], t + 1)
                    V.tensor_scalar(h2[:, n, :], h2[:, n, :], mx[:, n, 0:1], rs[:, n, 0:1], ALU.subtract, ALU.mult)\
                     .then_inc(q["n2"], 1)
                if n == 0 and in_range(r * 4 + 4):
                    v.wait_ge(q["zT_ps"], r * 2 + 2)
                    norm(q, r + 1, r + 1)
                if in_range(t - 2):
                    v.wait_ge(q["nT_sb"], t - 1)
                    if in_range(t - 4):
                        v.wait_ge(q["y_ps"], t - 3)
                    V.tensor_copy(h2s[:, 0, n % 2], h2T[:, n % 2]).then_inc(q["nTh"], 1)
                if n >= 2 and in_range(r * 4 + 4):
                    low_z(r + 1, n - 2)
                if in_range(t - 4):
                    v.wait_ge(q["y_ps"], t - 3)
                    xt = x[:, ds(t - 4, 1), :].rearrange("p t n -> p (t n)")
                    V.scalar_tensor_tensor(xt, psum[7][:, 0:D], tg[:, 6:7], xt, ALU.mult, ALU.add).then_inc(q["x"], 1)

            def low_z(r, u):
                v.wait_ge(q["zT_sb"], r * 2 + u + 1)
                V.tensor_tensor(zTs[:, 1, u], zT[:, u], zTs[:, 0, u], ALU.subtract).then_inc(q["zTs"], 1)

            norm(q, 0, 0)
            for u in range(2):
                low_z(0, u)
            for n in range(4):
                step(0, n)
            with v.Fori(1, NT // 4 - 1) as r:
                for n in range(4):
                    step(r, n)
            for t in range(NT - 4, NT + 4):
                step(t // 4, t % 4)
            phase_end(v, 10)
            one_head(3)
            phase_end(v, 11)
            gate(3)
            phase_end(v, 12)
            route(3)
            phase_end(v, 13)
            experts(3)
            phase_end(v, 14)
            with v.Fori(0, NT // 4) as i:
                for u in range(2):
                    v.wait_ge(fin[f"g{u}"], i * 32 + 32)
                    for t in range(TB):
                        xt = x[:, ds(i * 4 + 2 * u + t, 1), :].rearrange("p t n -> p (t n)")
                        m = V.scalar_tensor_tensor(xt, eout[:, u, t, :],
                                                   wtok[:, ds(i * 4 + 2 * u + t, 1)], xt, ALU.mult, ALU.add)
                    m.then_inc(fin["x"], 1)
            phase_end(v, 15)


def _layout(a):
    import numpy as np
    i = {k: np.asarray(v_) for k, v_ in a.items()}

    def kp(w):
        k, n = w.shape
        return np.ascontiguousarray(w.reshape(k // P, P, n).transpose(1, 0, 2))

    def flat(w):
        return kp(w).reshape(P, -1)

    d = {"x": i["x"].reshape(NT, P, D).transpose(1, 0, 2), "ctxT": kp(i["ctx_1024"].reshape(NB * SK, D).T)}
    ww = {"q0": i["L0_xattn_Wq"], "k0": i["L0_xattn_Wk"], "v0": i["L0_xattn_Wv"],
          "q1": i["L1_xattn_Wq_w"].T, "k1": i["L1_xattn_Wkv_w"][:D].T, "v1": i["L1_xattn_Wkv_w"][D:].T,
          "o1": i["L1_xattn_out_w"].T,
          "q2": i["L2_xattn_Wq"], "k2": i["L2_xattn_Wk"], "v2": i["L2_xattn_Wv"], "o2": i["L2_xattn_Wo"],
          "q3": i["L3_xattn_Wq"].T, "k3": i["L3_xattn_Wk"].T, "v3": i["L3_xattn_Wv"].T, "o3": i["L3_xattn_Wo"].T}
    for n, w in ww.items():
        d["W" + n] = kp(w)
    zero = np.zeros(D, np.float32)
    cb = {"q0": i["L0_xattn_bq"], "k0": i["L0_xattn_bk"], "q1": i["L1_xattn_Wq_b"], "k1": i["L1_xattn_Wkv_b"][:D],
          "q2": i["L2_xattn_bq"], "k2": i["L2_xattn_bk"], "q3": i["L3_xattn_bq"], "k3": zero, "v3": i["L3_xattn_bv"]}
    d["cols"] = np.concatenate([cb[n].reshape(2, P).T for n in COL], 1)
    rb = {"v0": i["L0_xattn_bv"], "s0": i["L0_ffn_bs2"], "v1": i["L1_xattn_Wkv_b"][D:], "o1": i["L1_xattn_out_b"],
          "f1": i["L1_ffn_bias"], "v2": i["L2_xattn_bv"], "o2": i["L2_xattn_bo"], "o3": i["L3_xattn_bo"]}
    d["rows"] = np.stack([rb[n] for n in ROWS])
    d["g"] = np.concatenate([i["g_xattn"], i["g_ffn"]])
    d["gates"] = np.stack([kp(i["L0_ffn_gate"]), kp(i["L3_ffn_wg"])], 1)
    d["b1T"] = np.concatenate([i["L0_ffn_b1"].reshape(E * MC, P).T, i["L0_ffn_bs1"].reshape(MC, P).T], 1)
    d["lnwb"] = np.stack([i["L2_ffn_ln_w"].reshape(MC, P).T, i["L2_ffn_ln_b"].reshape(MC, P).T], 1)
    d["m0"] = i["mask_BxS2_ik1"].reshape(1, -1)
    d["m1"] = i["mask_BxS2_bk0"].reshape(1, -1)
    d["m2"] = i["mask_BxS2_ik0"].reshape(1, -1)
    d["fside"] = i["fside_BxS2_0"].reshape(1, -1)
    d["shared0"], d["shared1"] = flat(i["L0_ffn_Ws1"]), flat(i["L0_ffn_Ws2"])
    d["tern0"], d["tern1"] = flat(i["L2_ffn_W_fc"].T), flat(i["L2_ffn_W_proj"].T)
    d["b2"] = i["L0_ffn_b2"]
    for L, a, b in ((0, "L0_ffn_W1", "L0_ffn_W2"), (3, "L3_ffn_w1", "L3_ffn_w2")):
        d[f"w0_{L}"] = i[a].reshape(E, KC, P, HID).transpose(0, 2, 1, 3).reshape(E, P, -1)
        d[f"w1_{L}"] = i[b].reshape(E, MC, P, D).transpose(0, 2, 1, 3).reshape(E, P, -1)
    d["wr"], d["wi"] = kp(i["L1_ffn_w_freq_real"]), kp(i["L1_ffn_w_freq_imag"])
    n = np.arange(D)
    ang = 2 * np.pi * ((n[:, None] * n[None, :]) % D) / D
    d["cosm"], d["sinm"], d["nsinm"] = (kp(t.astype(np.float32)) for t in (np.cos(ang), np.sin(ang), -np.sin(ang)))
    d["ident"] = np.eye(P, dtype=np.float32)
    p = np.arange(P)
    d["headmask"] = (p[:, None] // HD == np.arange(HC)[None]).astype(np.float32)
    d["iota16"] = np.tile(np.arange(16, dtype=np.float32), (P, 1))
    d["bits"] = np.ascontiguousarray(np.broadcast_to(
        np.array([0] + [1 << b for b in range(BITS - 2, -1, -1)], np.int32)[None, :, None], (P, BITS, E)))
    d["tokt"] = np.concatenate([
        np.tile(np.arange(NT, dtype=np.float32), (P, 1)), p[:, None].astype(np.float32), np.zeros((P, 1), np.float32),
        np.tile(E - np.arange(E, dtype=np.float32), (P, 1)),
        (p[:, None] // 16 == np.repeat(np.arange(E), 16)[None]).astype(np.float32)], 1)
    return {k: np.ascontiguousarray(v_) for k, v_ in d.items()}


def kernel(**inputs):
    import numpy as np
    import concourse.bacc as bacc
    from concourse.bass_utils import run_bass_kernel_spmd as run

    arrays = _layout(inputs)
    nc = bacc.Bacc("TRN2", target_bir_lowering=False, num_devices=1)
    d = {k: nc.dram_tensor(f"in_{k}", a.shape, mybir.dt.from_np(a.dtype), kind="ExternalInput").ap()
         for k, a in arrays.items()}
    out = nc.dram_tensor("out_0", (P, NT, D), F32, kind="ExternalOutput").ap()
    flamingo_kernel(nc, d, out)
    r = run(nc, [{f"in_{k}": a for k, a in arrays.items()}], core_ids=[0])
    got = r.results[0]["out_0"]
    return np.ascontiguousarray(got.transpose(1, 0, 2).reshape(NB, SQ, D))
```

```python
from contextlib import ExitStack

import concourse.bass as bass
from concourse import mybir

ALU = mybir.AluOpType
ACT = mybir.ActivationFunctionType
F32 = mybir.dt.float32
BF16 = mybir.dt.bfloat16
F16 = mybir.dt.float16
I32 = mybir.dt.int32
AX = mybir.AxisListType

P = 128
D = 256
KC = D // P
NB, SQ, SK = 8, 256, 120
T = NB * SQ
NT = T // P
TB = SQ // P
NH, HD = 16, 16
HC = P // HD
HID = 1024
MC = HID // P
E = 8
CAP = T // E
ROW = D + E
EPS = 1e-5
NEG = -1e30
BITS = 32
HALF = BITS // (T // 512)

COL = {n: 2 * i for i, n in enumerate(["q0", "k0", "q1", "k1", "q2", "k2", "q3", "k3", "v3"])}
ROWS = ["v0", "s0", "v1", "o1", "f1", "v2", "o2", "o3"]
WEIGHTS = ["q0", "k0", "v0", "q1", "k1", "v1", "o1", "q2", "k2", "v2", "o2", "q3", "k3", "v3", "o3"]


def bcast(ap, axis, n):
    ap = ap.unsqueeze(axis)
    shape = list(ap.shape)
    shape[axis] = n
    return ap.to_broadcast(shape)


def flamingo_kernel(nc, d, out):
    ctx = ExitStack()
    with ctx:
        def sb(name, shape, dt):
            return ctx.enter_context(nc.sbuf_tensor(name, shape, dt))

        def sems(phase, names):
            return {n: ctx.enter_context(nc.semaphore(f"{phase}_{n}")) for n in names.split()}

        x = sb("x", [P, NT, D], F32)
        ctxT = sb("ctxT", [P, KC, NB * SK], F32)
        W = {n: sb(f"W{n}", [P, KC, D], F32) for n in WEIGHTS if n not in ("q3", "k3", "v3")}
        W |= {f"{n}3": W[f"{n}0"] for n in "qkv"}
        Mf = sb("Mf", [P, KC, D], F32)
        ident = sb("ident", [P, P], F32)
        tri = sb("tri", [P, P], BF16)
        ones = sb("ones", [P, P], BF16)
        headmask = sb("headmask", [P, HC], F32)
        cols = sb("cols", [P, 2 * len(COL)], F32)
        rows = sb("rows", [P, len(ROWS), D], F32)
        tg = sb("tg", [P, 8], F32)
        gates = sb("gates", [P, 2, KC, E], F32)
        brow = sb("brow", [96, 3, NB * SK], BF16)
        mhalf = sb("mhalf", [P, 4], F32)
        ffw = sb("ffw", [P, 2, 2048], F32)
        ew = sb("ew", [P, 2, 2, 2048], F32)
        small = sb("small", [P, 1024], F32)
        arena = sb("arena", [P, 22016], F32)

        class Cut:

            def __init__(self, buf):
                self.buf, self.at = buf, 0

            def take(self, n, pat=None, dt=F32, **kw):
                words = n if dt not in (BF16, F16) else (n + 1) // 2
                v = self.buf[:, self.at:self.at + words]
                self.at += words
                assert self.at <= self.buf.shape[1], self.at
                if dt != F32:
                    v = v.bitcast(dt)
                return v if pat is None else v.rearrange(pat, **kw)

        psum = [ctx.enter_context(nc.psum_tensor(f"bank{i}", [P, 512], F32)) for i in range(8)]
        MISC = psum[6:8]

        zrow = nc.dram_tensor("zrow", (T, ROW), F32, kind="Internal").ap()
        zrow3 = nc.dram_tensor("zrow3", (T, D), F32, kind="Internal").ap()
        acc = nc.dram_tensor("acc", (T, D), F32, kind="Internal").ap()
        eo = nc.dram_tensor("eo", (T, D), F32, kind="Internal").ap()
        slotd = [nc.dram_tensor(f"slotd{i}", (P, 16), F32, kind="Internal").ap() for i in range(2)]

        c = Cut(arena)
        z = c.take(4 * D, "p (t n) -> p t n", t=4)
        zT = c.take(2 * KC * SQ, "p (u k n) -> p u k n", u=2, k=KC)
        qT = c.take(2 * KC * SQ, "p (u k n) -> p u k n", u=2, k=KC)
        OT = c.take(2 * KC * SQ, "p (u k n) -> p u k n", u=2, k=KC)
        KT = c.take(2 * KC * SK, "p (u k n) -> p u k n", u=2, k=KC)
        cT = c.take(2 * KC * SK, "p (u k n) -> p u k n", u=2, k=KC)
        Vp = c.take(2 * NH * 32, "p (u h n) -> p u h n", u=2, h=NH)
        after_common = c.at
        KBD = c.take(2 * KC * HC * SK, "p (u k h n) -> p u k h n", u=2, k=KC, h=HC)
        Pr = c.take(4 * HC * SK, "p (b h n) -> p b h n", b=4, h=HC)
        PT = c.take(2 * NH * SQ, "p (u h n) -> p u h n", u=2, h=NH)
        c.at = after_common
        V1 = c.take(2 * D, "p (u n) -> p u n", u=2)
        P1 = c.take(2 * TB * SK, "p (u t n) -> p u t n", u=2, t=TB)
        PT1 = c.take(2 * SQ, "p (u n) -> p u n", u=2)
        VT1 = c.take(2 * KC * SK, "p (u k n) -> p u k n", u=2, k=KC)
        c.at = after_common
        zT_all = c.take(KC * T, "p (k n) -> p k n", k=KC)
        hT = c.take(MC * 512, "p (m n) -> p m n", m=MC)
        c.at = 0
        b2row = c.take(E * D, "p (e n) -> p e n", e=E)
        G = c.take(2 * TB * ROW, "p (u t n) -> p u t n", u=2, t=TB)
        assert c.at <= after_common
        c.at = after_common
        xeT = c.take(2 * KC * CAP, "p (u k n) -> p u k n", u=2, k=KC)
        heT = c.take(2 * MC * CAP, "p (u m n) -> p u m n", u=2, m=MC)
        eout = c.take(2 * TB * D, "p (u t n) -> p u t n", u=2, t=TB)
        c.at = 18432
        hi1 = c.take(NT * P, "p (t e a) -> p t e a", dt=BF16, t=NT, e=E)
        lo1 = c.take(NT * P, "p (t e a) -> p t e a", dt=BF16, t=NT, e=E)
        c.at = 0
        lo2 = c.take(NT * 2 * P, "p (t w n) -> p t w n", dt=BF16, t=NT, w=2)
        c.at = 15360
        bits = c.take(BITS * E, "p (b e) -> p b e", dt=I32, b=BITS)
        bitf = c.take(BITS * E, "p (b e) -> p b e", b=BITS)
        work = c.take(3 * P, "p (a n) -> p a n", a=3)
        posi = c.take(3 * P, "p (a n) -> p a n", dt=I32, a=3)
        c.at = after_common
        h2 = c.take(4 * HID, "p (u n) -> p u n", u=4)
        h2T = c.take(2 * HID, "p (u m n) -> p u m n", u=2, m=MC)
        h2s = c.take(2 * 2 * HID, "p (a u m n) -> p a u m n", dt=F16, a=2, u=2, m=MC)
        zTs = c.take(2 * 2 * KC * SQ, "p (a u k n) -> p a u k n", dt=F16, a=2, u=2, k=KC)
        sign = c.take(HID * KC, dt=BF16)
        below = c.take(HID * KC, dt=BF16)
        tern = [ffw[:, a, 0:HID * KC // 2].bitcast(BF16) for a in range(2)]
        c.at = 0
        dft = c.take(5 * KC * D, "p (a k n) -> p a k n", a=5, k=KC)
        ABT = c.take(2 * KC * D, "p (a k n) -> p a k n", a=2, k=KC)
        mrow = c.take(3 * NB * SK, "p (a n) -> p a n", a=3)
        mrow_i = c.take(3 * NB * SK, "p (a n) -> p a n", a=3, dt=I32)
        mrow_r = c.take(NB * SK)
        mrow_b = c.take(NB * SK, dt=BF16)
        fside_r = c.take(NB * SK)

        c = Cut(small)
        st = c.take(24, "p (t n) -> p t n", t=4)
        mv = c.take(8, "p (t n) -> p t n", t=4)
        ve = c.take(4)
        rstd = c.take(4)
        mx = c.take(4 * HC, "p (b h) -> p b h", b=4)
        sm = c.take(4 * HC, "p (b h) -> p b h", b=4)
        rs = c.take(4 * HC, "p (b h) -> p b h", b=4)
        logit = c.take(NT * E, "p (t e) -> p t e", t=NT)
        prob = c.take(NT * E, "p (t e) -> p t e", t=NT)
        pos = c.take(NT * E, "p (t e) -> p t e", t=NT)
        thr = c.take(E, dt=I32)
        cand = c.take(E, dt=I32)
        flag = c.take(E, dt=I32)
        cnt = c.take(E)
        sumT = c.take(NT)
        gmax = c.take(NT)
        sel = c.take(NT * E, "p (t e) -> p t e", dt=BF16, t=NT)
        sel2 = c.take(NT * E, "p (t e) -> p t e", dt=BF16, t=NT)
        idx = c.take(16, dt=I32)
        slot16 = c.take(16)
        wtok = c.take(NT)
        slotf = c.take(NT)
        slot_i = c.take(NT, dt=I32)
        b1u = c.take(2 * MC, "p (u m) -> p u m", u=2)
        wsl = c.take(4, "p (u j) -> p u j", u=2)
        gam = c.take(8)
        b1T = sb("b1T", [P, (E + 1) * MC], F32)
        lnwb = sb("lnwb", [P, 2, MC], F32)
        onesf = sb("onesf", [P, P], F32)
        iota16 = sb("iota16", [P, 16], F32)
        tokt = sb("tokt", [P, NT + 2 + E + P], F32)
        tcol, pcol, m8 = tokt[:, 0:NT], tokt[:, NT:NT + 1], tokt[:, NT + 2:NT + 2 + E]
        blk = tokt[:, NT + 2 + E:].rearrange("p (e a) -> p e a", e=E)

        load = sems("load", "x x0 ctx wone base weights dft masks shared ternary b2row")
        s_phase = ctx.enter_context(nc.semaphore("phase_done"))
        s_store = ctx.enter_context(nc.semaphore("stored"))

        def in_range(t, n=NT):
            return not isinstance(t, int) or 0 <= t < n

        UNITS = 4 * NB

        def unit_steps(eng, step):
            for n in range(8):
                step(0, n)
            with eng.Fori(1, NB // 2 - 1) as r:
                for n in range(8):
                    step(r, n)
            for n in range(8 + 7):
                step(NB // 2 - 1 + n // 8, n % 8)

        def batch_of(r, n):
            return r * 8 + n, r * 2 + n // 4, n % 4, n // 4

        def rounds_of(eng, L, front, back):
            front(BASE[L], 0)
            with eng.Fori(0, R - 1) as b:
                back(b + BASE[L], b, True)
            back(R - 1 + BASE[L], R - 1, False)

        def phase_end(eng, n):
            eng.drain().then_inc(s_phase, 1)
            eng.wait_ge(s_phase, 5 * n)

        ln_names = "var rstd z zT_ps zT_sb"
        kv_names = "cT K_ps V_ps KT_sb V_sb"
        su = sems("setup", "AB_ps AB_sb M_ps tanh gsum_in gsum_ps gsum_out tri")
        R = NB // 2
        BASE = {0: 0, 1: 0, 2: R, 3: R}
        one = sems("one", f"{ln_names} {kv_names} q_ps q_sb s_ps nmax p_sb pT_ps pT_sb y_ps x VT_sb")
        multi = sems("multi", f"{ln_names} {kv_names} q_ps q_sb kbd s_ps sub p_exp rsum p_norm pT_ps pT_sb "
                              "O_ps O_sb y_ps x")
        gt = sems("gate", f"{ln_names} zT_all l_ps l_sb stored")
        f1 = sems("ffn1", f"{ln_names} y_ps x")
        f2 = sems("ffn2", f"{ln_names} zTs h_ps h_sb st2 rstd2 n2 nT_ps nT_sb nTh nTs y_ps x")
        sh = sems("shared", "cmp cnt_ps h_ps h_sb y_ps x")
        rt = sems("route", "logit prob_exp prob probs_out rank_in rank_ps hot idx_ps idxf slot_out slot_in sT_ps idx c_ps c_in")
        ex = sems("experts", "w0 w1 gather0 gather1 idx b1 xT_ps xT_sb h_ps h_sb y_ps y_sb o0 o1 e0 e1 acc")
        fin = sems("final", "g0 g1 x")

        block = ctx.enter_context(nc.Block())
        ds = bass.ds
        N_ONE = {0: 2, 3: 9}

        @block.sync
        def _(sp):
            sp.dma_start(cols[:, :], d["cols"]).then_inc(load["base"], 16)
            sp.dma_start(ident[:, :], d["ident"]).then_inc(load["base"], 16)
            sp.dma_start(tokt[:, :], d["tokt"]).then_inc(load["base"], 16)
            sp.dma_start(headmask[:, :], d["headmask"]).then_inc(load["base"], 16)
            sp.dma_start(iota16[:, :], d["iota16"]).then_inc(load["base"], 16)
            sp.dma_start(tg[:, :], d["g"].partition_broadcast(P)).then_inc(load["base"], 16)
            sp.dma_start(bits[:, :, :], d["bits"]).then_inc(load["base"], 16)
            sp.dma_start(gates[:, :, :, :], d["gates"]).then_inc(load["base"], 16)
            sp.dma_start(b1T[:, :], d["b1T"]).then_inc(load["base"], 16)
            sp.dma_start(lnwb[:, :, :], d["lnwb"]).then_inc(load["base"], 16)
            for r, n in enumerate(ROWS):
                sp.dma_start(rows[:, r, :], d["rows"][r].partition_broadcast(P)).then_inc(load["base"], 16)
            sp.dma_start(mrow_i[0:1, 0, :], d["m0"]).then_inc(load["masks"], 16)
            sp.dma_start(mrow_i[0:1, 2, :], d["m2"]).then_inc(load["masks"], 16)
            sp.dma_start(mrow_i[0:1, 1, 0:NB * SK // 4].bitcast(mybir.dt.uint8), d["m1"]).then_inc(load["masks"], 16)
            sp.dma_start(fside_r[0:1, :], d["fside"]).then_inc(load["masks"], 16)
            for a, n in enumerate(["cosm", "sinm", "nsinm", "wr", "wi"]):
                sp.dma_start(dft[:, a, :, :], d[n]).then_inc(load["dft"], 16)
            for t in (0, 4):
                w = 4 if t == 0 else NT - 4
                sp.dma_start(x[:, t:t + w, :], d["x"][:, t:t + w, :]).then_inc(load["x0" if t == 0 else "x"], 16)
            sp.dma_start(ctxT[:, :, :], d["ctxT"]).then_inc(load["ctx"], 16)
            for n in WEIGHTS[:-4] + ["o3"]:
                sp.dma_start(W[n][:, :, :], d["W" + n]).then_inc(load["wone" if n in ("q0", "k0", "v0") else "weights"], 16)
            for a in range(2):
                sp.dma_start(ffw[:, a, :], d[f"shared{a}"]).then_inc(load["shared"], 16)

            eo_v = eo.rearrange("(e t p) n -> p e t n", p=P, t=TB)

            def first_experts(L):
                for u in range(2):
                    for a in range(2):
                        sp.dma_start(ew[:, u, a, :], d[f"w{a}_{L}"][u]).then_inc(ex[f"w{u}"], 16)

            def experts(L):
                def weights(i, b, u):
                    sp.wait_ge(ex["y_ps"], i * 2 + u + 1)
                    for a in range(2):
                        sp.dma_start(ew[:, u, a, :],
                                     d[f"w{a}_{L}"][ds(b * 2 + u + 2, 1), :, :].rearrange("e p n -> p (e n)"))\
                          .then_inc(ex[f"w{u}"], 16)

                def store(i, b, u):
                    sp.wait_ge(ex["y_sb"], i * 2 + u + 1)
                    sp.dma_start(eo_v[:, ds(b * 2 + u, 1), :, :].rearrange("p e t n -> p (e t) n"), eout[:, u, :, :])\
                      .then_inc(ex[f"e{u}"], 16)

                with sp.Fori(0, E // 2 - 1) as b:
                    for u in range(2):
                        weights(b + BASE[L], b, u)
                        if L == 3:
                            store(b + BASE[L], b, u)
                if L == 3:
                    for u in range(2):
                        store(BASE[L] + E // 2 - 1, E // 2 - 1, u)

            first_experts(0)
            phase_end(sp, 1)
            phase_end(sp, 2)
            for n in ("q3", "k3", "v3"):
                sp.dma_start(W[n][:, :, :], d["W" + n]).then_inc(load["wone"], 16)
            zr = zrow.rearrange("(t p) n -> p t n", p=P)
            q = gt
            with sp.Fori(0, R) as i:
                for u in range(2):
                    sp.wait_ge(q["z"], i * 2 + u + 1)
                    sp.dma_start(zr[:, ds(i * 4 + 2 * u, 2), 0:D], z[:, 2 * u:2 * u + 2, :]).then_inc(q["stored"], 16)
            phase_end(sp, 3)
            q = rt
            sp.wait_ge(q["prob"], 1)
            sp.dma_start(zr[:, :, D:ROW], prob).then_inc(q["probs_out"], 16)
            phase_end(sp, 4)

            def route(L, q):
                n = 1 + L // 3
                sp.wait_ge(q["idxf"], n)
                sp.dma_start(slotd[L // 3], work[:, 1, 0:16]).then_inc(q["slot_out"], 16)
                sp.wait_ge(q["slot_out"], 16 * n)
                sp.dma_start(work[0:16, 2, :], slotd[L // 3].rearrange("(j a) b -> j (a b)", j=16)).then_inc(q["slot_in"], 16)

            for a in range(2):
                sp.dma_start(ffw[:, a, :], d[f"tern{a}"]).then_inc(load["ternary"], 16)
            sp.dma_start(acc.rearrange("(t p) n -> p t n", p=P), x[:, :, :]).then_inc(ex["acc"], 16)
            route(0, q)
            sp.wait_ge(q["idx"], 1)
            sp.dma_start(b2row[:, :, :], d["b2"].partition_broadcast(P)).then_inc(load["b2row"], 16)
            phase_end(sp, 5)
            experts(0)
            phase_end(sp, 6)
            for t in (0, 4):
                w = 4 if t == 0 else NT - 4
                sp.dma_start(x[:, t:t + w, :], acc.rearrange("(t p) n -> p t n", p=P)[:, t:t + w, :])\
                  .then_inc(load["x0" if t == 0 else "x"], 16)
            first_experts(3)
            for n in range(7, 12):
                phase_end(sp, n)
            q = gt
            zr3 = zrow3.rearrange("(t p) n -> p t n", p=P)
            with sp.Fori(0, R) as b:
                for u in range(2):
                    sp.wait_ge(q["z"], (b + R) * 2 + u + 1)
                    sp.dma_start(zr3[:, ds(b * 4 + 2 * u, 2), :], z[:, 2 * u:2 * u + 2, :]).then_inc(q["stored"], 16)
            phase_end(sp, 12)
            route(3, rt)
            phase_end(sp, 13)
            experts(3)
            phase_end(sp, 14)
            for t in range(0, NT, 4):
                sp.wait_ge(fin["x"], t // 2 + 2)
                sp.dma_start(out[:, t:t + 4, :], x[:, t:t + 4, :]).then_inc(s_store, 16)
            phase_end(sp, 15)
            sp.wait_ge(s_store, 16 * (NT // 4))
            for u in range(2):
                sp.wait_ge(ex[f"o{u}"], 32 * (E // 2))
                sp.wait_ge(ex[f"e{u}"], 16 * (E // 2))
            sp.wait_ge(gt["stored"], 16 * NT)

        @block.gpsimd
        def _(g):
            def rstd_step(q, i):
                g.wait_ge(q["var"], i + 1)
                g.tensor_tensor(rstd, ve, mhalf[:, :], ALU.pow).then_inc(q["rstd"], 1)

            g.memset(mhalf[:, :], -0.5)
            g.memset(ones[:, :], 1.0)
            g.memset(onesf[:, :], 1.0)
            g.memset(tri[:, :], 1.0)
            g.memset(brow[:, :, :], 0.0)
            g.drain()
            g.affine_select(out=tri[:, :], in_=tri[:, :], compare_op=ALU.is_ge, fill=0.0,
                            base=0, pattern=[[1, P]], channel_multiplier=-1).then_inc(su["tri"], 1)
            phase_end(g, 1)

            def one_head(L):
                q = one
                g.wait_ge(load["ctx"], 16)

                def front(i, b):
                    for u in range(2):
                        g.tensor_copy(cT[:, u], ctxT[:, :, ds((b * 2 + u) * SK, SK)]).then_inc(q["cT"], 1)
                    rstd_step(q, i)

                def back(i, b, more):
                    if more:
                        g.wait_ge(q["V_sb"], i * 2 + 2)
                        front(i + 1, b + 1)

                rounds_of(g, L, front, back)

            one_head(0)
            phase_end(g, 2)
            def gate_back(i, b, more):
                for u in range(2):
                    g.wait_ge(gt["zT_sb"], i * 2 + u + 1)
                    g.tensor_copy(zT_all[:, :, ds((b * 2 + u) * SQ, SQ)], zT[:, u]).then_inc(gt["zT_all"], 1)
                    if more and u == 0:
                        rstd_step(gt, i + 1)

            rounds_of(g, 0, lambda i, b: rstd_step(gt, i), gate_back)
            phase_end(g, 3)
            phase_end(g, 4)
            phase_end(g, 5)

            def experts(L):
                q = ex
                src = zrow if L == 0 else zrow3
                rounds = BASE[L]

                def gather(e):
                    u = e % 2
                    g.tensor_copy(b1u[:, u], b1T[:, e * MC:(e + 1) * MC]).then_inc(q["b1"], 1)
                    for j in range(TB):
                        g.indirect_dma_start(
                            G[:, u, j, 0:src.shape[1]], None, src,
                            bass.IndirectOffsetOnAxis(ap=idx[:, TB * e + j:TB * e + j + 1], axis=0))\
                         .then_inc(q[f"gather{u}"], 16)

                if L == 0:
                    g.wait_ge(rt["probs_out"], 16)
                g.wait_ge(gt["stored"], 16 * (NT // 2) * (1 + L // 3))
                gather(0)
                gather(1)
                if L == 0:
                    g.wait_ge(q["acc"], 16)
                for e in range(E):
                    g.wait_ge(q["y_sb"], 2 * rounds + e + 1)
                    if e + 2 < E:
                        gather(e + 2)
                    if L == 0:
                        if e >= 1:
                            g.wait_ge(q[f"o{(e - 1) % 2}"], 32 * ((e - 1) // 2 + 1))
                        for j in range(TB):
                            g.indirect_dma_start(
                                acc, bass.IndirectOffsetOnAxis(ap=idx[:, TB * e + j:TB * e + j + 1], axis=0),
                                eout[:, e % 2, j, :], None, compute_op=ALU.add).then_inc(q[f"o{e % 2}"], 16)

            experts(0)
            phase_end(g, 6)

            def multi_head(L):
                q = multi
                k0, t0 = NB * (L // 2), UNITS * (L // 2)

                def context(k, u):
                    if in_range(k - 2, NB):
                        g.wait_ge(q["V_ps"], k0 + k - 1)
                    g.tensor_copy(cT[:, u], ctxT[:, :, ds(k * SK, SK)]).then_inc(q["cT"], 1)

                def rstd_of(k, u):
                    g.wait_ge(q["var"], k0 + k + 1)
                    g.tensor_tensor(rstd[:, 2 * u:2 * u + 2], ve[:, 2 * u:2 * u + 2], mhalf[:, 0:2], ALU.pow).then_inc(q["rstd"], 1)

                def spread_keys(k, u):
                    g.wait_ge(q["KT_sb"], k0 + k + 1)
                    if in_range(k - 2, NB):
                        g.wait_ge(q["s_ps"], t0 + k * 4 - 4)
                    for c in range(KC):
                        g.tensor_tensor(KBD[:, u, c], bcast(KT[:, u, c], 1, HC), bcast(headmask[:, :], 2, SK),
                                        ALU.mult).then_inc(q["kbd"], 1)

                def step(r, n):
                    t, k, m_, u = batch_of(r, n)
                    if in_range(t - 1, UNITS):
                        w = (n - 1) % 4
                        g.wait_ge(q["rsum"], t0 + t)
                        g.tensor_tensor(Pr[:, w], Pr[:, w], bcast(rs[:, w], 2, SK), ALU.mult).then_inc(q["p_norm"], 1)
                    if in_range(k + 1, NB):
                        if m_ == 1:
                            spread_keys(k + 1, 1 - u)
                    if in_range(k + 2, NB):
                        if m_ == 1:
                            rstd_of(k + 2, u)
                        if m_ == 3:
                            context(k + 2, u)

                for u in range(2):
                    context(u, u)
                rstd_of(0, 0)
                spread_keys(0, 0)
                rstd_of(1, 1)
                unit_steps(g, step)

            multi_head(1)
            phase_end(g, 7)
            with g.Fori(0, NB // 2) as i:
                rstd_step(f1, i)
            phase_end(g, 8)
            multi_head(2)
            phase_end(g, 9)
            q = f2

            def step(r, n):
                t = r * 4 + n
                if in_range(t):
                    g.wait_ge(q["st2"], t + 1)
                    g.tensor_tensor(rs[:, n, 0:1], sm[:, n, 0:1], mhalf[:, 0:1], ALU.pow).then_inc(q["rstd2"], 1)
                if in_range(r * 4 + 4):
                    if n == 0:
                        rstd_step(q, r + 1)
                if in_range(t - 2):
                    g.wait_ge(q["nTh"], t - 1)
                    g.tensor_tensor(h2s[:, 1, n % 2], h2T[:, n % 2], h2s[:, 0, n % 2], ALU.subtract).then_inc(q["nTs"], 1)

            rstd_step(q, 0)
            for n in range(4):
                step(0, n)
            with g.Fori(1, NT // 4 - 1) as r:
                for n in range(4):
                    step(r, n)
            for t in range(NT - 4, NT + 2):
                step(t // 4, t % 4)
            phase_end(g, 10)
            one_head(3)
            phase_end(g, 11)
            with g.Fori(0, R) as b:
                rstd_step(gt, b + R)
            phase_end(g, 12)
            phase_end(g, 13)
            experts(3)
            phase_end(g, 14)
            for u in range(2):
                g.wait_ge(ex[f"e{u}"], 16 * (E // 2))
            for t in range(NT):
                if t >= 4:
                    g.wait_ge(fin["x"], t // 2 - 1)
                g.indirect_dma_start(eout[:, t // 2 % 2, t % 2, :], None, eo,
                                     bass.IndirectOffsetOnAxis(ap=slot_i[:, t:t + 1], axis=0))\
                 .then_inc(fin[f"g{t // 2 % 2}"], 16)
            phase_end(g, 15)

        @block.tensor
        def _(pe):
            def mm(o, l, r, a, b):
                return pe.matmul(o, l, r, start=a, stop=b)

            def transposed_z(q, i, u, banks=MISC):
                pe.wait_ge(q["z"], i * 2 + u + 1)
                o = banks[u][:, :].rearrange("p (k n) -> p k n", k=KC)
                for k in range(KC):
                    for t in range(TB):
                        m = pe.transpose(o[:, k, t * P:(t + 1) * P], z[:, 2 * u + t, k * P:(k + 1) * P], ident[:, :])
                m.then_inc(q["zT_ps"], 1)

            def project_q(q, L, i, u, banks=MISC):
                pe.wait_ge(q["zT_sb"], i * 2 + u + 1)
                o = banks[u][:, :].rearrange("p (k n) -> p k n", k=KC)
                for m_ in range(KC):
                    for k in range(KC):
                        m = mm(o[:, m_, :], W[f"q{L}"][:, k, m_ * P:(m_ + 1) * P], zT[:, u, k, :], k == 0, k == KC - 1)
                m.then_inc(q["q_ps"], 1)

            def keys_values(q, L, i, b, u):
                pe.wait_ge(q["cT"], i * 2 + u + 1)
                bank = MISC[u]
                for m_ in range(KC):
                    for k in range(KC):
                        m = mm(bank[:, m_ * SK:(m_ + 1) * SK], W[f"k{L}"][:, k, m_ * P:(m_ + 1) * P], cT[:, u, k, :],
                               k == 0, k == KC - 1)
                if L != 3:
                    for k in range(KC):
                        m = mm(bank[0:SK, 256:512], cT[:, u, k, :], W[f"v{L}"][:, k, :], k == 0, k == KC - 1)
                    m.then_inc(q["K_ps"], 1)
                else:
                    for m_ in range(KC):
                        for k in range(KC):
                            m = mm(bank[:, 256 + m_ * SK:256 + (m_ + 1) * SK], W["v3"][:, k, m_ * P:(m_ + 1) * P],
                                   cT[:, u, k, :], k == 0, k == KC - 1)
                    m.then_inc(q["K_ps"], 1)
                    pe.wait_ge(q["VT_sb"], b * 2 + u + 1)
                    for k in range(KC):
                        m = mm(bank[0:SK, 256:512], VT1[:, u, k, :], W["o3"][:, k, :], k == 0, k == KC - 1)
                    m.then_inc(q["V_ps"], 1)

            pe.wait_ge(load["base"], 16 * (10 + len(ROWS)))
            pe.wait_ge(load["dft"], 16 * 5)
            C, S, nS, Wr, Wi = range(5)
            for a, terms in enumerate([[(Wr, C), (Wi, S)], [(Wi, C), (Wr, nS)]]):
                o = psum[a][:, :].rearrange("p (k n) -> p k n", k=KC)
                for m_ in range(KC):
                    for n, (w, f) in enumerate(terms):
                        for k in range(KC):
                            m = mm(o[:, m_, :], dft[:, w, k, m_ * P:(m_ + 1) * P], dft[:, f, k, :],
                                   n == 0 and k == 0, n == 1 and k == KC - 1)
            m.then_inc(su["AB_ps"], 1)
            pe.wait_ge(su["AB_sb"], 1)
            o = psum[2][:, :].rearrange("p (k n) -> p k n", k=KC)
            for m_ in range(KC):
                for a, f in enumerate([C, nS]):
                    for k in range(KC):
                        m = mm(o[:, m_, :], ABT[:, a, k, m_ * P:(m_ + 1) * P], dft[:, f, k, :],
                               a == 0 and k == 0, a == 1 and k == KC - 1)
            m.then_inc(su["M_ps"], 1)
            phase_end(pe, 1)

            def one_head(L):
                q = one
                turned = psum[0:2]
                pe.wait_ge(load["wone"], 48 * (1 + L // 3))

                def front(i, b):
                    for u in range(2):
                        keys_values(q, L, i, b, u)
                    for u in range(2):
                        transposed_z(q, i, u, turned)
                    for u in range(2):
                        project_q(q, L, i, u, turned)

                def back(i, b, more):
                    for u in range(2):
                        pe.wait_ge(q["q_sb"], i * 2 + u + 1)
                        o = psum[u][:, 0:TB * SK].rearrange("p (t n) -> p t n", t=TB)
                        if L == 0:
                            mm(o, ones[0:96, :], bcast(brow[:, 0, ds((b * 2 + u) * SK, SK)], 1, TB), True, False)
                        for t in range(TB):
                            for k in range(KC):
                                m = mm(o[:, t, :], qT[:, u, k, t * P:(t + 1) * P], KT[:, u, k, :],
                                       L == 3 and k == 0, k == KC - 1 and (L == 3 or t == TB - 1))
                        m.then_inc(q["s_ps"], 1)
                    if more:
                        for u in range(2):
                            pe.wait_ge(q["V_sb"], i * 2 + u + 1)
                            keys_values(q, L, i + 1, b + 1, u)
                    for u in range(2):
                        pe.wait_ge(q["p_sb"], i * 2 + u + 1)
                        for t in range(TB):
                            m = pe.transpose(psum[2 + u][0:SK, t * P:(t + 1) * P], P1[:, u, t, :], ident[:, :])
                        m.then_inc(q["pT_ps"], 1)
                    if more:
                        for u in range(2):
                            transposed_z(q, i + 1, u, turned)
                    for u in range(2):
                        pe.wait_ge(q["pT_sb"], i * 2 + u + 1)
                        pe.wait_ge(q["V_sb"], i * 2 + u + 1)
                        for t in range(TB):
                            m = mm(psum[4 + u][:, t * D:(t + 1) * D], PT1[0:SK, u, t * P:(t + 1) * P], V1[0:SK, u, :], True, True)
                        m.then_inc(q["y_ps"], 1)
                    if more:
                        for u in range(2):
                            project_q(q, L, i + 1, u, turned)
                        pe.wait_ge(q["x"], i * 4 + 4)

                rounds_of(pe, L, front, back)

            one_head(0)
            phase_end(pe, 2)

            def gate(L):
                q = gt

                def front(i, b):
                    for u in range(2):
                        transposed_z(q, i, u)

                def back(i, b, more):
                    for u in range(2):
                        pe.wait_ge(q["zT_sb"], i * 2 + u + 1)
                        for t in range(TB):
                            for k in range(KC):
                                m = mm(psum[u][:, t * E:(t + 1) * E], zT[:, u, k, t * P:(t + 1) * P],
                                       gates[:, L // 3, k, :], k == 0, k == KC - 1)
                        m.then_inc(q["l_ps"], 1)
                    if more:
                        front(i + 1, b + 1)
                        pe.wait_ge(q["l_sb"], i * 2 + 2)

                rounds_of(pe, L, front, back)

            gate(0)
            phase_end(pe, 3)

            pe.wait_ge(load["shared"], 32)
            ws1 = ffw[:, 0, :].rearrange("p (k n) -> p k n", k=KC)
            ws2 = ffw[:, 1, :].rearrange("p (m n) -> p m n", m=MC)
            q = sh
            with pe.Fori(0, T // 512) as i:
                for m_ in range(MC):
                    if m_ >= 4:
                        pe.wait_ge(q["h_sb"], i * MC + m_ - 3)
                    for k in range(KC):
                        m = mm(psum[m_ % 4][:, :], ws1[:, k, m_ * P:(m_ + 1) * P], zT_all[:, k, ds(i * 512, 512)],
                               k == 0, k == KC - 1)
                    m.then_inc(q["h_ps"], 1)
                    pe.wait_ge(q["cmp"], i * HALF + m_ + 1)
                    mm(psum[6][:, 0:P], ones[:, :], sel.rearrange("p t e -> p (t e)"), True, True).then_inc(q["cnt_ps"], 1)
                pe.wait_ge(q["h_sb"], i * MC + MC)
                for t in range(4):
                    for k in range(MC):
                        m = mm(psum[4 + t // 2][:, (t % 2) * D:(t % 2 + 1) * D], hT[:, k, t * P:(t + 1) * P], ws2[:, k, :],
                               k == 0, k == MC - 1)
                    if t % 2:
                        m.then_inc(q["y_ps"], 1)
                pe.wait_ge(q["x"], i * 2 + 2)
            phase_end(pe, 4)

            def ranks(bank, s):
                o = bank[:, 0:P].rearrange("p (t e) -> p t e", t=NT)
                m = mm(o, tri[:, :], s, True, False)
                for t in range(NT - 1):
                    m = mm(o[:, t + 1:, :], ones[:, :], bcast(s[:, t, :], 1, NT - 1 - t), False, t == NT - 2)
                return m

            def route(L):
                q = rt
                n = 1 + L // 3
                if L == 0:
                    pe.wait_ge(q["c_in"], 1)
                    mm(psum[0][:, 0:P], ones[:, :], sel.rearrange("p t e -> p (t e)"), True, True)
                    ranks(psum[1], sel2).then_inc(q["c_ps"], 1)
                pe.wait_ge(q["rank_in"], n)
                ranks(psum[2], sel).then_inc(q["rank_ps"], 1)
                pe.wait_ge(q["hot"], n)
                for t in range(NT):
                    m = mm(psum[3][:, 0:2 * P], hi1[:, t].rearrange("p e a -> p (e a)"),
                           lo2[:, t].rearrange("p w n -> p (w n)"), t == 0, t == NT - 1)
                m.then_inc(q["idx_ps"], 1)
                pe.wait_ge(q["slot_in"], 16 * n)
                pe.transpose(psum[4][:, 0:16], work[0:16, 2, :], ident[0:16, 0:16]).then_inc(q["sT_ps"], 1)

            route(0)
            phase_end(pe, 5)

            def experts(L):
                q = ex

                def prepare(i, u):
                    pe.wait_ge(q[f"gather{u}"], i * 32 + 32)
                    o = MISC[u][:, :].rearrange("p (k n) -> p k n", k=KC)
                    for k in range(KC):
                        for t in range(TB):
                            m = pe.transpose(o[:, k, t * P:(t + 1) * P], G[:, u, t, k * P:(k + 1) * P], ident[:, :])
                    m.then_inc(q["xT_ps"], 1)

                def first(i, u):
                    pe.wait_ge(q["xT_sb"], i * 2 + u + 1)
                    pe.wait_ge(q[f"w{u}"], i * 32 + 32)
                    w = ew[:, u, 0, :].rearrange("p (k n) -> p k n", k=KC)
                    for m_ in range(MC):
                        if m_ % 2 == 0:
                            pe.wait_ge(q["h_sb"], i * 2 * MC + u * MC + m_ - 6) if u * MC + m_ >= 8 else None
                        for k in range(KC):
                            m = mm(psum[m_ // 2][:, (m_ % 2) * CAP:(m_ % 2 + 1) * CAP], w[:, k, m_ * P:(m_ + 1) * P],
                                   xeT[:, u, k, :], k == 0, k == KC - 1)
                        if m_ % 2:
                            m.then_inc(q["h_ps"], 1)

                def second(i, u):
                    pe.wait_ge(q["h_sb"], i * 2 * MC + (u + 1) * MC)
                    w = ew[:, u, 1, :].rearrange("p (m n) -> p m n", m=MC)
                    for t in range(TB):
                        for k in range(MC):
                            m = mm(psum[4 + u][:, t * D:(t + 1) * D], heT[:, u, k, t * P:(t + 1) * P], w[:, k, :],
                                   k == 0, k == MC - 1)
                    m.then_inc(q["y_ps"], 1)

                with pe.Fori(0, E // 2) as b:
                    i = b + BASE[L]
                    prepare(i, 0)
                    first(i, 0)
                    prepare(i, 1)
                    second(i, 0)
                    first(i, 1)
                    second(i, 1)

            pe.wait_ge(su["gsum_in"], 1)
            mm(psum[5][:, 0:2], onesf[:, :], gam[:, 0:2], True, True).then_inc(su["gsum_ps"], 1)
            pe.wait_ge(su["gsum_out"], 1)
            experts(0)
            phase_end(pe, 6)

            def multi_head(L):
                q = multi
                k0, t0 = NB * (L // 2), UNITS * (L // 2)

                def keys(k, u):
                    pe.wait_ge(q["cT"], k0 + k + 1)
                    if in_range(k - 1, NB):
                        pe.wait_ge(q["V_sb"], k0 + k)
                    for m_ in range(KC):
                        for c in range(KC):
                            m = mm(psum[6][:, m_ * SK:(m_ + 1) * SK], W[f"k{L}"][:, c, m_ * P:(m_ + 1) * P], cT[:, u, c, :],
                                   c == 0, c == KC - 1)
                    m.then_inc(q["K_ps"], 1)

                def turn_z(k, u):
                    pe.wait_ge(q["z"], k0 + k + 1)
                    pe.wait_ge(q["KT_sb"], k0 + k + 1)
                    o = psum[6][:, :].rearrange("p (k n) -> p k n", k=KC)
                    for c in range(KC):
                        for t in range(TB):
                            m = pe.transpose(o[:, c, t * P:(t + 1) * P], z[:, 2 * u + t, c * P:(c + 1) * P], ident[:, :])
                    m.then_inc(q["zT_ps"], 1)

                def queries(k, u):
                    pe.wait_ge(q["zT_sb"], k0 + k + 1)
                    o = psum[6][:, :].rearrange("p (k n) -> p k n", k=KC)
                    for m_ in range(KC):
                        for c in range(KC):
                            m = mm(o[:, m_, :], W[f"q{L}"][:, c, m_ * P:(m_ + 1) * P], zT[:, u, c, :], c == 0, c == KC - 1)
                    m.then_inc(q["q_ps"], 1)

                def values(k, u):
                    pe.wait_ge(q["q_sb"], k0 + k + 1)
                    for c in range(KC):
                        m = mm(psum[6][0:SK, 256:512], cT[:, u, c, :], W[f"v{L}"][:, c, :], c == 0, c == KC - 1)
                    m.then_inc(q["V_ps"], 1)

                def scores(t, k, m_, u, n):
                    if m_ == 0:
                        pe.wait_ge(q["q_sb"], k0 + k + 1)
                        pe.wait_ge(q["kbd"], 2 * k0 + k * 2 + 2)
                    if in_range(t - 2, UNITS):
                        pe.wait_ge(q["sub"], t0 + t - 1)
                    for j in range(2):
                        o = psum[2 * (n % 2) + j][:, 0:4 * SK].rearrange("p (h n) -> p h n", h=4)
                        mm(o, ones[0:96, :], bcast(brow[:, L, ds(k * SK, SK)], 1, 4), True, False)
                        m = mm(o, qT[:, u, m_ % 2, (m_ // 2) * P:(m_ // 2 + 1) * P], KBD[:, u, m_ % 2, 4 * j:4 * j + 4, :],
                               False, True)
                    m.then_inc(q["s_ps"], 1)

                def turn(w, slot):
                    pe.wait_ge(q["p_norm"], t0 + w + 1)
                    for j in range(2):
                        if in_range(w - 1, UNITS):
                            pe.wait_ge(q["pT_sb"], 2 * t0 + w * 2 + j - 1)
                        for h in range(4):
                            m = pe.transpose(psum[4 + j][0:SK, h * P:(h + 1) * P], Pr[:, slot, 4 * j + h, :], ident[:, :])
                        m.then_inc(q["pT_ps"], 1)

                def attend(k, u):
                    pe.wait_ge(q["pT_sb"], 2 * t0 + k * 8 + 8)
                    pe.wait_ge(q["V_sb"], k0 + k + 1)
                    if in_range(k - 1, NB):
                        pe.wait_ge(q["x"], k0 + k)
                    o = psum[7][:, :].rearrange("p (k n) -> p k n", k=KC)
                    for c in range(KC):
                        for j in range(2):
                            for g_ in range(4):
                                h = c * HC + 2 * g_ + j
                                m = mm(o[32 * g_:32 * g_ + 32, c, :], Vp[0:SK, u, h, :], PT[0:SK, u, h, :], j == 0, j == 1)
                    m.then_inc(q["O_ps"], 1)

                def output(k, u):
                    pe.wait_ge(q["O_sb"], k0 + k + 1)
                    for t in range(TB):
                        for c in range(KC):
                            m = mm(psum[7][:, t * D:(t + 1) * D], OT[:, u, c, t * P:(t + 1) * P], W[f"o{L}"][:, c, :],
                                   c == 0, c == KC - 1)
                    m.then_inc(q["y_ps"], 1)

                def step(r, n):
                    t, k, m_, u = batch_of(r, n)
                    if in_range(t, UNITS):
                        scores(t, k, m_, u, n)
                    if in_range(t - 3, UNITS):
                        turn(t - 3, (n - 3) % 4)
                    if in_range(k + 1, NB):
                        (keys, turn_z, queries, values)[m_](k + 1, 1 - u)
                    if in_range(k - 2, NB) and m_ == 1:
                        output(k - 2, u)
                    if in_range(k - 1, NB) and m_ == 3:
                        attend(k - 1, 1 - u)

                pe.wait_ge(load["weights"], 16 * (len(WEIGHTS) - 6))
                for part in (keys, turn_z, queries, values):
                    part(0, 0)
                unit_steps(pe, step)

            multi_head(1)
            phase_end(pe, 7)

            q = f1

            def spectral_front(i, b):
                for u in range(2):
                    transposed_z(q, i, u)

            def spectral_back(i, b, more):
                for u in range(2):
                    pe.wait_ge(q["zT_sb"], i * 2 + u + 1)
                    for t in range(TB):
                        for k in range(KC):
                            m = mm(psum[u][:, t * D:(t + 1) * D], zT[:, u, k, t * P:(t + 1) * P], Mf[:, k, :],
                                   k == 0, k == KC - 1)
                    m.then_inc(q["y_ps"], 1)
                if more:
                    spectral_front(i + 1, b + 1)
                    pe.wait_ge(q["x"], i * 2 + 2)

            rounds_of(pe, 0, spectral_front, spectral_back)
            phase_end(pe, 8)
            multi_head(2)
            phase_end(pe, 9)
            q = f2
            wf = tern[0].rearrange("p (k n) -> p k n", k=KC)
            wp = tern[1].rearrange("p (m n) -> p m n", m=MC)

            def turn_z(r, u):
                pe.wait_ge(q["z"], r * 2 + u + 1)
                if in_range(r * 4 - 4) or u:
                    pe.wait_ge(q["zT_sb"], r * 2 + u)
                o = psum[6][:, :].rearrange("p (k n) -> p k n", k=KC)
                for k in range(KC):
                    for t in range(TB):
                        m = pe.transpose(o[:, k, t * P:(t + 1) * P], z[:, 2 * u + t, k * P:(k + 1) * P], ident[:, :])
                m.then_inc(q["zT_ps"], 1)

            def step(r, n):
                t = r * 4 + n
                if in_range(t):
                    pe.wait_ge(q["zTs"], r * 2 + n // 2 + 1)
                    if in_range(t - 2):
                        pe.wait_ge(q["h_sb"], t - 1)
                    for j in range(2):
                        for k in range(KC):
                            for a in range(2):
                                m = mm(psum[2 * (n % 2) + j][:, :], zTs[:, a, n // 2, k, (n % 2) * P:(n % 2 + 1) * P],
                                       wf[:, k, j * 512:(j + 1) * 512], k == 0 and a == 0, k == KC - 1 and a == 1)
                    m.then_inc(q["h_ps"], 1)
                if in_range(t - 2):
                    pe.wait_ge(q["n2"], t - 1)
                    if in_range(t - 3):
                        pe.wait_ge(q["nT_sb"], t - 2)
                    for h in range(MC):
                        m = pe.transpose(psum[4 + h // 4][:, (h % 4) * P:(h % 4 + 1) * P],
                                         h2[:, (n + 2) % 4, h * P:(h + 1) * P], ident[:, :])
                    m.then_inc(q["nT_ps"], 1)
                if in_range(t - 4):
                    pe.wait_ge(q["nTs"], t - 3)
                    pe.wait_ge(q["x"], t - 3)
                    for h in range(MC):
                        for a in range(2):
                            m = mm(psum[7][:, 0:D], h2s[:, a, n % 2, h, :], wp[:, h, :],
                                   h == 0 and a == 0, h == MC - 1 and a == 1)
                    m.then_inc(q["y_ps"], 1)
                if n in (1, 2) and in_range(r * 4 + 4):
                    turn_z(r + 1, n - 1)

            for u in range(2):
                turn_z(0, u)
            for n in range(4):
                step(0, n)
            with pe.Fori(1, NT // 4 - 1) as r:
                for n in range(4):
                    step(r, n)
            for t in range(NT - 4, NT + 4):
                step(t // 4, t % 4)
            phase_end(pe, 10)
            one_head(3)
            phase_end(pe, 11)
            gate(3)
            phase_end(pe, 12)
            route(3)
            phase_end(pe, 13)
            experts(3)
            phase_end(pe, 14)
            phase_end(pe, 15)

        @block.scalar
        def _(act):
            def copy(o, i_):
                return nc.scalar.activation(o, i_, ACT.Copy)

            def take_z(q, i, u, banks=MISC):
                act.wait_ge(q["zT_ps"], i * 2 + u + 1)
                copy(zT[:, u], banks[u][:, :].rearrange("p (k n) -> p k n", k=KC)).then_inc(q["zT_sb"], 1)

            def take_q(q, L, i, u, banks=MISC):
                act.wait_ge(q["q_ps"], i * 2 + u + 1)
                for k in range(KC):
                    c = COL[f"q{L}"] + k
                    m = nc.scalar.activation(qT[:, u, k], banks[u][:, k * SQ:(k + 1) * SQ], ACT.Identity, bias=cols[:, c:c + 1])
                m.then_inc(q["q_sb"], 1)

            def take_k(q, L, i, u, scale):
                act.wait_ge(q["K_ps"], i * 2 + u + 1)
                for k in range(KC):
                    c = COL[f"k{L}"] + k
                    m = nc.scalar.activation(KT[:, u, k], MISC[u][:, k * SK:(k + 1) * SK], ACT.Identity,
                                             bias=cols[:, c:c + 1], scale=scale)
                m.then_inc(q["KT_sb"], 1)

            act.wait_ge(load["base"], 16 * (10 + len(ROWS)))
            nc.scalar.activation(tg[:, :], tg[:, :], ACT.Tanh).then_inc(su["tanh"], 1)
            act.wait_ge(su["AB_ps"], 1)
            for a in range(2):
                m = copy(ABT[:, a], psum[a][:, :].rearrange("p (k n) -> p k n", k=KC))
            m.then_inc(su["AB_sb"], 1)
            phase_end(act, 1)

            def one_head(L):
                q = one
                turned = psum[0:2]

                def take_keys(i, u):
                    take_k(q, L, i, u, 1.0 / 16)
                    if L == 3:
                        for k in range(KC):
                            c = COL["v3"] + k
                            m = nc.scalar.activation(VT1[:, u, k], MISC[u][:, 256 + k * SK:256 + (k + 1) * SK],
                                                     ACT.Identity, bias=cols[:, c:c + 1])
                        m.then_inc(q["VT_sb"], 1)

                def front(i, b):
                    for u in range(2):
                        take_keys(i, u)
                    for u in range(2):
                        take_z(q, i, u, turned)
                    for u in range(2):
                        take_q(q, L, i, u, turned)

                def back(i, b, more):
                    for u in range(2):
                        act.wait_ge(q["nmax"], i * 2 + u + 1)
                        for t in range(TB):
                            m = nc.scalar.activation(P1[:, u, t, :], psum[u][:, t * SK:(t + 1) * SK], ACT.Exp,
                                                     bias=mx[:, u, t:t + 1], accum_out=sm[:, u, t:t + 1])
                        m.then_inc(q["p_sb"], 1)
                    if more:
                        for u in range(2):
                            take_keys(i + 1, u)
                    for u in range(2):
                        act.wait_ge(q["pT_ps"], i * 2 + u + 1)
                        copy(PT1[0:SK, u, :], psum[2 + u][0:SK, 0:SQ]).then_inc(q["pT_sb"], 1)
                    if more:
                        for u in range(2):
                            take_z(q, i + 1, u, turned)
                        for u in range(2):
                            take_q(q, L, i + 1, u, turned)

                rounds_of(act, L, front, back)

            one_head(0)
            phase_end(act, 2)

            def gate(L):
                q = gt

                def front(i, b):
                    for u in range(2):
                        take_z(q, i, u)

                def back(i, b, more):
                    if more:
                        act.wait_ge(q["l_ps"], i * 2 + 2)
                        if L == 0:
                            act.wait_ge(q["zT_all"], i * 2 + 2)
                        front(i + 1, b + 1)

                rounds_of(act, L, front, back)
                act.wait_ge(rt["logit"], 1 + L // 3)
                nc.scalar.activation(prob, logit, ACT.Exp).then_inc(rt["prob_exp"], 1)

            gate(0)
            phase_end(act, 3)
            q = sh
            with act.Fori(0, T // 512) as i:
                for m_ in range(MC):
                    act.wait_ge(q["h_ps"], i * MC + m_ + 1)
                    nc.scalar.activation(hT[:, m_, :], psum[m_ % 4][:, :], ACT.Gelu_apprx_tanh,
                                         bias=b1T[:, E * MC + m_:E * MC + m_ + 1]).then_inc(q["h_sb"], 1)
            phase_end(act, 4)
            phase_end(act, 5)

            def experts(L):
                q = ex
                with act.Fori(0, E // 2) as b:
                    i = b + BASE[L]

                    def take_rows(u):
                        act.wait_ge(q["b1"], i * 2 + u + 1)
                        act.wait_ge(q["xT_ps"], i * 2 + u + 1)
                        copy(xeT[:, u], MISC[u][:, :].rearrange("p (k n) -> p k n", k=KC)).then_inc(q["xT_sb"], 1)

                    take_rows(0)
                    for u in range(2):
                        if u == 1:
                            take_rows(1)
                        for m_ in range(MC):
                            if m_ % 2 == 0:
                                act.wait_ge(q["h_ps"], i * MC + u * 4 + m_ // 2 + 1)
                            src = psum[m_ // 2][:, (m_ % 2) * CAP:(m_ % 2 + 1) * CAP]
                            if L == 0:
                                m = nc.scalar.activation(heT[:, u, m_, :], src, ACT.Gelu_apprx_tanh, bias=b1u[:, u, m_:m_ + 1])
                            else:
                                m = nc.scalar.activation(heT[:, u, m_, :], src, ACT.Relu)
                            m.then_inc(q["h_sb"], 1)

            experts(0)
            phase_end(act, 6)

            def multi_head(L):
                q = multi
                k0, t0 = NB * (L // 2), UNITS * (L // 2)

                def take_keys(k, u):
                    act.wait_ge(q["K_ps"], k0 + k + 1)
                    if in_range(k - 2, NB):
                        act.wait_ge(q["kbd"], 2 * k0 + k * 2 - 2)
                    for c in range(KC):
                        b = COL[f"k{L}"] + c
                        m = nc.scalar.activation(KT[:, u, c], psum[6][:, c * SK:(c + 1) * SK], ACT.Identity,
                                                 bias=cols[:, b:b + 1], scale=0.25)
                    m.then_inc(q["KT_sb"], 1)

                def take_turned_z(k, u):
                    act.wait_ge(q["zT_ps"], k0 + k + 1)
                    copy(zT[:, u], psum[6][:, :].rearrange("p (k n) -> p k n", k=KC)).then_inc(q["zT_sb"], 1)

                def take_queries(k, u):
                    act.wait_ge(q["q_ps"], k0 + k + 1)
                    if in_range(k - 2, NB):
                        act.wait_ge(q["s_ps"], t0 + k * 4 - 4)
                    for c in range(KC):
                        b = COL[f"q{L}"] + c
                        m = nc.scalar.activation(qT[:, u, c], psum[6][:, c * SQ:(c + 1) * SQ], ACT.Identity,
                                                 bias=cols[:, b:b + 1])
                    m.then_inc(q["q_sb"], 1)

                def take_O(k, u):
                    act.wait_ge(q["O_ps"], k0 + k + 1)
                    if in_range(k - 2, NB):
                        act.wait_ge(q["y_ps"], k0 + k - 1)
                    copy(OT[:, u], psum[7][:, :].rearrange("p (k n) -> p k n", k=KC)).then_inc(q["O_sb"], 1)

                def take_turned(w, k, m_, u):
                    if m_ == 0 and in_range(k - 2, NB):
                        act.wait_ge(q["O_ps"], k0 + k - 1)
                    for j in range(2):
                        act.wait_ge(q["pT_ps"], 2 * t0 + w * 2 + j + 1)
                        h = (m_ % 2) * HC + 4 * j
                        copy(PT[0:SK, u, h:h + 4, (m_ // 2) * P:(m_ // 2 + 1) * P],
                             psum[4 + j][0:SK, :].rearrange("p (h n) -> p h n", h=4)).then_inc(q["pT_sb"], 1)

                def step(r, n):
                    t, k, m_, u = batch_of(r, n)
                    if in_range(t, UNITS):
                        act.wait_ge(q["sub"], t0 + t + 1)
                        nc.scalar.activation(Pr[:, n % 4], Pr[:, n % 4], ACT.Exp).then_inc(q["p_exp"], 1)
                    if in_range(t - 3, UNITS):
                        if m_ == 3:
                            take_turned(t - 3, k, 0, u)
                        else:
                            take_turned(t - 3, k - 1, m_ + 1, 1 - u)
                    if in_range(k + 1, NB) and m_ < 3:
                        (take_keys, take_turned_z, take_queries)[m_](k + 1, 1 - u)
                    if in_range(k - 1, NB) and m_ == 3:
                        take_O(k - 1, 1 - u)

                for part in (take_keys, take_turned_z, take_queries):
                    part(0, 0)
                unit_steps(act, step)

            multi_head(1)
            phase_end(act, 7)

            def spectral_front(i, b):
                for u in range(2):
                    take_z(f1, i, u)

            def spectral_back(i, b, more):
                if more:
                    act.wait_ge(f1["y_ps"], i * 2 + 2)
                    spectral_front(i + 1, b + 1)

            rounds_of(act, 0, spectral_front, spectral_back)
            phase_end(act, 8)
            multi_head(2)
            phase_end(act, 9)
            q = f2

            def take_turned_z(r, u):
                act.wait_ge(q["zT_ps"], r * 2 + u + 1)
                if in_range(r * 4 - 4):
                    act.wait_ge(q["zTs"], r * 2 + u - 1)
                    act.wait_ge(q["h_ps"], r * 4 + 2 * u - 2)
                copy(zTs[:, 0, u], psum[6][:, :].rearrange("p (k n) -> p k n", k=KC))
                copy(zT[:, u], psum[6][:, :].rearrange("p (k n) -> p k n", k=KC)).then_inc(q["zT_sb"], 1)

            def step(r, n):
                t = r * 4 + n
                if in_range(t):
                    act.wait_ge(q["h_ps"], t + 1)
                    if in_range(t - 4):
                        act.wait_ge(q["nT_ps"], t - 3)
                    for j in range(2):
                        m = nc.scalar.activation(h2[:, n, j * 512:(j + 1) * 512], psum[2 * (n % 2) + j][:, :], ACT.Gelu)
                    m.then_inc(q["h_sb"], 1)
                if in_range(t - 2):
                    act.wait_ge(q["nT_ps"], t - 1)
                    if in_range(t - 4):
                        act.wait_ge(q["nTs"], t - 3)
                    for h in range(MC):
                        m = nc.scalar.activation(h2T[:, n % 2, h, :], psum[4 + h // 4][:, (h % 4) * P:(h % 4 + 1) * P],
                                                 ACT.Identity, bias=lnwb[:, 1, h:h + 1], scale=lnwb[:, 0, h:h + 1])
                    m.then_inc(q["nT_sb"], 1)
                if n in (1, 3) and in_range(r * 4 + 4):
                    take_turned_z(r + 1, n // 2)

            for u in range(2):
                take_turned_z(0, u)
            for n in range(4):
                step(0, n)
            with act.Fori(1, NT // 4 - 1) as r:
                for n in range(4):
                    step(r, n)
            for t in range(NT - 4, NT + 2):
                step(t // 4, t % 4)
            phase_end(act, 10)
            one_head(3)
            phase_end(act, 11)
            gate(3)
            phase_end(act, 12)
            phase_end(act, 13)
            experts(3)
            phase_end(act, 14)
            phase_end(act, 15)

        @block.vector
        def _(v):
            V = nc.vector

            def norm(q, i, b, add=None, z_free=None):
                for t in range(4):
                    V.bn_stats(st[:, t, :], x[:, ds(b * 4 + t, 1), :].rearrange("p t n -> p (t n)"))
                v.drain()
                for t in range(4):
                    V.bn_aggr(mv[:, t, :], st[:, t, :])
                v.drain()
                V.tensor_scalar(ve, mv[:, :, 1], EPS, None, ALU.add).then_inc(q["var"], 1)
                v.wait_ge(q["rstd"], i + 1)
                if z_free is not None:
                    z_free()
                for t in range(4):
                    m = V.tensor_scalar(z[:, t, :], x[:, ds(b * 4 + t, 1), :].rearrange("p t n -> p (t n)"), mv[:, t, 0:1],
                                        rstd[:, t:t + 1], ALU.subtract, ALU.mult)
                    if t % 2:
                        m.then_inc(q["z"], 1)
                if add is not None:
                    v.drain()
                    V.tensor_tensor(x[:, ds(b * 4, 4), :], x[:, ds(b * 4, 4), :], bcast(rows[:, ROWS.index(add), :], 1, 4), ALU.add)

            v.wait_ge(load["base"], 16 * (10 + len(ROWS)))
            v.wait_ge(su["tanh"], 1)
            for n in range(4):
                c = COL[f"k{n}"]
                V.tensor_scalar(cols[:, c:c + 2], cols[:, c:c + 2], 0.25 if n in (1, 2) else 1.0 / 16, None, ALU.mult)
            for n, t_ in (("s0", 4), ("o1", 1), ("f1", 5), ("o2", 2), ("o3", 3)):
                r = rows[:, ROWS.index(n), :]
                V.tensor_scalar(r, r, tg[:, t_:t_ + 1], None, ALU.mult)
            V.tensor_copy(bitf[:, :, :], bits[:, :, :])
            v.wait_ge(load["masks"], 64)
            v.wait_ge(su["tri"], 1)
            for a in range(3):
                src = mrow_i[0:1, a, :] if a != 1 else mrow_i[0:1, 1, 0:NB * SK // 4].bitcast(mybir.dt.uint8)
                V.tensor_scalar(mrow[0:1, a, :], src, 0.0, NEG, ALU.is_equal, ALU.mult)
            v.drain()
            V.tensor_tensor(mrow[0:1, 1, :], mrow[0:1, 1, :], fside_r[0:1, :], ALU.add)
            v.drain()
            for a in range(3):
                for part in range(3):
                    V.tensor_copy(mrow_b[0:1, :], mrow[0:1, a, :])
                    v.drain()
                    V.tensor_copy(brow[32 * part:32 * part + 1, a, :], mrow_b[0:1, :])
                    V.tensor_tensor(mrow[0:1, a, :], mrow[0:1, a, :], mrow_b[0:1, :], ALU.subtract)
                    v.drain()
            v.wait_ge(su["M_ps"], 1)
            V.tensor_scalar(Mf[:, :, :], psum[2][:, :].rearrange("p (k n) -> p k n", k=KC), tg[:, 5:6], 1.0 / D,
                            ALU.mult, ALU.mult)
            phase_end(v, 1)

            def one_head(L):
                q = one
                for n in ("x0", "x"):
                    v.wait_ge(load[n], 16 if L == 0 else 32)

                def take_values(i, b):
                    for u in range(2):
                        v.wait_ge(q["V_ps" if L == 3 else "KT_sb"], (b if L == 3 else i) * 2 + u + 1)
                        if L == 0:
                            V.tensor_tensor(V1[0:SK, u, :], MISC[u][0:SK, 256:512], rows[0:SK, ROWS.index("v0"), :], ALU.add)\
                             .then_inc(q["V_sb"], 1)
                        else:
                            V.tensor_copy(V1[0:SK, u, :], MISC[u][0:SK, 256:512]).then_inc(q["V_sb"], 1)

                def front(i, b):
                    norm(q, i, b, "o3" if L == 3 else None)
                    take_values(i, b)

                def back(i, b, more):
                    for u in range(2):
                        v.wait_ge(q["s_ps"], i * 2 + u + 1)
                        V.tensor_reduce(mx[:, u, 0:TB], psum[u][:, 0:TB * SK].rearrange("p (t n) -> p t n", t=TB),
                                        AX.X, ALU.max, negate=True).then_inc(q["nmax"], 1)
                    if more:
                        norm(q, i + 1, b + 1, "o3" if L == 3 else None)
                    for u in range(2):
                        v.wait_ge(q["p_sb"], i * 2 + u + 1)
                        V.reciprocal(rs[:, u, 0:TB], sm[:, u, 0:TB])
                        v.drain()
                        V.tensor_scalar(rs[:, u, 0:TB], rs[:, u, 0:TB], tg[:, L:L + 1], None, ALU.mult)
                        v.drain()
                        v.wait_ge(q["y_ps"], i * 2 + u + 1)
                        for t in range(TB):
                            xt = x[:, ds(b * 4 + 2 * u + t, 1), :].rearrange("p t n -> p (t n)")
                            V.scalar_tensor_tensor(xt, psum[4 + u][:, t * D:(t + 1) * D], rs[:, u, t:t + 1], xt,
                                                   ALU.mult, ALU.add).then_inc(q["x"], 1)
                    if more:
                        take_values(i + 1, b + 1)
                    v.drain()

                rounds_of(v, L, front, back)

            one_head(0)
            phase_end(v, 2)

            def gate(L):
                q = gt

                def back(i, b, more):
                    if more:
                        def z_free():
                            v.wait_ge(q["zT_ps"], i * 2 + 2)
                            v.wait_ge(q["stored"], i * 32 + 32)
                        norm(q, i + 1, b + 1, None, z_free)
                    for u in range(2):
                        v.wait_ge(q["l_ps"], i * 2 + u + 1)
                        V.tensor_copy(logit[:, ds(b * 4 + 2 * u, 2), :],
                                      psum[u][:, 0:TB * E].rearrange("p (t e) -> p t e", t=TB)).then_inc(q["l_sb"], 1)

                rounds_of(v, L, lambda i, b: norm(q, i, b), back)
                q = rt
                v.drain()
                V.tensor_reduce(gmax, logit, AX.X, ALU.max)
                v.drain()
                V.tensor_tensor(logit, logit, bcast(gmax, 2, E), ALU.subtract).then_inc(q["logit"], 1)
                v.wait_ge(q["prob_exp"], 1 + L // 3)
                V.tensor_reduce(sumT, prob, AX.X, ALU.add)
                v.drain()
                V.reciprocal(sumT, sumT)
                v.drain()
                V.tensor_tensor(prob, prob, bcast(sumT, 2, E), ALU.mult).then_inc(q["prob"], 1)

            gate(0)
            v.drain()
            V.memset(thr, 0)
            phase_end(v, 3)
            q = sh
            with v.Fori(0, T // 512) as i:
                V.tensor_tensor(x[:, ds(i * 4, 4), :], x[:, ds(i * 4, 4), :], bcast(rows[:, ROWS.index("s0"), :], 1, 4), ALU.add)
                for m_ in range(HALF):
                    b = i * HALF + m_
                    V.tensor_tensor(cand, thr, bits[:, ds(b, 1), :].rearrange("p t n -> p (t n)"), ALU.bitwise_or)
                    v.drain()
                    V.tensor_tensor(sel, prob, bcast(cand.bitcast(F32), 1, NT), ALU.is_ge).then_inc(q["cmp"], 1)
                    v.wait_ge(q["cnt_ps"], i * HALF + m_ + 1)
                    V.tensor_reduce(cnt, psum[6][:, 0:P].rearrange("p (t e) -> p e t", t=NT), AX.X, ALU.add)
                    v.drain()
                    V.scalar_tensor_tensor(flag, cnt, float(CAP), bitf[:, ds(b, 1), :].rearrange("p t n -> p (t n)"),
                                           ALU.is_ge, ALU.mult)
                    v.drain()
                    V.tensor_tensor(thr, thr, flag, ALU.bitwise_or)
                    v.drain()
                for t in range(2):
                    v.wait_ge(q["y_ps"], i * 2 + t + 1)
                    xt = x[:, ds(i * 4 + 2 * t, 2), :]
                    V.scalar_tensor_tensor(xt.rearrange("p t n -> p (t n)"), psum[4 + t][:, :], tg[:, 4:5],
                                           xt.rearrange("p t n -> p (t n)"), ALU.mult, ALU.add).then_inc(q["x"], 1)
            phase_end(v, 4)

            def route(L):
                n = 1 + L // 3
                q = rt
                w0 = work[:, 0, :].rearrange("p (t e) -> p t e", t=NT)
                w1 = work[:, 1, :].rearrange("p (t e) -> p t e", t=NT)
                w2 = work[:, 2, :].rearrange("p (t e) -> p t e", t=NT)
                if L == 0:
                    tf = bcast(thr.bitcast(F32), 1, NT)
                    V.tensor_tensor(sel, prob, tf, ALU.is_gt)
                    V.tensor_tensor(sel2, prob, tf, ALU.is_equal).then_inc(q["c_in"], 1)
                    v.wait_ge(q["c_ps"], 1)
                    V.tensor_reduce(cnt, psum[0][:, 0:P].rearrange("p (t e) -> p e t", t=NT), AX.X, ALU.add)
                    v.drain()
                    V.tensor_tensor(w0, psum[1][:, 0:P].rearrange("p (t e) -> p t e", t=NT), bcast(cnt, 1, NT), ALU.add)
                    v.drain()
                    V.tensor_scalar(w0, w0, float(CAP), None, ALU.is_le)
                    v.drain()
                    V.tensor_tensor(w0, w0, sel2, ALU.mult)
                    v.drain()
                    V.tensor_tensor(sel, w0, sel, ALU.add).then_inc(q["rank_in"], 1)
                else:
                    V.tensor_reduce(gmax, prob, AX.X, ALU.max)
                    v.drain()
                    V.tensor_tensor(w0, prob, bcast(gmax, 2, E), ALU.is_equal)
                    v.drain()
                    V.tensor_tensor(w0, w0, bcast(m8, 1, NT), ALU.mult)
                    v.drain()
                    V.tensor_reduce(sumT, w0, AX.X, ALU.max)
                    v.drain()
                    V.tensor_tensor(sel, w0, bcast(sumT, 2, E), ALU.is_equal).then_inc(q["rank_in"], 1)
                v.wait_ge(q["rank_ps"], n)
                V.tensor_copy(w1, psum[2][:, 0:P].rearrange("p (t e) -> p t e", t=NT))
                v.drain()
                V.scalar_tensor_tensor(work[:, 0, :], work[:, 1, :], float(CAP), sel.rearrange("p t e -> p (t e)"),
                                       ALU.is_le, ALU.mult)
                v.drain()
                V.tensor_tensor(work[:, 1, :], work[:, 1, :], work[:, 0, :], ALU.mult)
                v.drain()
                if L == 3:
                    V.tensor_scalar(w2, bcast(m8, 1, NT), -float(CAP), float(CAP * E - 1), ALU.mult, ALU.add)
                    v.drain()
                    V.tensor_tensor(w2, w2, w0, ALU.mult)
                    v.drain()
                    V.tensor_tensor(w2, w2, w1, ALU.add)
                    v.drain()
                    V.tensor_reduce(slotf, w2, AX.X, ALU.add)
                    V.tensor_reduce(wtok, w0, AX.X, ALU.add)
                    v.drain()
                    V.tensor_copy(slot_i, slotf)
                    V.tensor_tensor(wtok, wtok, gmax, ALU.mult)
                    v.drain()
                    V.tensor_scalar(wtok, wtok, tg[:, 7:8], None, ALU.mult)
                V.tensor_scalar(work[:, 1, :], work[:, 1, :], -1.0, None, ALU.add)
                v.drain()
                V.tensor_copy(posi[:, 0, :], work[:, 1, :])
                v.drain()
                V.tensor_scalar(posi[:, 1, :], posi[:, 0, :], 4, None, ALU.arith_shift_right)
                V.tensor_scalar(posi[:, 2, :], posi[:, 0, :], 15, None, ALU.bitwise_and)
                v.drain()
                V.tensor_copy(work[:, 0, :], posi[:, 1, :])
                V.tensor_copy(work[:, 1, :], posi[:, 2, :])
                v.drain()
                for a, hot in enumerate((hi1, lo1)):
                    V.tensor_tensor(hot.rearrange("p t e a -> p (t e) a"), bcast(work[:, a, :], 2, 16),
                                    bcast(iota16[:, :], 1, NT * E), ALU.is_equal)
                v.drain()
                v.wait_ge(gt["stored"], 16 * (NT // 2) * n)
                l = lo1.rearrange("p t e a -> p t (e a)")
                V.tensor_tensor(lo2[:, :, 0, :], l, bcast(tcol, 2, P), ALU.mult)
                V.tensor_scalar(lo2[:, :, 1, :], l, pcol, None, ALU.mult).then_inc(q["hot"], 1)
                v.wait_ge(q["idx_ps"], n)
                V.tensor_scalar(work[:, 0, :], psum[3][:, 0:P], float(P), None, ALU.mult)
                v.drain()
                V.tensor_tensor(work[:, 0, :], work[:, 0, :], psum[3][:, P:2 * P], ALU.add)
                v.drain()
                V.tensor_tensor(work[:, 0, :].rearrange("p (e b) -> p e b", e=E), work[:, 0, :].rearrange("p (e b) -> p e b", e=E),
                                blk, ALU.mult)
                v.drain()
                V.tensor_reduce(work[:, 1, 0:16], work[:, 0, :].rearrange("p (e b) -> p b e", e=E), AX.X, ALU.add)\
                 .then_inc(q["idxf"], 1)
                v.wait_ge(q["sT_ps"], n)
                V.tensor_copy(idx, psum[4][:, 0:16]).then_inc(q["idx"], 1)

            route(0)
            v.wait_ge(load["b2row"], 16)
            phase_end(v, 5)

            def experts(L):
                q = ex
                with v.Fori(0, E // 2) as b:
                    i = b + BASE[L]
                    for u in range(2):
                        v.wait_ge(q["y_ps"], i * 2 + u + 1)
                        if L == 0:
                            v.wait_ge(q[f"gather{u}"], i * 32 + 32)
                            V.tensor_scalar(wsl[:, u, :], G[:, u, :, ds(D + b * 2 + u, 1)].rearrange("p t n -> p (t n)"),
                                            tg[:, 4:5], None, ALU.mult)
                            V.tensor_tensor(eout[:, u], psum[4 + u][:, :].rearrange("p (t n) -> p t n", t=TB),
                                            bcast(b2row[:, ds(b * 2 + u, 1), :].rearrange("p t n -> p (t n)"), 1, TB), ALU.add)
                            v.drain()
                            for t in range(TB):
                                m = V.tensor_scalar(eout[:, u, t, :], eout[:, u, t, :], wsl[:, u, t:t + 1], None, ALU.mult)
                        else:
                            m = V.tensor_copy(eout[:, u], psum[4 + u][:, :].rearrange("p (t n) -> p t n", t=TB))
                        m.then_inc(q["y_sb"], 1)
                    for u in range(2):
                        v.wait_ge(q[f"o{u}"], i * 32 + 32) if L == 0 else v.wait_ge(q[f"e{u}"], b * 16 + 16)

            v.wait_ge(load["ternary"], 32)
            for a in range(2):
                V.tensor_reduce(gam[:, a:a + 1], ffw[:, a, :], AX.X, ALU.add, apply_absolute_value=True)
            v.drain().then_inc(su["gsum_in"], 1)
            v.wait_ge(su["gsum_ps"], 1)
            V.tensor_scalar(gam[:, 4:6], psum[5][:, 0:2], 0.5 / (HID * D), 0.5e-6, ALU.mult, ALU.add)
            v.drain()
            V.tensor_scalar(gam[:, 2:4], gam[:, 4:6], -1.0, None, ALU.mult)
            v.drain().then_inc(su["gsum_out"], 1)
            for a in range(2):
                V.tensor_scalar(below, ffw[:, a, :], gam[:, 2 + a:3 + a], None, ALU.is_lt)
                v.drain()
                V.scalar_tensor_tensor(sign, ffw[:, a, :], gam[:, 4 + a:5 + a], below, ALU.is_gt, ALU.subtract)
                v.drain()
                V.tensor_copy(tern[a], sign)
                v.drain()
            experts(0)
            phase_end(v, 6)

            def multi_head(L):
                q = multi
                k0, t0 = NB * (L // 2), UNITS * (L // 2)
                V.memset(Vp, 0.0)
                v.drain()

                def norm_batch(k, u):
                    if L == 1 and isinstance(k, int) and k == 2:
                        v.wait_ge(load["x"], 32)
                    for t in range(TB):
                        V.bn_stats(st[:, t, :], x[:, ds(k * 2 + t, 1), :].rearrange("p t n -> p (t n)"))
                    v.drain()
                    for t in range(TB):
                        V.bn_aggr(mv[:, t, :], st[:, t, :])
                    v.drain()
                    V.tensor_scalar(ve[:, 2 * u:2 * u + 2], mv[:, 0:TB, 1], EPS, None, ALU.add).then_inc(q["var"], 1)

                def norm_batch_end(k, u):
                    v.wait_ge(q["rstd"], k0 + k + 1)
                    if in_range(k - 2, NB):
                        v.wait_ge(q["zT_ps"], k0 + k - 1)
                    for t in range(TB):
                        m = V.tensor_scalar(z[:, 2 * u + t, :], x[:, ds(k * 2 + t, 1), :].rearrange("p t n -> p (t n)"),
                                            mv[:, t, 0:1], rstd[:, 2 * u + t:2 * u + t + 1], ALU.subtract, ALU.mult)
                    m.then_inc(q["z"], 1)
                    v.drain()
                    xt = x[:, ds(k * 2, 2), :]
                    V.tensor_tensor(xt, xt, bcast(rows[:, ROWS.index(f"o{L}"), :], 1, TB), ALU.add)

                def take_values(k, u):
                    v.wait_ge(q["V_ps"], k0 + k + 1)
                    if in_range(k - 2, NB):
                        v.wait_ge(q["O_ps"], k0 + k - 1)
                    for j in range(2):
                        o = Vp[0:SK, u].rearrange("p (a b) (c n) -> p a b c n", b=2, c=2)[:, :, j, j, :]
                        s = psum[6][0:SK, 256:512].rearrange("p (a b n) -> p a b n", b=2, n=HD)[:, :, j, :]
                        r = rows[0:SK, ROWS.index(f"v{L}"), :].rearrange("p (a b n) -> p a b n", b=2, n=HD)[:, :, j, :]
                        m = V.tensor_tensor(o, s, r, ALU.add)
                    m.then_inc(q["V_sb"], 1)

                def shift(t, n):
                    v.wait_ge(q["s_ps"], t0 + t + 1)
                    if in_range(t - 4, UNITS):
                        v.wait_ge(q["pT_ps"], 2 * t0 + t * 2 - 6)
                    for j in range(2):
                        V.tensor_reduce(mx[:, n % 4, 4 * j:4 * j + 4],
                                        psum[2 * (n % 2) + j][:, 0:4 * SK].rearrange("p (h n) -> p h n", h=4), AX.X, ALU.max)
                    v.drain()
                    for j in range(2):
                        m = V.tensor_tensor(Pr[:, n % 4, 4 * j:4 * j + 4, :],
                                            psum[2 * (n % 2) + j][:, 0:4 * SK].rearrange("p (h n) -> p h n", h=4),
                                            bcast(mx[:, n % 4, 4 * j:4 * j + 4], 2, SK), ALU.subtract)
                    m.then_inc(q["sub"], 1)

                def sums(t, n):
                    v.wait_ge(q["p_exp"], t0 + t + 1)
                    V.tensor_reduce(sm[:, n % 4], Pr[:, n % 4], AX.X, ALU.add)
                    v.drain()
                    V.reciprocal(rs[:, n % 4], sm[:, n % 4]).then_inc(q["rsum"], 1)

                def add_output(k):
                    v.wait_ge(q["y_ps"], k0 + k + 1)
                    xt = x[:, ds(k * 2, 2), :].rearrange("p t n -> p (t n)")
                    V.scalar_tensor_tensor(xt, psum[7][:, :], tg[:, L:L + 1], xt, ALU.mult, ALU.add).then_inc(q["x"], 1)

                def step(r, n):
                    t, k, m_, u = batch_of(r, n)
                    if in_range(t, UNITS):
                        shift(t, n)
                    if in_range(t - 1, UNITS):
                        sums(t - 1, n - 1)
                    if m_ == 2 and in_range(k - 2, NB):
                        add_output(k - 2)
                    if m_ == 1 and in_range(k + 2, NB):
                        norm_batch(k + 2, u)
                    if m_ == 0 and in_range(k + 1, NB):
                        norm_batch_end(k + 1, 1 - u)
                    if m_ == 3 and in_range(k + 1, NB):
                        take_values(k + 1, 1 - u)

                norm_batch(0, 0)
                norm_batch_end(0, 0)
                take_values(0, 0)
                norm_batch(1, 1)
                unit_steps(v, step)

            v.wait_ge(load["x0"], 32)
            multi_head(1)
            phase_end(v, 7)
            q = f1

            def spectral_back(i, b, more):
                if more:
                    norm(q, i + 1, b + 1, "f1", lambda: v.wait_ge(q["zT_ps"], i * 2 + 2))
                    v.drain()
                for u in range(2):
                    v.wait_ge(q["y_ps"], i * 2 + u + 1)
                    xt = x[:, ds(b * 4 + 2 * u, 2), :].rearrange("p t n -> p (t n)")
                    V.tensor_tensor(xt, psum[u][:, :], xt, ALU.add).then_inc(q["x"], 1)

            rounds_of(v, 0, lambda i, b: norm(q, i, b, "f1"), spectral_back)
            v.drain()
            phase_end(v, 8)
            multi_head(2)
            phase_end(v, 9)

            q = f2

            def step(r, n):
                t = r * 4 + n
                if in_range(t):
                    v.wait_ge(q["h_sb"], t + 1)
                    for j in range(2):
                        V.bn_stats(st[:, j, :], h2[:, n, j * 512:(j + 1) * 512])
                    v.drain()
                    V.bn_aggr(mx[:, n, 0:2], st[:, 0:2, :])
                    v.drain()
                    V.tensor_scalar(sm[:, n, 0:1], mx[:, n, 1:2], EPS, None, ALU.add).then_inc(q["st2"], 1)
                if in_range(t):
                    v.wait_ge(q["rstd2"], t + 1)
                    V.tensor_scalar(h2[:, n, :], h2[:, n, :], mx[:, n, 0:1], rs[:, n, 0:1], ALU.subtract, ALU.mult)\
                     .then_inc(q["n2"], 1)
                if n == 0 and in_range(r * 4 + 4):
                    v.wait_ge(q["zT_ps"], r * 2 + 2)
                    norm(q, r + 1, r + 1)
                if in_range(t - 2):
                    v.wait_ge(q["nT_sb"], t - 1)
                    if in_range(t - 4):
                        v.wait_ge(q["y_ps"], t - 3)
                    V.tensor_copy(h2s[:, 0, n % 2], h2T[:, n % 2]).then_inc(q["nTh"], 1)
                if n >= 2 and in_range(r * 4 + 4):
                    low_z(r + 1, n - 2)
                if in_range(t - 4):
                    v.wait_ge(q["y_ps"], t - 3)
                    xt = x[:, ds(t - 4, 1), :].rearrange("p t n -> p (t n)")
                    V.scalar_tensor_tensor(xt, psum[7][:, 0:D], tg[:, 6:7], xt, ALU.mult, ALU.add).then_inc(q["x"], 1)

            def low_z(r, u):
                v.wait_ge(q["zT_sb"], r * 2 + u + 1)
                V.tensor_tensor(zTs[:, 1, u], zT[:, u], zTs[:, 0, u], ALU.subtract).then_inc(q["zTs"], 1)

            norm(q, 0, 0)
            for u in range(2):
                low_z(0, u)
            v.drain().then_inc(q["x"], 1)
            for n in range(4):
                step(0, n)
            with v.Fori(1, NT // 4 - 1) as r:
                for n in range(4):
                    step(r, n)
            for t in range(NT - 4, NT + 4):
                step(t // 4, t % 4)
            phase_end(v, 10)
            one_head(3)
            phase_end(v, 11)
            gate(3)
            phase_end(v, 12)
            route(3)
            phase_end(v, 13)
            experts(3)
            phase_end(v, 14)
            with v.Fori(0, NT // 4) as i:
                for u in range(2):
                    v.wait_ge(fin[f"g{u}"], i * 32 + 32)
                    for t in range(TB):
                        xt = x[:, ds(i * 4 + 2 * u + t, 1), :].rearrange("p t n -> p (t n)")
                        m = V.scalar_tensor_tensor(xt, eout[:, u, t, :],
                                                   wtok[:, ds(i * 4 + 2 * u + t, 1)], xt, ALU.mult, ALU.add)
                    m.then_inc(fin["x"], 1)
            phase_end(v, 15)


def _layout(a):
    import numpy as np
    i = {k: np.asarray(v_) for k, v_ in a.items()}

    def kp(w):
        k, n = w.shape
        return np.ascontiguousarray(w.reshape(k // P, P, n).transpose(1, 0, 2))

    def flat(w):
        return kp(w).reshape(P, -1)

    d = {"x": i["x"].reshape(NT, P, D).transpose(1, 0, 2), "ctxT": kp(i["ctx_1024"].reshape(NB * SK, D).T)}
    ww = {"q0": i["L0_xattn_Wq"], "k0": i["L0_xattn_Wk"], "v0": i["L0_xattn_Wv"],
          "q1": i["L1_xattn_Wq_w"].T, "k1": i["L1_xattn_Wkv_w"][:D].T, "v1": i["L1_xattn_Wkv_w"][D:].T,
          "o1": i["L1_xattn_out_w"].T,
          "q2": i["L2_xattn_Wq"], "k2": i["L2_xattn_Wk"], "v2": i["L2_xattn_Wv"], "o2": i["L2_xattn_Wo"],
          "q3": i["L3_xattn_Wq"].T, "k3": i["L3_xattn_Wk"].T, "v3": i["L3_xattn_Wv"].T, "o3": i["L3_xattn_Wo"].T}
    for n, w in ww.items():
        d["W" + n] = kp(w)
    zero = np.zeros(D, np.float32)
    cb = {"q0": i["L0_xattn_bq"], "k0": i["L0_xattn_bk"], "q1": i["L1_xattn_Wq_b"], "k1": i["L1_xattn_Wkv_b"][:D],
          "q2": i["L2_xattn_bq"], "k2": i["L2_xattn_bk"], "q3": i["L3_xattn_bq"], "k3": zero, "v3": i["L3_xattn_bv"]}
    d["cols"] = np.concatenate([cb[n].reshape(2, P).T for n in COL], 1)
    rb = {"v0": i["L0_xattn_bv"], "s0": i["L0_ffn_bs2"], "v1": i["L1_xattn_Wkv_b"][D:], "o1": i["L1_xattn_out_b"],
          "f1": i["L1_ffn_bias"], "v2": i["L2_xattn_bv"], "o2": i["L2_xattn_bo"], "o3": i["L3_xattn_bo"]}
    d["rows"] = np.stack([rb[n] for n in ROWS])
    d["g"] = np.concatenate([i["g_xattn"], i["g_ffn"]])
    d["gates"] = np.stack([kp(i["L0_ffn_gate"]), kp(i["L3_ffn_wg"])], 1)
    d["b1T"] = np.concatenate([i["L0_ffn_b1"].reshape(E * MC, P).T, i["L0_ffn_bs1"].reshape(MC, P).T], 1)
    d["lnwb"] = np.stack([i["L2_ffn_ln_w"].reshape(MC, P).T, i["L2_ffn_ln_b"].reshape(MC, P).T], 1)
    d["m0"] = i["mask_BxS2_ik1"].reshape(1, -1)
    d["m1"] = i["mask_BxS2_bk0"].reshape(1, -1)
    d["m2"] = i["mask_BxS2_ik0"].reshape(1, -1)
    d["fside"] = i["fside_BxS2_0"].reshape(1, -1)
    d["shared0"], d["shared1"] = flat(i["L0_ffn_Ws1"]), flat(i["L0_ffn_Ws2"])
    d["tern0"], d["tern1"] = flat(i["L2_ffn_W_fc"].T), flat(i["L2_ffn_W_proj"].T)
    d["b2"] = i["L0_ffn_b2"]
    for L, a, b in ((0, "L0_ffn_W1", "L0_ffn_W2"), (3, "L3_ffn_w1", "L3_ffn_w2")):
        d[f"w0_{L}"] = i[a].reshape(E, KC, P, HID).transpose(0, 2, 1, 3).reshape(E, P, -1)
        d[f"w1_{L}"] = i[b].reshape(E, MC, P, D).transpose(0, 2, 1, 3).reshape(E, P, -1)
    d["wr"], d["wi"] = kp(i["L1_ffn_w_freq_real"]), kp(i["L1_ffn_w_freq_imag"])
    n = np.arange(D)
    ang = 2 * np.pi * ((n[:, None] * n[None, :]) % D) / D
    d["cosm"], d["sinm"], d["nsinm"] = (kp(t.astype(np.float32)) for t in (np.cos(ang), np.sin(ang), -np.sin(ang)))
    d["ident"] = np.eye(P, dtype=np.float32)
    p = np.arange(P)
    d["headmask"] = (p[:, None] // HD == np.arange(HC)[None]).astype(np.float32)
    d["iota16"] = np.tile(np.arange(16, dtype=np.float32), (P, 1))
    d["bits"] = np.ascontiguousarray(np.broadcast_to(
        np.array([0] + [1 << b for b in range(BITS - 2, -1, -1)], np.int32)[None, :, None], (P, BITS, E)))
    d["tokt"] = np.concatenate([
        np.tile(np.arange(NT, dtype=np.float32), (P, 1)), p[:, None].astype(np.float32), np.zeros((P, 1), np.float32),
        np.tile(E - np.arange(E, dtype=np.float32), (P, 1)),
        (p[:, None] // 16 == np.repeat(np.arange(E), 16)[None]).astype(np.float32)], 1)
    return {k: np.ascontiguousarray(v_) for k, v_ in d.items()}


def kernel(**inputs):
    import numpy as np
    import concourse.bacc as bacc
    from concourse.bass_utils import run_bass_kernel_spmd as run

    arrays = _layout(inputs)
    nc = bacc.Bacc("TRN2", target_bir_lowering=False, num_devices=1)
    d = {k: nc.dram_tensor(f"in_{k}", a.shape, mybir.dt.from_np(a.dtype), kind="ExternalInput").ap()
         for k, a in arrays.items()}
    out = nc.dram_tensor("out_0", (P, NT, D), F32, kind="ExternalOutput").ap()
    flamingo_kernel(nc, d, out)
    r = run(nc, [{f"in_{k}": a for k, a in arrays.items()}], core_ids=[0])
    got = r.results[0]["out_0"]
    return np.ascontiguousarray(got.transpose(1, 0, 2).reshape(NB, SQ, D))
```
